# Optimizing a Trainium2 kernel written in Bass

```python
import numpy as np
import jax
import jax.numpy as jnp

def _softmax(x, axis=-1):
    return jax.nn.softmax(x, axis=axis)

def _gelu(x):
    return jax.nn.gelu(x, approximate=True)

def _silu(x):
    return jax.nn.silu(x)

def _sigmoid(x):
    return jax.nn.sigmoid(x)

def _layernorm(x, axis=-1, eps=1e-05):
    m = jnp.mean(x, axis=axis, keepdims=True)
    v = jnp.var(x, axis=axis, keepdims=True)
    return (x - m) / jnp.sqrt(v + eps)

def _scatter_add(tgt, idx, src, axis=0):
    return tgt.at[idx].add(src)

def _segment_sum(src, seg, n):
    return jax.ops.segment_sum(src, seg, n)
kernel_name = 'mk_sandwich_d1_jaxref_r4_3bc11c'

def setup_inputs(seed: int=0):
    np.random.seed(seed)
    _w = jnp.asarray

    def _L0_attn_setup():
        import jax, jax.numpy as jnp
        import numpy as np
        D_MODEL = 256
        N_HEADS = 16
        HEAD_DIM = D_MODEL // N_HEADS

        def _rope(x):
            B = x.shape[0]
            half = HEAD_DIM // 2
            theta = 1.0 / 10000.0 ** (jnp.arange(0, HEAD_DIM, 2, dtype=jnp.float32) / HEAD_DIM)
            pos = jnp.arange(B, dtype=jnp.float32)
            ang = pos[:, None] * theta[None, :]
            ang2 = jnp.concatenate([ang, ang], axis=-1)
            cos = jnp.cos(ang2)[:, None, None, :]
            sin = jnp.sin(ang2)[:, None, None, :]
            neg_half = jnp.concatenate([x[..., :half], -x[..., half:]], axis=-1)
            return x * cos + neg_half * sin
        key = jax.random.key(seed)
        k_x, k_q, k_k, k_v = jax.random.split(key, 4)
        B, S = (4, 512)
        scale = 1.0 / np.sqrt(D_MODEL)
        x = jax.random.normal(k_x, (B, S, D_MODEL), dtype=jnp.float32)
        Wq = jax.random.normal(k_q, (D_MODEL, D_MODEL), dtype=jnp.float32) * scale
        Wk = jax.random.normal(k_k, (D_MODEL, D_MODEL), dtype=jnp.float32) * scale
        Wv = jax.random.normal(k_v, (D_MODEL, D_MODEL), dtype=jnp.float32) * scale
        return {'x': x, 'Wq': Wq, 'Wk': Wk, 'Wv': Wv}
    _L0_attn_in = _L0_attn_setup()

    def _L0_ffn_setup():
        import jax, jax.numpy as jnp
        import numpy as np
        B, S, D, F, E = (1, 256, 256, 1024, 8)
        EPS = 1e-05

        def _sublayer(xs, g, b, W1e, b1e, W2e, b2e):
            mu = jnp.mean(xs, axis=-1, keepdims=True)
            var = jnp.mean(jnp.square(xs - mu), axis=-1, keepdims=True)
            h = (xs - mu) * jax.lax.rsqrt(var + EPS) * g + b
            return xs + jax.nn.relu(h @ W1e.T + b1e) @ W2e.T + b2e
        key = jax.random.key(seed)
        ks = jax.random.split(key, 4)
        x = jax.random.normal(ks[0], (B, S, D), jnp.float32)
        centroids = jax.random.normal(ks[1], (E, D), jnp.float32) * 0.1
        gamma = jnp.ones((E, D), jnp.float32)
        beta = jnp.zeros((E, D), jnp.float32)
        W1 = jax.random.normal(ks[2], (E, F, D), jnp.float32) * 0.02
        b1 = jnp.zeros((E, F), jnp.float32)
        W2 = jax.random.normal(ks[3], (E, D, F), jnp.float32) * 0.02
        b2 = jnp.zeros((E, D), jnp.float32)
        return {'x': x, 'centroids': centroids, 'gamma': gamma, 'beta': beta, 'W1': W1, 'b1': b1, 'W2': W2, 'b2': b2}
    _L0_ffn_in = _L0_ffn_setup()
    _d = {'L0_attn_x': _L0_attn_in['x'], 'L0_attn_Wq': _L0_attn_in['Wq'], 'L0_attn_Wk': _L0_attn_in['Wk'], 'L0_attn_Wv': _L0_attn_in['Wv'], 'L0_ffn_centroids': _L0_ffn_in['centroids'], 'L0_ffn_gamma': _L0_ffn_in['gamma'], 'L0_ffn_beta': _L0_ffn_in['beta'], 'L0_ffn_W1': _L0_ffn_in['W1'], 'L0_ffn_b1': _L0_ffn_in['b1'], 'L0_ffn_W2': _L0_ffn_in['W2'], 'L0_ffn_b2': _L0_ffn_in['b2']}
    _x0 = _d['L0_attn_x']
    _d['L0_attn_x'] = jax.random.normal(jax.random.fold_in(jax.random.key(seed), 1), (8, 512, 256), dtype=_x0.dtype)
    del _x0
    return _d

def reference(L0_attn_x, L0_attn_Wq, L0_attn_Wk, L0_attn_Wv, L0_ffn_centroids, L0_ffn_gamma, L0_ffn_beta, L0_ffn_W1, L0_ffn_b1, L0_ffn_W2, L0_ffn_b2):

    def _L0_attn_ref(x, Wq, Wk, Wv):
        import jax, jax.numpy as jnp
        import numpy as np
        D_MODEL = 256
        N_HEADS = 16
        HEAD_DIM = D_MODEL // N_HEADS

        def _rope(x):
            B = x.shape[0]
            half = HEAD_DIM // 2
            theta = 1.0 / 10000.0 ** (jnp.arange(0, HEAD_DIM, 2, dtype=jnp.float32) / HEAD_DIM)
            pos = jnp.arange(B, dtype=jnp.float32)
            ang = pos[:, None] * theta[None, :]
            ang2 = jnp.concatenate([ang, ang], axis=-1)
            cos = jnp.cos(ang2)[:, None, None, :]
            sin = jnp.sin(ang2)[:, None, None, :]
            neg_half = jnp.concatenate([x[..., :half], -x[..., half:]], axis=-1)
            return x * cos + neg_half * sin
        B, S, D = x.shape
        q = (x @ Wq.T).reshape(B, S, N_HEADS, HEAD_DIM)
        k = (x @ Wk.T).reshape(B, S, N_HEADS, HEAD_DIM)
        v = (x @ Wv.T).reshape(B, S, N_HEADS, HEAD_DIM)
        q = _rope(q)
        k = _rope(k)
        q = q.transpose(0, 2, 1, 3)
        k = k.transpose(0, 2, 1, 3)
        v = v.transpose(0, 2, 1, 3)
        scores = jnp.einsum('bhqd,bhkd->bhqk', q, k) / np.sqrt(HEAD_DIM)
        weights = jax.nn.softmax(scores, axis=-1)
        out = jnp.einsum('bhqk,bhkd->bhqd', weights, v)
        return out.transpose(0, 2, 1, 3).reshape(B, S, D)

    def _L0_ffn_ref(x, centroids, gamma, beta, W1, b1, W2, b2):
        import jax, jax.numpy as jnp
        import numpy as np
        B, S, D, F, E = (1, 256, 256, 1024, 8)
        EPS = 1e-05

        def _sublayer(xs, g, b, W1e, b1e, W2e, b2e):
            mu = jnp.mean(xs, axis=-1, keepdims=True)
            var = jnp.mean(jnp.square(xs - mu), axis=-1, keepdims=True)
            h = (xs - mu) * jax.lax.rsqrt(var + EPS) * g + b
            return xs + jax.nn.relu(h @ W1e.T + b1e) @ W2e.T + b2e
        feats = x.reshape(-1, x.shape[-1])
        scores = jax.lax.stop_gradient(feats @ centroids.T)
        expert = jnp.argmax(scores, axis=1)
        onehot = jax.nn.one_hot(expert, E, dtype=feats.dtype)
        alpha = jax.nn.sigmoid(jnp.sum(feats * centroids[expert], axis=-1, keepdims=True))
        ys = jax.vmap(_sublayer, in_axes=(None, 0, 0, 0, 0, 0, 0))(feats, gamma, beta, W1, b1, W2, b2)
        y = jnp.einsum('te,etd->td', onehot, ys)
        out = alpha * y + (1.0 - alpha) * feats
        return out.reshape(x.shape)
    x = L0_attn_x
    x = x + _layernorm(_L0_attn_ref(_layernorm(x, axis=-1), L0_attn_Wq, L0_attn_Wk, L0_attn_Wv), axis=-1)
    x = x + _layernorm(_L0_ffn_ref(_layernorm(x, axis=-1), L0_ffn_centroids, L0_ffn_gamma, L0_ffn_beta, L0_ffn_W1, L0_ffn_b1, L0_ffn_W2, L0_ffn_b2), axis=-1)
    return x

_drawn_inputs = setup_inputs


def setup_inputs(seed=0):
    import zlib

    import numpy as np

    out = dict(_drawn_inputs(seed))
    spreads = {'L0_ffn_gamma': (1.0, 0.6),
     'L0_ffn_beta': (0.0, 0.8),
     'L0_ffn_b1': (0.0, 0.49),
     'L0_ffn_b2': (0.0, 0.1)}
    factors = {}
    for name, (base, spread) in spreads.items():
        noise = np.random.default_rng([zlib.crc32(name.encode()), seed]).standard_normal(out[name].shape)
        drawn = base * np.exp(spread * noise) if base else spread * noise
        out[name] = jnp.asarray(drawn.astype(out[name].dtype))
    for name, factor in factors.items():
        out[name] = (out[name] * factor).astype(out[name].dtype)
    return out
```

```python
from contextlib import ExitStack

import numpy as np

import concourse.bass as bass
from concourse import mybir
from concourse.alu_op_type import AluOpType as ALU

ACT = mybir.ActivationFunctionType
F32 = mybir.dt.float32
BF16 = mybir.dt.bfloat16
I32 = mybir.dt.int32
U32 = mybir.dt.uint32
AX = mybir.AxisListType.X

P = 128
EPS = 1e-5
BATCHES, SEQ, DIM = 8, 512, 256
HEADS, HEAD = 16, 16
CHUNKS = DIM // P
TILES = SEQ // P
GROUPS = 4
UNIT_HEADS = HEADS // GROUPS
UNITS = BATCHES * GROUPS
TOKENS = BATCHES * SEQ
TOKEN_TILES = TOKENS // P
EXPERTS, HIDDEN = 8, 1024
BLOCKS = HIDDEN // P
SLOTS = (TOKENS - EXPERTS) // P + EXPERTS
ROW = 2 * DIM
SKIP = 2 * TOKENS

Q_PARTS = (0, 0, 1, 1, 0, 2)
K_PARTS = (0, 1, 0, 1, 2, 0)
STACK = len(Q_PARTS) * HEAD
MAX_PARTS = 3
FULL = STACK + MAX_PARTS

C_IDENT, C_BELOW, C_ROPE, C_COUNT, C_PART, C_END = 0, P, 2 * P, 2 * P + BATCHES, 3 * P + BATCHES, 3 * P + BATCHES + 1

RING = 6
W1_RING = 3
AHEAD = 4
LOOPED = (SLOTS - AHEAD) // RING * RING
PEELED = SLOTS - LOOPED
FILLS = 4
LOADS = 6


def wait(eng, sem, value):
    if not isinstance(value, int) or value > 0:
        eng.wait_ge(sem, value)


def wait_alone(eng, sem, value, passed):
    eng.wait_ge(sem, value).then_inc(passed, 1)


def build(nc, x, wqt, wkt, wvt, cent, cent_t, gamma_t, beta_t, w1t, b1_t, w2t, b2, consts, minus_ones, out):
    ctx = ExitStack()
    with ctx:
        def sb(name, shape, dt=F32):
            return ctx.enter_context(nc.sbuf_tensor(name, shape, dt))

        def sem(name):
            return ctx.enter_context(nc.semaphore(name))

        def dram(name, shape, dt=F32):
            return nc.dram_tensor(name, shape, dt, kind="Internal").ap()

        parts_dram = dram("parts_dram", (2, 4, MAX_PARTS, P, SEQ), BF16)
        max_dram = dram("max_dram", (2, MAX_PARTS, HEADS, P), BF16)
        rows_dram = dram("rows_dram", (TOKENS, ROW))

        cst = sb("cst", [P, C_END])
        ident = cst[:, C_IDENT:C_IDENT + P]
        wq = sb("wq", [P, CHUNKS, DIM])
        wk = sb("wk", [P, CHUNKS, DIM])
        wv = sb("wv", [P, CHUNKS, DIM])
        centT = sb("centT", [P, CHUNKS, EXPERTS])
        half_neg = sb("half_neg", [P, TILES])
        x_in = sb("x_in", [P, TILES, DIM])
        x_res = sb("x_res", [P, TILES, DIM])
        normedT = sb("normedT", [P, CHUNKS, SEQ])
        parts = sb("parts", [P, 4, MAX_PARTS, SEQ], BF16)
        rest = sb("rest", [P, 2, SEQ])
        QS = sb("QS", [P, 2, HEADS, SEQ], BF16)
        KS = sb("KS", [P, 2, HEADS, SEQ], BF16)
        values = sb("values", [P, 2, TILES, HEADS, 32])
        big = sb("big", [P, 2 * UNIT_HEADS, TILES * SEQ])
        probs = big[:, :, :].rearrange("p (u h) (t q) -> p u h t q", u=2, t=TILES)
        w2 = big[:, :, :].rearrange("p e (f d) -> p e f d", f=BLOCKS)
        row_max = sb("row_max", [P, 2, UNIT_HEADS * TILES])
        max_parts = sb("max_parts", [UNIT_HEADS * TILES, 2, MAX_PARTS, P], BF16)
        max_rest = sb("max_rest", [UNIT_HEADS * TILES, 2, P])
        outT = sb("outT", [P, SEQ])
        attn = sb("attn", [P, 2, TILES, DIM])
        inv_sum = sb("inv_sum", [P, TILES, UNIT_HEADS])
        rows = sb("rows", [P, TILES, ROW])
        featsT = normedT
        scoreT = sb("scoreT", [P, SEQ])
        scores = sb("scores", [P, TOKEN_TILES, EXPERTS])
        stats = sb("stats", [P, 3, TILES, 6])
        moments = sb("moments", [P, 3, TILES, 2])
        rstd = sb("rstd", [P, 3, TILES])

        score_bank = [ctx.enter_context(nc.psum_tensor(f"score_bank{i}", [P, SEQ], F32)) for i in range(3)]
        keyed_bank = [ctx.enter_context(nc.psum_tensor(f"keyed_bank{i}", [P, SEQ], F32)) for i in range(2)]
        value_bank = ctx.enter_context(nc.psum_tensor("value_bank", [P, SEQ], F32))
        misc = [ctx.enter_context(nc.psum_tensor(f"misc{i}", [P, SEQ], F32)) for i in range(2)]

        s_const = sem("s_const")
        s_fill = sem("s_fill")
        s_passed = sem("s_passed")
        s_x = sem("s_x")
        s_res = sem("s_res")
        s_xst = sem("s_xst")
        s_xmom = sem("s_xmom")
        s_pool = sem("s_pool")
        s_normed = sem("s_normed")
        s_nT_ps = sem("s_nT_ps")
        s_nT = sem("s_nT")
        s_qk_ps = sem("s_qk_ps")
        s_part1 = sem("s_part1")
        s_rest = sem("s_rest")
        s_part2 = sem("s_part2")
        s_part3 = sem("s_part3")
        s_parts_out = [sem("s_parts_out0"), sem("s_parts_out1")]
        s_stack = [sem("s_stack0"), sem("s_stack1")]
        s_v_ps = sem("s_v_ps")
        s_v = sem("s_v")
        s_score = sem("s_score")
        s_rowmax = sem("s_rowmax")
        s_mT_ps = sem("s_mT_ps")
        s_m1 = sem("s_m1")
        s_mrest = sem("s_mrest")
        s_m2 = sem("s_m2")
        s_mrest2 = sem("s_mrest2")
        s_m3 = sem("s_m3")
        s_m_out = [sem("s_m_out0"), sem("s_m_out1")]
        s_m_row = [sem("s_m_row0"), sem("s_m_row1")]
        s_keyed = sem("s_keyed")
        s_exp = sem("s_exp")
        s_pv = sem("s_pv")
        s_outT = sem("s_outT")
        s_out_ps = sem("s_out_ps")
        s_inv = sem("s_inv")
        s_attn = sem("s_attn")
        s_ast = sem("s_ast")
        s_amom = sem("s_amom")
        s_attn_n = sem("s_attn_n")
        s_x1 = sem("s_x1")
        s_x1st = sem("s_x1st")
        s_x1mom = sem("s_x1mom")
        s_feats = sem("s_feats")
        s_rows = sem("s_rows")
        s_fT_ps = sem("s_fT_ps")
        s_fT = sem("s_fT")
        s_sc_ps = sem("s_sc_ps")
        s_sc = sem("s_sc")
        s_scT_ps = sem("s_scT_ps")
        s_scores = sem("s_scores")

        count = cst[:, C_COUNT:C_COUNT + P]
        small = rest[:].rearrange("p a n -> p (a n)")
        one_hot, running, masked, no_carry = (small[:, i * 256:(i + 1) * 256].rearrange(
            "p (e t) -> p e t", e=EXPERTS) for i in range(4))
        hits = x_res[:, 0, :].rearrange("p (t e) -> p t e", e=EXPERTS)
        count_bf = x_res[:, 1, 0:P // 2].bitcast(BF16)
        slot_ge = x_in[:].rearrange("p t d -> p (t d)")[:, 0:SLOTS * EXPERTS].rearrange("p (s e) -> p s e", e=EXPERTS)
        ones = outT[:, 0:P]
        place_hot = attn[:].rearrange("p a t d -> p (a t d)").bitcast(BF16).rearrange("p (t r) -> p t r", r=P)
        first = QS[:].rearrange("p a h n -> p (a h n)").bitcast(F32)
        second = KS[:].rearrange("p a h n -> p (a h n)").bitcast(F32)
        W = HIDDEN * CHUNKS
        w1 = first[:, 0:W1_RING * W].rearrange("p (k c f) -> p k c f", k=W1_RING, c=CHUNKS)
        hidden = first[:, W1_RING * W:(W1_RING + 1) * W].rearrange("p (k f t) -> p k f t", k=2, f=BLOCKS)
        third = values[:].rearrange("p a t h d -> p (a t h d)")
        tokT = third[:, 0:512].rearrange("p (k c t) -> p k c t", k=2, c=CHUNKS)
        new_rows = third[:, 512:512 + RING * DIM].rearrange("p (k d) -> p k d", k=RING)
        product = third[:, 512 + RING * DIM:768 + RING * DIM]
        slot_eq = third[:, 0:TOKEN_TILES * SLOTS].rearrange("p (t s) -> p t s", s=SLOTS)
        n_hot = TOKEN_TILES * 3 * SLOTS
        slot_hot = third[:, TOKEN_TILES * SLOTS:TOKEN_TILES * SLOTS + n_hot // 2].bitcast(BF16).rearrange(
            "p (t m s) -> p t m s", m=3, s=SLOTS)
        b2_all = second[:, 0:W].rearrange("p (e d) -> p e d", e=EXPERTS)
        cent_all = second[:, W:2 * W].rearrange("p (e d) -> p e d", e=EXPERTS)
        got = second[:, 2 * W:2 * W + RING * ROW].rearrange("p (k r) -> p k r", k=RING)
        tok_n = second[:, 2 * W + RING * ROW:2 * W + RING * ROW + 512].rearrange("p (k d) -> p k d", k=2)
        mixed = second[:, 2 * W + RING * ROW + 512:4 * W].rearrange("p (k d) -> p k d", k=2)
        best = sb("best", [P, TOKEN_TILES])
        first_hit = sb("first_hit", [P, TOKEN_TILES])
        less_8 = sb("less_8", [P, EXPERTS])
        tiles_i = sb("tiles_i", [P, EXPERTS], I32)
        tiles_f = sb("tiles_f", [P, EXPERTS])
        tiles_end = sb("tiles_end", [P, EXPERTS])
        offset = sb("offset", [P, EXPERTS])
        place = sb("place", [P, TOKEN_TILES])
        place_i = sb("place_i", [P, TOKEN_TILES], I32)
        slot_f = sb("slot_f", [P, TOKEN_TILES])
        within = sb("within", [P, TOKEN_TILES])
        expert_f = sb("expert_f", [P, SLOTS])
        expert_of = sb("expert_of", [P, SLOTS], I32)
        found = sb("found", [P, 3, SLOTS])
        token_f = sb("token_f", [P, SLOTS])
        index_all = sb("index_all", [P, SLOTS, 2], I32)
        index_now = sb("index_now", [P, RING, 2], I32)
        NPAR = 2 * CHUNKS + BLOCKS
        params = sb("params", [P, EXPERTS, NPAR])
        params_now = sb("params_now", [P, RING, NPAR])
        slot_stats = sb("slot_stats", [P, 2, 2, 6])
        slot_mom = sb("slot_mom", [P, 2, 2, 2])
        slot_rstd = sb("slot_rstd", [P, 2, 2])
        dot = sb("dot", [P, RING])
        minus = sb("minus", [P, RING])
        alpha = sb("alpha", [P, RING])

        hidden_bank = ((score_bank[0], score_bank[1]), (score_bank[2], keyed_bank[0]))
        y_bank = (keyed_bank[1], value_bank)

        s_route = sem("s_route")
        s_counted = sem("s_counted")
        s_totals = sem("s_totals")
        s_experts = sem("s_experts")
        s_hot = sem("s_hot")
        s_found = sem("s_found")
        s_index = sem("s_index")
        s_par = sem("s_par")
        s_w2 = sem("s_w2")
        s_w1 = [sem(f"s_w1_{i}") for i in range(W1_RING)]
        s_prep = sem("s_prep")
        s_gather = [sem(f"s_gather{i}") for i in range(RING)]
        s_scatter = [sem(f"s_scatter{i}") for i in range(RING)]
        s_gst = sem("s_gst")
        s_gmom = sem("s_gmom")
        s_dot = sem("s_dot")
        s_minus = sem("s_minus")
        s_plus1 = sem("s_plus1")
        s_alpha = sem("s_alpha")
        s_chain = sem("s_chain")
        s_grstd = sem("s_grstd")
        s_mrstd = sem("s_mrstd")
        s_tok = sem("s_tok")
        s_tokT_ps = sem("s_tokT_ps")
        s_tokT = sem("s_tokT")
        s_h_ps = sem("s_h_ps")
        s_h = sem("s_h")
        s_y_ps = sem("s_y_ps")
        s_y = sem("s_y")
        s_mix = sem("s_mix")
        s_mst = sem("s_mst")
        s_mmom = sem("s_mmom")
        s_mixn = sem("s_mixn")
        s_new = sem("s_new")

        block = ctx.enter_context(nc.Block())
        x_tiled = x.rearrange("b (t p) d -> b p t d", p=P)
        rows_tiled = rows_dram.rearrange("(b t p) r -> b p t r", p=P, t=TILES)

        def slot_at(r, k, ahead):
            return r * RING + (k + ahead), (k + ahead) % RING, r + (k + ahead) // RING

        def expert_reg(eng, n):
            return eng.value_load(expert_of[0:1, bass.ds(n, 1)], min_val=0, max_val=EXPERTS - 1)

        def sp_load_x(sp, b):
            wait(sp, s_nT_ps, CHUNKS * b)
            sp.dma_start(x_in[:], x_tiled[b]).then_inc(s_x, 16)

        def sp_load_residual(sp, b):
            sp.dma_start(x_res[:], x_tiled[b]).then_inc(s_res, 16)

        def sp_stack_half(sp, b, par, half):
            for kind in (0, 1):
                job = 2 * half + kind
                sp.wait_ge(s_part3, 4 * b + job + 1)
                sp.dma_start(parts_dram[par, job].rearrange("k p n -> p k n"),
                             parts[:, job]).then_inc(s_parts_out[half], 16)
            wait(sp, s_keyed, 64 * (b - 1) if not isinstance(b, int) else max(0, 64 * (b - 1)))
            sp.wait_ge(s_parts_out[half], 32 * (b + 1))
            for kind, stack, order in ((0, QS, Q_PARTS), (1, KS, K_PARTS)):
                for blk, part in enumerate(order):
                    src = parts_dram[par, 2 * half + kind, part].rearrange("(h d) n -> d h n", d=HEAD)
                    sp.dma_start(stack[blk * HEAD:(blk + 1) * HEAD, par, half * 8:half * 8 + 8, :],
                                 src).then_inc(s_stack[half], 16)

        def sp_max(sp, b, group, par):
            k = group % 2
            sp.wait_ge(s_m3, 4 * b + group + 1)
            sp.dma_start(max_dram[k].rearrange("m r n -> r m n"), max_parts[:, k]).then_inc(s_m_out[k], 16)
            sp.wait_ge(s_m_out[k], (2 * b + group // 2 + 1) * 16)
            rows_of = QS[STACK:FULL, par, 4 * group:4 * group + 4, :].rearrange("m h (t q) -> m (h t) q", t=TILES)
            sp.dma_start(rows_of, max_dram[k]).then_inc(s_m_row[k], 16)

        def sp_store_rows(sp, b):
            sp.wait_ge(s_feats, TILES * (b + 1))
            sp.dma_start(rows_tiled[b], rows[:]).then_inc(s_rows, 16)

        def sp_batch(sp, b, par, first=False, last=False):
            if not last:
                sp_load_x(sp, b + 1)
            sp_max(sp, b, 1, par)
            if not first:
                sp_load_residual(sp, b - 1)
            sp_max(sp, b, 2, par)
            if not last:
                sp_stack_half(sp, b + 1, 1 - par, 0)
            sp_max(sp, b, 3, par)
            if not last:
                sp_stack_half(sp, b + 1, 1 - par, 1)
            if not first:
                sp_store_rows(sp, b - 1)
                sp.wait_ge(s_rows, 16 * b)
            if not last:
                sp_max(sp, b + 1, 0, 1 - par)

        def sp_w1(sp, n, k):
            e = expert_reg(sp, n)
            sp.dma_start(w1[:, k], w1t[bass.ds(e, 1)].rearrange("o p c f -> (o p) c f")).then_inc(s_w1[k], 16)

        def sp_slot(sp, r, k):
            n, _, _ = slot_at(r, k, 0)
            if not isinstance(r, int) or n + W1_RING < SLOTS:
                sp.wait_ge(s_h_ps, 2 * (n + 1))
                sp_w1(sp, n + W1_RING, k % W1_RING)

        @block.sync
        def _(sp):
            sp.dma_start(x_in[:], x_tiled[0]).then_inc(s_x, 16)
            sp.dma_start(cst[:], consts).then_inc(s_const, 16)
            for tile, src in ((wq, wqt), (wk, wkt), (wv, wvt)):
                sp.dma_start(tile[:], src.rearrange("(c p) n -> p c n", p=P)).then_inc(s_const, 16)
            sp.dma_start(centT[:], cent_t.rearrange("(c p) e -> p c e", p=P)).then_inc(s_const, 16)
            sp.dma_start(KS[STACK:FULL, :, :, :], minus_ones).then_inc(s_const, 16)
            sp_stack_half(sp, 0, 0, 0)
            sp_stack_half(sp, 0, 0, 1)
            sp_max(sp, 0, 0, 0)
            sp_batch(sp, 0, 0, first=True)
            with sp.Fori(0, 3) as r:
                sp_batch(sp, r * 2 + 1, 1)
                sp_batch(sp, r * 2 + 2, 0)
            sp_batch(sp, 7, 1, last=True)
            sp_load_residual(sp, 7)
            sp_store_rows(sp, 7)
            sp.wait_ge(s_keyed, 16 * UNITS)
            sp.dma_start(b2_all, b2.partition_broadcast(P)).then_inc(s_par, 16)
            sp.dma_start(cent_all, cent.partition_broadcast(P)).then_inc(s_par, 16)
            sp.dma_start(params[:, :, 0:CHUNKS], gamma_t).then_inc(s_par, 16)
            sp.dma_start(params[:, :, CHUNKS:2 * CHUNKS], beta_t).then_inc(s_par, 16)
            sp.dma_start(params[:, :, 2 * CHUNKS:NPAR], b1_t).then_inc(s_par, 16)
            sp.wait_ge(s_pv, UNITS)
            for e in range(EXPERTS):
                sp.dma_start(w2[:, e], w2t[:, e]).then_inc(s_w2, 16)
            sp.wait_ge(s_experts, 1)
            for n in range(W1_RING):
                sp_w1(sp, n, n)
            with sp.Fori(0, LOOPED // RING) as r:
                for k in range(RING):
                    sp_slot(sp, r, k)
            for k in range(PEELED):
                sp_slot(sp, LOOPED // RING, k)
            for k in range(RING):
                sp.wait_ge(s_scatter[k], 16 * ((SLOTS - k + RING - 1) // RING))

        def pe_normed_t(c):
            for t in range(TILES):
                last = nc.tensor.transpose(misc[c][:, t * P:(t + 1) * P], x_in[:, t, c * P:(c + 1) * P], ident)
            last.then_inc(s_nT_ps, 1)

        def pe_project(bank, weight, half):
            for c in range(CHUNKS):
                last = nc.tensor.matmul(misc[bank][:], weight[:, c, half * P:(half + 1) * P], normedT[:, c, :],
                                        start=(c == 0), stop=(c == CHUNKS - 1))
            last.then_inc(s_qk_ps, 1)

        def pe_values(bank, pair):
            for i in range(2):
                t = 2 * pair + i
                for c in range(CHUNKS):
                    last = nc.tensor.matmul(misc[bank][:, i * DIM:(i + 1) * DIM], normedT[:, c, t * P:(t + 1) * P],
                                            wv[:, c, :], start=(c == 0), stop=(c == CHUNKS - 1))
            last.then_inc(s_v_ps, 1)

        def pe_max_t(bank, k):
            nc.tensor.transpose(misc[bank][0:UNIT_HEADS * TILES, 0:P], row_max[:, k, :], ident).then_inc(s_mT_ps, 1)

        def pe_out_t(bank):
            for t in range(TILES):
                last = nc.tensor.transpose(misc[bank][:, t * P:(t + 1) * P], outT[:, t * P:(t + 1) * P], ident)
            last.then_inc(s_out_ps, 1)

        def pe_feats_t(c):
            for t in range(TILES):
                last = nc.tensor.transpose(misc[c][:, t * P:(t + 1) * P], rows[:, t, c * P:(c + 1) * P], ident)
            last.then_inc(s_fT_ps, 1)

        def pe_expert_scores():
            for c in range(CHUNKS):
                last = nc.tensor.matmul(misc[0][0:EXPERTS, :], centT[:, c, :], featsT[:, c, :],
                                        start=(c == 0), stop=(c == CHUNKS - 1))
            last.then_inc(s_sc_ps, 1)

        def pe_expert_scores_t():
            for t in range(TILES):
                last = nc.tensor.transpose(misc[0][:, t * P:(t + 1) * P], scoreT[:, t * P:(t + 1) * P], ident)
            last.then_inc(s_scT_ps, 1)

        def pe_score(pe, tile_no, i, par, group):
            head, t = 4 * group + i // TILES, i % TILES
            back = 3 if i >= 3 else (1 if i == 0 else 3)
            wait(pe, s_rowmax, tile_no - back + 1)
            nc.tensor.matmul(score_bank[i % 3][:], QS[0:STACK, par, head, t * P:(t + 1) * P],
                             KS[0:STACK, par, head, :], start=True, stop=True).then_inc(s_score, 1)

        def pe_keyed(pe, tile_no, i, par, group):
            head, t = 4 * group + i // TILES, i % TILES
            wait(pe, s_exp, tile_no - 1)
            nc.tensor.matmul(keyed_bank[i % 2][:], KS[0:FULL, par, head, t * P:(t + 1) * P],
                             QS[0:FULL, par, head, :], start=True, stop=True).then_inc(s_keyed, 1)

        def pe_values_sum(t, k, par, group):
            for j in range(UNIT_HEADS):
                last = nc.tensor.matmul(value_bank[32 * j:32 * j + 32, :], values[:, par, t, 4 * group + j, :],
                                        probs[:, k, j, t, :], start=(t == 0), stop=(t == TILES - 1),
                                        tile_position=(0, 32 * j))
            return last

        def pe_unit_start(pe, b, group, par, scoring):
            v = 4 * b + group
            pe.wait_ge(s_m_row[group % 2], (2 * b + group // 2 + 1) * 16)
            if scoring:
                half_b = b if group < 2 else b + 1
                pe.wait_ge(s_stack[1 if group < 2 else 0], 192 * (half_b + 1))

        def pe_slot(pe, b, par, s, first=False, last=False):
            g, j = s // 4, s % 4
            u = 4 * b + g
            scoring = not (last and g >= 2)
            v_par, v_group = (par, g + 2) if g < 2 else (1 - par, g - 2)
            if j == 0:
                pe_unit_start(pe, b, g, par, scoring)
            for c in range(TILES):
                i = TILES * j + c
                if scoring:
                    pe_score(pe, 16 * (u + 2) + i, i, v_par, v_group)
                pe_keyed(pe, 16 * u + i, i, par, g)
            pe_jobs(pe, b, par, s, first, last)
            if not (first and g == 0):
                if j == 0:
                    pe.wait_ge(s_exp, 16 * u)
                    wait(pe, s_outT, u - 1)
                w_par, w_group = (par, g - 1) if g else (1 - par, 3)
                done = pe_values_sum(j, (g + 1) % 2, w_par, w_group)
                if j == 3:
                    done.then_inc(s_pv, 1)

        def pe_max_job(pe, b, group, bank):
            pe.wait_ge(s_rowmax, 16 * (4 * b + group + 1))
            pe_max_t(bank, group % 2)

        def pe_out_job(pe, w, bank):
            pe.wait_ge(s_outT, w + 1)
            pe_out_t(bank)

        def pe_jobs(pe, b, par, s, first, last):
            if s == 0:
                pe_max_job(pe, b, 1, 0)
            if s == 1 and not first:
                wait(pe, s_attn, 4 * b - 2)
                pe_out_job(pe, 4 * b - 2, 1)
            if s == 2 and not last:
                pe.wait_ge(s_normed, TILES * (b + 2))
                pe.wait_ge(s_mrest, 4 * b + 2)
                pe_normed_t(0)
                if first:
                    pe.wait_ge(s_v, 2)
                else:
                    pe.wait_ge(s_attn, 4 * b - 1)
                pe_normed_t(1)
            if s == 3 and not last:
                pe.wait_ge(s_nT, 2 * (b + 1) + 2)
                pe_project(0, wq, 0)
            if s == 4:
                if last:
                    pe.wait_ge(s_attn, 4 * b - 1)
                pe_max_job(pe, b, 2, 1)
                if not last:
                    pe.wait_ge(s_rest, 4 * (b + 1) + 1)
                    pe_project(0, wk, 0)
            if s == 5:
                if not first:
                    pe.wait_ge(s_mrest, 4 * b + 3)
                    pe_out_job(pe, 4 * b - 1, 1)
                if not last:
                    pe.wait_ge(s_rest, 4 * (b + 1) + 2)
                    pe_project(0, wq, 1)
            if s == 6 and not last:
                if first:
                    pe.wait_ge(s_mrest, 3)
                else:
                    pe.wait_ge(s_attn, 4 * b)
                pe_project(1, wk, 1)
            if s == 7 and not last:
                pe.wait_ge(s_rest, 4 * (b + 1) + 3)
                pe_values(0, 0)
            if s == 8:
                if last:
                    pe.wait_ge(s_attn, 4 * b)
                else:
                    pe.wait_ge(s_rest, 4 * (b + 1) + 4)
                pe_max_job(pe, b, 3, 1)
                if not last:
                    pe.wait_ge(s_v, 2 * (b + 1) + 1)
                    pe_values(0, 1)
            if s == 9:
                pe.wait_ge(s_mrest, 4 * b + 4)
                pe_out_job(pe, 4 * b, 1)
            if s == 12 and not first:
                pe.wait_ge(s_feats, TILES * b)
                if last:
                    pe.wait_ge(s_mrest, 4 * b + 2)
                else:
                    pe.wait_ge(s_v, 2 * (b + 1) + 2)
                pe_feats_t(0)
                pe.wait_ge(s_attn, 4 * b + 1)
                pe_feats_t(1)
            if s == 13:
                if not first:
                    pe.wait_ge(s_fT, 2 * b)
                    pe_expert_scores()
                if not last:
                    if first:
                        pe.wait_ge(s_attn, 1)
                    pe_max_job(pe, b + 1, 0, 1)
            if s == 14:
                if not first:
                    pe.wait_ge(s_sc, b)
                    pe_expert_scores_t()
                if not last:
                    pe.wait_ge(s_mrest, 4 * b + 5)
                pe_out_job(pe, 4 * b + 1, 1)

        def pe_tok_t(pe, n, k):
            pe.wait_ge(s_tok, n + 1)
            for c in range(CHUNKS):
                last = nc.tensor.transpose(misc[k][:, c * P:(c + 1) * P], tok_n[:, k, c * P:(c + 1) * P], ident)
            last.then_inc(s_tokT_ps, 1)

        def pe_hidden(pe, n, k, ring, w1_loads):
            pe.wait_ge(s_w1[ring], 16 * w1_loads)
            pe.wait_ge(s_tokT, CHUNKS * (n + 1))
            for f in range(BLOCKS):
                dst = hidden_bank[k][f // 4][:, (f % 4) * P:(f % 4 + 1) * P]
                for c in range(CHUNKS):
                    last = nc.tensor.matmul(dst, w1[:, ring, c, f * P:(f + 1) * P], tokT[:, k, c, :],
                                            start=(c == 0), stop=(c == CHUNKS - 1))
                if f % 4 == 3:
                    last.then_inc(s_h_ps, 1)

        def pe_second(pe, n, k, expert):
            pe.wait_ge(s_h, BLOCKS * (n + 1))
            for f in range(BLOCKS):
                last = nc.tensor.matmul(y_bank[k][:, 0:DIM], hidden[:, k, f, :],
                                        w2[:, bass.ds(expert, 1), f, :].rearrange("p o d -> p (o d)"),
                                        start=(f == 0), stop=(f == BLOCKS - 1))
            last.then_inc(s_y_ps, 1)

        def pe_slot_step(pe, r, k):
            n, _, _ = slot_at(r, k, 0)
            expert = expert_reg(pe, n)
            known = isinstance(r, int)
            if not known or n + 1 < SLOTS:
                pe_hidden(pe, n + 1, (k + 1) % 2, (k + 1) % W1_RING,
                          r * (RING // W1_RING) + (k + 1) // W1_RING + 1)
            if not known or n + 2 < SLOTS:
                pe_tok_t(pe, n + 2, k % 2)
            else:
                pe.wait_ge(s_y, n - 1)
            pe_second(pe, n, k % 2, expert)

        @block.tensor
        def _(pe):
            pe.wait_ge(s_const, 16 * LOADS)
            pe.wait_ge(s_fill, FILLS)
            pe.wait_ge(s_normed, TILES)
            pe_normed_t(0)
            pe_normed_t(1)
            pe.wait_ge(s_nT, 2)
            pe_project(0, wq, 0)
            pe_project(1, wk, 0)
            pe.wait_ge(s_rest, 1)
            pe_project(0, wq, 1)
            pe.wait_ge(s_rest, 2)
            pe_project(1, wk, 1)
            pe.wait_ge(s_rest, 3)
            pe_values(0, 0)
            pe.wait_ge(s_rest, 4)
            pe_values(1, 1)
            for v in range(2):
                pe.wait_ge(s_stack[0], 192)
                for i in range(16):
                    pe_score(pe, 16 * v + i, i, 0, v)
                if v == 0:
                    pe.wait_ge(s_v, 1)
                    pe_max_job(pe, 0, 0, 0)
            pe.wait_ge(s_mrest, 1)
            for s in range(16):
                pe_slot(pe, 0, 0, s, first=True)
            pe.wait_ge(s_v, 4)
            with pe.Fori(0, 3) as r:
                for k in range(2):
                    for s in range(16):
                        pe_slot(pe, r * 2 + 1 + k, 1 - k, s)
            for s in range(16):
                pe_slot(pe, 7, 1, s, last=True)
            pe.wait_ge(s_attn, UNITS - 2)
            pe_out_job(pe, UNITS - 2, 1)
            pe.wait_ge(s_exp, 16 * UNITS)
            for t in range(TILES):
                done = pe_values_sum(t, 1, 1, 3)
            done.then_inc(s_pv, 1)
            pe.wait_ge(s_scores, BATCHES - 1)
            pe_out_job(pe, UNITS - 1, 0)
            pe.wait_ge(s_feats, TILES * BATCHES)
            pe_feats_t(0)
            pe_feats_t(1)
            pe.wait_ge(s_fT, 2 * BATCHES)
            pe_expert_scores()
            pe.wait_ge(s_sc, BATCHES)
            pe_expert_scores_t()
            pe.wait_ge(s_counted, 1)
            nc.tensor.matmul(score_bank[0][:, 0:EXPERTS], cst[:, C_BELOW:C_BELOW + P], running[:, :, TOKEN_TILES - 1],
                             start=True, stop=True)
            nc.tensor.matmul(score_bank[0][:, EXPERTS:2 * EXPERTS], ones, running[:, :, TOKEN_TILES - 1],
                             start=True, stop=True).then_inc(s_totals, 1)
            pe.wait_ge(s_hot, 1)
            for t in range(TOKEN_TILES):
                last = nc.tensor.matmul(score_bank[1][:, 0:3 * SLOTS], place_hot[:, t, :],
                                        slot_hot[:, t].rearrange("p m s -> p (m s)"),
                                        start=(t == 0), stop=(t == TOKEN_TILES - 1))
            last.then_inc(s_found, 1)
            pe.wait_ge(s_index, 1)
            pe.wait_ge(s_w2, 16 * EXPERTS)
            pe_tok_t(pe, 0, 0)
            pe_hidden(pe, 0, 0, 0, 1)
            pe_tok_t(pe, 1, 1)
            with pe.Fori(0, LOOPED // RING) as r:
                for k in range(RING):
                    pe_slot_step(pe, r, k)
            for k in range(PEELED):
                pe_slot_step(pe, LOOPED // RING, k)

        def act_normed_t(act, b):
            for c in range(CHUNKS):
                act.wait_ge(s_nT_ps, 2 * b + c + 1)
                nc.scalar.activation(normedT[:, c, :], misc[c][:], ACT.Copy).then_inc(s_nT, 1)

        def act_part(act, b, job, bank):
            wait(act, s_parts_out[job // 2], 32 * b)
            wait_alone(act, s_qk_ps, 4 * b + job + 1, s_passed)
            scale = cst[:, bass.ds(C_ROPE + b, 1)] if job % 2 == 0 else 1.0
            nc.scalar.activation(parts[:, job, 0, :], misc[bank][:], ACT.Copy if job % 2 else ACT.Identity,
                                 scale=scale).then_inc(s_part1, 1)

        def act_values(act, b, par, pair, bank):
            act.wait_ge(s_v_ps, 2 * b + pair + 1)
            if pair == 0:
                wait(act, s_pv, 4 * (b - 1) if not isinstance(b, int) else max(0, 4 * (b - 1)))
            src = misc[bank][:].rearrange("p (t h d) -> p t h d", t=2, d=HEAD)
            nc.scalar.activation(values[:, par, 2 * pair:2 * pair + 2, :, 0:HEAD], src,
                                 ACT.Copy).then_inc(s_v, 1)

        def act_out(act, w):
            act.wait_ge(s_pv, w + 1)
            nc.scalar.activation(outT[:], value_bank[:], ACT.Copy).then_inc(s_outT, 1)

        def act_feats_t(act, b):
            for c in range(CHUNKS):
                act.wait_ge(s_fT_ps, 2 * b + c + 1)
                nc.scalar.activation(featsT[:, c, :], misc[c][:], ACT.Copy).then_inc(s_fT, 1)

        def act_scores(act, b):
            act.wait_ge(s_sc_ps, b + 1)
            nc.scalar.activation(scoreT[0:EXPERTS, :], misc[0][0:EXPERTS, :], ACT.Copy).then_inc(s_sc, 1)

        def act_scores_t(act, b):
            wait_alone(act, s_scT_ps, b + 1, s_passed)
            nc.scalar.activation(scores[:, bass.ds(b * TILES, TILES), :],
                                 misc[0][:].rearrange("p (t k) -> p t k", t=TILES)[:, :, 0:EXPERTS],
                                 ACT.Copy).then_inc(s_scores, 1)

        def act_slot(act, b, par, s, first=False, last=False):
            g, j = s // 4, s % 4
            u = 4 * b + g
            if j == 0:
                wait(act, s_pv, u - 1)
            for c in range(TILES):
                i = TILES * j + c
                act.wait_ge(s_keyed, 16 * u + i + 1)
                nc.scalar.activation(probs[:, g % 2, j, c, :], keyed_bank[i % 2][:], ACT.Exp).then_inc(s_exp, 1)
                if c == 0:
                    if j == 0 and not (first and g < 2):
                        act_out(act, u - 2)
                    if not last:
                        if s == 3:
                            act_normed_t(act, b + 1)
                        if s in (4, 5, 6, 7):
                            act_part(act, b + 1, s - 4, (0, 0, 0, 1)[s - 4])
                        if s in (8, 9):
                            act_values(act, b + 1, 1 - par, s - 8, 0)
                    if not first:
                        if s == 13:
                            act_feats_t(act, b - 1)
                        if s == 14:
                            act_scores(act, b - 1)
                        if s == 15:
                            act_scores_t(act, b - 1)

        def act_tok_t(act, n, k, ring):
            act.wait_ge(s_tokT_ps, n + 1)
            for c in range(CHUNKS):
                nc.scalar.activation(tokT[:, k, c, :], misc[k][:, c * P:(c + 1) * P], ACT.Identity,
                                     bias=params_now[:, ring, CHUNKS + c:CHUNKS + c + 1],
                                     scale=params_now[:, ring, c:c + 1]).then_inc(s_tokT, 1)

        def act_minus(act, n, ring):
            act.wait_ge(s_dot, n + 1)
            nc.scalar.activation(minus[:, ring:ring + 1], dot[:, ring:ring + 1], ACT.Exp,
                                 scale=-1.0).then_inc(s_minus, 1)

        def act_hidden(act, n, k, ring):
            for f in range(BLOCKS):
                if f % 4 == 0:
                    act.wait_ge(s_h_ps, 2 * n + f // 4 + 1)
                col = 2 * CHUNKS + f
                nc.scalar.activation(hidden[:, k, f, :], hidden_bank[k][f // 4][:, (f % 4) * P:(f % 4 + 1) * P],
                                     ACT.Relu, bias=params_now[:, ring, col:col + 1]).then_inc(s_h, 1)

        def act_slot_step(act, r, k):
            known = isinstance(r, int)
            n, ring, _ = slot_at(r, k, 1)
            if not known or n < SLOTS:
                act_hidden(act, n, (k + 1) % 2, ring)
            n, ring, _ = slot_at(r, k, 2)
            if not known or n < SLOTS:
                act_tok_t(act, n, k % 2, ring)
            n, ring, _ = slot_at(r, k, 3)
            if not known or n < SLOTS:
                act_minus(act, n, ring)

        @block.scalar
        def _(act):
            act.wait_ge(s_const, 16 * LOADS)
            act_normed_t(act, 0)
            for job in range(4):
                act_part(act, 0, job, job % 2)
            for pair in range(2):
                act_values(act, 0, 0, pair, pair)
            for s in range(16):
                act_slot(act, 0, 0, s, first=True)
            with act.Fori(0, 3) as r:
                for k in range(2):
                    for s in range(16):
                        act_slot(act, r * 2 + 1 + k, 1 - k, s)
            for s in range(16):
                act_slot(act, 7, 1, s, last=True)
            act_out(act, UNITS - 2)
            act.wait_ge(s_out_ps, UNITS - 1)
            act_out(act, UNITS - 1)
            act_feats_t(act, BATCHES - 1)
            act_scores(act, BATCHES - 1)
            act_scores_t(act, BATCHES - 1)
            for n in range(3):
                act_minus(act, n, n)
            for n in range(2):
                act_tok_t(act, n, n, n)
            act_hidden(act, 0, 0, 0)
            with act.Fori(0, LOOPED // RING) as r:
                for k in range(RING):
                    act_slot_step(act, r, k)
            for k in range(PEELED):
                act_slot_step(act, LOOPED // RING, k)

        def dve_stats(which, t, src, done):
            nc.vector.bn_stats(stats[:, which, t, :], src).then_inc(done, 1)

        def dve_moments(dve, which, b, stats_done, done):
            wait_alone(dve, stats_done, TILES * (b + 1), s_passed)
            for t in range(TILES):
                nc.vector.bn_aggr(moments[:, which, t, :], stats[:, which, t, :]).then_inc(done, 1)

        def dve_rest(dve, b, job, bank):
            dve.wait_ge(s_part1, 4 * b + job + 1)
            wait(dve, s_part3, 4 * b + job - 1)
            if job % 2 == 0:
                nc.vector.scalar_tensor_tensor(rest[:, job % 2, :], misc[bank][:], cst[:, bass.ds(C_ROPE + b, 1)],
                                               parts[:, job, 0, :], ALU.mult, ALU.subtract).then_inc(s_rest, 1)
            else:
                nc.vector.tensor_tensor(rest[:, job % 2, :], misc[bank][:], parts[:, job, 0, :],
                                        ALU.subtract).then_inc(s_rest, 1)

        def dve_max_part(dve, v, k, bank):
            dve.wait_ge(s_mT_ps, v + 1)
            wait(dve, s_m_out[k], (v - k) * 8)
            nc.vector.tensor_copy(max_parts[:, k, 0, :], misc[bank][0:UNIT_HEADS * TILES, 0:P]).then_inc(s_m1, 1)

        def dve_max_rest(dve, v, k, bank):
            dve.wait_ge(s_m1, v + 1)
            nc.vector.tensor_tensor(max_rest[:, k, :], misc[bank][0:UNIT_HEADS * TILES, 0:P],
                                    max_parts[:, k, 0, :], ALU.subtract).then_inc(s_mrest, 1)

        def dve_inv(dve, w, bank):
            dve.wait_ge(s_out_ps, w + 1)
            src = misc[bank][:].rearrange("p (t h d) -> p t h d", t=TILES, d=32)
            nc.vector.reciprocal(inv_sum[:], src[:, :, :, HEAD]).then_inc(s_inv, 1)

        def dve_attn(dve, w, bank, par, group):
            dve.wait_ge(s_inv, w + 1)
            src = misc[bank][:].rearrange("p (t h d) -> p t h d", t=TILES, d=32)[:, :, :, 0:HEAD]
            dst = attn[:, par, :, 64 * group:64 * group + 64].rearrange("p t (h d) -> p t h d", d=HEAD)
            inv = inv_sum[:].unsqueeze(3).broadcast_to([P, TILES, UNIT_HEADS, HEAD])
            nc.vector.tensor_tensor(dst, src, inv, ALU.mult).then_inc(s_attn, 1)

        def dve_rowmax(dve, tile_no, i, k):
            dve.wait_ge(s_score, tile_no + 1)
            nc.vector.reduce_max(row_max[:, k, i:i + 1], score_bank[i % 3][:], AX).then_inc(s_rowmax, 1)

        def dve_slot(dve, b, par, s, first=False, last=False):
            g, j = s // 4, s % 4
            u = 4 * b + g
            scoring = not (last and g >= 2)
            if j == 0 and scoring:
                dve.wait_ge(s_mT_ps, u + 1)
            for c in range(TILES):
                if scoring:
                    dve_rowmax(dve, 16 * (u + 2) + TILES * j + c, TILES * j + c, g % 2)
                dve_between(dve, b, par, s, c, first, last)

        def dve_between(dve, b, par, s, c, first, last):
            g = s // 4
            if s == 0 and not last:
                if c == 0:
                    dve.wait_ge(s_x, 16 * (b + 2))
                dve_stats(0, c, x_in[:, c, :], s_xst)
            if s == 1 and c == 0 and not last:
                dve_moments(dve, 0, b + 1, s_xst, s_xmom)
            if s in (1, 5, 9) or (s == 14 and not last):
                v, k, bank = {1: (4 * b + 1, 1, 0), 5: (4 * b + 2, 0, 1), 9: (4 * b + 3, 1, 1),
                              14: (4 * b + 4, 0, 1)}[s]
                if c == 1:
                    dve_max_part(dve, v, k, bank)
                if c == 2:
                    dve_max_rest(dve, v, k, bank)
            if s in (2, 6, 10, 15) and not (first and s < 10):
                w = {2: 4 * b - 2, 6: 4 * b - 1, 10: 4 * b, 15: 4 * b + 1}[s]
                if c == 0:
                    dve_inv(dve, w, 1)
                if c == 1:
                    w_par, w_group = (1 - par, 2 + (s == 6)) if s < 10 else (par, int(s == 15))
                    dve_attn(dve, w, 1, w_par, w_group)
            if s in (4, 5, 6, 7) and c == 3 and not last:
                dve_rest(dve, b + 1, s - 4, (0, 0, 0, 1)[s - 4])
            if not first:
                if s == 7:
                    if c == 0:
                        dve.wait_ge(s_attn, 4 * b)
                    dve_stats(1, c, attn[:, 1 - par, c, :], s_ast)
                if s == 8 and c == 0:
                    dve_moments(dve, 1, b - 1, s_ast, s_amom)
                if s == 10:
                    if c == 0:
                        dve.wait_ge(s_x1, b)
                    dve_stats(2, c, rows[:, c, DIM:ROW], s_x1st)
                if s == 11 and c == 0:
                    dve_moments(dve, 2, b - 1, s_x1st, s_x1mom)

        def dve_route(dve):
            V = nc.vector
            steps = [0]

            def step(ins):
                ins.then_inc(s_route, 1)
                steps[0] += 1
                dve.wait_ge(s_route, steps[0])

            def over(ap, n):
                return ap.unsqueeze(2).broadcast_to([P, ap.shape[1], n])

            def under(ap, n):
                return ap.unsqueeze(1).broadcast_to([P, n, ap.shape[1]])

            dve.wait_ge(s_out_ps, UNITS)
            step(V.memset(ones, 1.0))
            step(V.memset(no_carry, 1.0))
            step(V.memset(no_carry[:, :, 0:1], 0.0))
            step(V.tensor_scalar(less_8[:], count[:, 0:EXPERTS], float(EXPERTS), None, ALU.subtract))
            step(V.tensor_copy(count_bf, count))
            dve.wait_ge(s_scores, BATCHES)
            step(V.tensor_reduce(best[:], scores[:], AX, ALU.max))
            step(V.tensor_tensor(hits, scores[:], over(best[:], EXPERTS), ALU.is_equal))
            step(V.tensor_tensor(hits, hits, under(less_8[:], TOKEN_TILES), ALU.mult))
            step(V.tensor_reduce(first_hit[:], hits, AX, ALU.min))
            step(V.tensor_tensor(one_hot, over(less_8[:], TOKEN_TILES), under(first_hit[:], EXPERTS), ALU.is_equal))
            flat = [a.rearrange("p e t -> p (e t)") for a in (running, no_carry, one_hot)]
            step(V.tensor_tensor_scan(flat[0], flat[1], flat[2], 0.0, ALU.mult, ALU.add))
            V.tensor_copy(masked, running).then_inc(s_counted, 1)
            dve.wait_ge(s_totals, 1)
            step(V.tensor_scalar(tiles_i[:], score_bank[0][:, EXPERTS:2 * EXPERTS], float(P - 1), None, ALU.add))
            step(V.tensor_scalar(tiles_i[:], tiles_i[:], 7, None, ALU.arith_shift_right))
            step(V.tensor_copy(tiles_f[:], tiles_i[:]))
            step(V.tensor_tensor_scan(tiles_end[:], ones[:, 0:EXPERTS], tiles_f[:], 0.0, ALU.mult, ALU.add))
            step(V.tensor_tensor(slot_ge, over(count[:, 0:SLOTS], EXPERTS), under(tiles_end[:], SLOTS), ALU.is_ge))
            step(V.tensor_reduce(expert_f[:], slot_ge, AX, ALU.add))
            V.tensor_scalar(expert_of[:], expert_f[:], float(EXPERTS - 1), None, ALU.min).then_inc(s_experts, 1)
            step(V.tensor_tensor(offset[:], tiles_end[:], tiles_f[:], ALU.subtract))
            step(V.scalar_tensor_tensor(offset[:], offset[:], float(P), score_bank[0][:, 0:EXPERTS],
                                        ALU.mult, ALU.add))
            step(V.tensor_tensor(masked, running, over(offset[:], TOKEN_TILES), ALU.add))
            step(V.scalar_tensor_tensor(masked, masked, -1.0, one_hot, ALU.add, ALU.mult))
            step(V.tensor_reduce(place[:], masked.rearrange("p e t -> p t e"), AX, ALU.add))
            step(V.tensor_copy(place_i[:], place[:]))
            step(V.tensor_scalar(place_i[:], place_i[:], 7, None, ALU.arith_shift_right))
            step(V.tensor_copy(slot_f[:], place_i[:]))
            step(V.scalar_tensor_tensor(within[:], slot_f[:], -float(P), place[:], ALU.mult, ALU.add))
            for t in range(TOKEN_TILES):
                V.tensor_scalar(place_hot[:, t, :], count_bf, within[:, t:t + 1], None, ALU.is_equal)
            step(V.tensor_tensor(slot_eq, under(count[:, 0:SLOTS], TOKEN_TILES), over(slot_f[:], SLOTS),
                                 ALU.is_equal))
            V.tensor_scalar(slot_hot[:, :, 0, :], slot_eq, cst[:, C_PART:C_PART + 1], None, ALU.mult)
            V.tensor_tensor(slot_hot[:, :, 1, :], slot_eq, over(count[:, 0:TOKEN_TILES], SLOTS), ALU.mult)
            V.tensor_copy(slot_hot[:, :, 2, :], slot_eq).then_inc(s_hot, 1)
            dve.wait_ge(s_found, 1)
            step(V.tensor_copy(found[:], score_bank[1][:, 0:3 * SLOTS].rearrange("p (m s) -> p m s", m=3)))
            step(V.scalar_tensor_tensor(token_f[:], found[:, 1, :], float(P), found[:, 0, :], ALU.mult, ALU.add))
            step(V.tensor_copy(index_all[:, :, 0], token_f[:]))
            step(V.tensor_scalar(found[:, 2, :], found[:, 2, :], -float(SKIP), float(SKIP), ALU.mult, ALU.add))
            V.tensor_tensor(index_all[:, :, 1], token_f[:], found[:, 2, :], ALU.add).then_inc(s_index, 1)
            dve.wait_ge(s_index, 1)
            dve.wait_ge(s_par, 16 * 5)

        def dve_prepare(dve, n, ring):
            e = expert_reg(dve, n)
            nc.vector.tensor_copy(index_now[:, ring, :].unsqueeze(1), index_all[:, bass.ds(n, 1), :]).then_inc(s_prep, 1)
            nc.vector.tensor_copy(params_now[:, ring, :].unsqueeze(1), params[:, bass.ds(e, 1), :]).then_inc(s_prep, 1)

        def dve_features(dve, n, ring, round_1, k):
            e = expert_reg(dve, n)
            dve.wait_ge(s_gather[ring], 16 * round_1)
            nc.vector.bn_stats(slot_stats[:, 0, k, :], got[:, ring, 0:DIM]).then_inc(s_gst, 1)
            nc.vector.scalar_tensor_tensor(product, got[:, ring, 0:DIM], 1.0,
                                           cent_all[:, bass.ds(e, 1), :].rearrange("p o d -> p (o d)"),
                                           ALU.mult, ALU.mult, accum_out=dot[:, ring:ring + 1]).then_inc(s_dot, 1)
            wait_alone(dve, s_gst, n + 1, s_passed)
            nc.vector.bn_aggr(slot_mom[:, 0, k, :], slot_stats[:, 0, k, :]).then_inc(s_gmom, 1)

        def dve_alpha(dve, n, ring):
            dve.wait_ge(s_minus, n + 1)
            nc.vector.tensor_scalar(minus[:, ring:ring + 1], minus[:, ring:ring + 1], 1.0, None,
                                    ALU.add).then_inc(s_plus1, 1)
            dve.wait_ge(s_plus1, n + 1)
            nc.vector.reciprocal(alpha[:, ring:ring + 1], minus[:, ring:ring + 1]).then_inc(s_alpha, 1)

        def dve_finish(dve, n, ring, k):
            e = expert_reg(dve, n)
            dve.wait_ge(s_y_ps, n + 1)
            nc.vector.tensor_tensor(mixed[:, k, :], y_bank[k][:, 0:DIM],
                                    b2_all[:, bass.ds(e, 1), :].rearrange("p o d -> p (o d)"),
                                    ALU.add).then_inc(s_y, 1)
            dve.wait_ge(s_y, n + 1)
            dve.wait_ge(s_alpha, n + 1)
            nc.vector.scalar_tensor_tensor(mixed[:, k, :], mixed[:, k, :], alpha[:, ring:ring + 1],
                                           got[:, ring, 0:DIM], ALU.mult, ALU.add).then_inc(s_mix, 1)
            dve.wait_ge(s_mix, n + 1)
            nc.vector.bn_stats(slot_stats[:, 1, k, :], mixed[:, k, :]).then_inc(s_mst, 1)
            wait_alone(dve, s_mst, n + 1, s_passed)
            nc.vector.bn_aggr(slot_mom[:, 1, k, :], slot_stats[:, 1, k, :]).then_inc(s_mmom, 1)

        def dve_tok(dve, n, ring, k):
            wait(dve, s_tokT_ps, n - 1)
            dve.wait_ge(s_grstd, n + 1)
            nc.vector.tensor_scalar(tok_n[:, k, :], got[:, ring, 0:DIM], slot_mom[:, 0, k, 0:1],
                                    slot_rstd[:, 0, k:k + 1], ALU.subtract, ALU.mult).then_inc(s_tok, 1)

        def dve_new(dve, n, ring, k):
            dve.wait_ge(s_mrstd, n + 1)
            nc.vector.tensor_scalar(new_rows[:, ring, :], mixed[:, k, :], slot_mom[:, 1, k, 0:1],
                                    slot_rstd[:, 1, k:k + 1], ALU.subtract, ALU.mult).then_inc(s_mixn, 1)
            dve.wait_ge(s_mixn, n + 1)
            nc.vector.tensor_tensor(new_rows[:, ring, :], new_rows[:, ring, :], got[:, ring, DIM:ROW],
                                    ALU.add).then_inc(s_new, 1)

        def dve_slot_step(dve, r, k):
            known = isinstance(r, int)
            j, ring0, _ = slot_at(r, k, 0)
            n, ring, rnd = slot_at(r, k, AHEAD)
            if not known or n < SLOTS:
                wait(dve, s_scatter[ring], 16 * rnd)
                dve_prepare(dve, n, ring)
            n, ring, rnd = slot_at(r, k, 3)
            if not known or n < SLOTS:
                dve_features(dve, n, ring, rnd + 1, (k + 1) % 2)
            if not known or j > 0:
                dve_new(dve, r * RING + (k - 1), (k - 1) % RING, (k - 1) % 2)
            m, ring2, _ = slot_at(r, k, 2)
            if not known or m < SLOTS:
                dve_alpha(dve, m, ring2)
            if not known or n < SLOTS:
                dve_tok(dve, n, ring, (k + 1) % 2)
            dve_finish(dve, j, ring0, k % 2)

        @block.vector
        def _(dve):
            dve.wait_ge(s_x, 16)
            for t in range(TILES):
                dve_stats(0, t, x_in[:, t, :], s_xst)
            dve_moments(dve, 0, 0, s_xst, s_xmom)
            dve.wait_ge(s_const, 16 * LOADS)
            for job in range(4):
                dve_rest(dve, 0, job, job % 2)
            for v in range(2):
                for i in range(16):
                    dve_rowmax(dve, 16 * v + i, i, v)
                if v == 0:
                    dve_max_part(dve, 0, 0, 0)
                    dve_max_rest(dve, 0, 0, 0)
            for s in range(16):
                dve_slot(dve, 0, 0, s, first=True)
            with dve.Fori(0, 3) as r:
                for k in range(2):
                    for s in range(16):
                        dve_slot(dve, r * 2 + 1 + k, 1 - k, s)
            for s in range(16):
                dve_slot(dve, 7, 1, s, last=True)
            for w, bank in ((UNITS - 2, 1), (UNITS - 1, 0)):
                dve.wait_ge(s_attn, w)
                dve_inv(dve, w, bank)
                dve_attn(dve, w, bank, 1, w % 4)
            dve.wait_ge(s_attn, UNITS)
            for t in range(TILES):
                dve_stats(1, t, attn[:, 1, t, :], s_ast)
            dve_moments(dve, 1, BATCHES - 1, s_ast, s_amom)
            dve.wait_ge(s_x1, BATCHES)
            for t in range(TILES):
                dve_stats(2, t, rows[:, t, DIM:ROW], s_x1st)
            dve_moments(dve, 2, BATCHES - 1, s_x1st, s_x1mom)
            dve_route(dve)
            for n in range(4):
                dve_prepare(dve, n, n)
            for n in range(3):
                dve_features(dve, n, n, 1, n % 2)
                dve_tok(dve, n, n, n % 2)
            for n in range(2):
                dve_alpha(dve, n, n)
            for k in range(RING):
                dve_slot_step(dve, 0, k)
            with dve.Fori(1, LOOPED // RING) as r:
                for k in range(RING):
                    dve_slot_step(dve, r, k)
            for k in range(PEELED):
                dve_slot_step(dve, LOOPED // RING, k)
            dve_new(dve, SLOTS - 1, (SLOTS - 1) % RING, (SLOTS - 1) % 2)

        def pool_rstd(pool, which, b, moments_done, steps):
            wait_alone(pool, moments_done, TILES * (b + 1), s_passed)
            nc.gpsimd.tensor_scalar(rstd[:, which, :], moments[:, which, :, 1], EPS, None,
                                    ALU.add).then_inc(s_pool, 1)
            pool.wait_ge(s_pool, steps + 1)
            nc.gpsimd.tensor_tensor(rstd[:, which, :], rstd[:, which, :], half_neg[:], ALU.pow).then_inc(s_pool, 1)
            wait_alone(pool, s_pool, steps + 2, s_passed)

        def pool_normalise(which, t, dst, src, done):
            nc.gpsimd.tensor_scalar(dst, src, moments[:, which, t, 0:1], rstd[:, which, t:t + 1],
                                    ALU.subtract, ALU.mult).then_inc(done, 1)

        def pool_normed(pool, b, steps):
            pool_rstd(pool, 0, b, s_xmom, steps)
            for t in range(TILES):
                pool_normalise(0, t, x_in[:, t, :], x_in[:, t, :], s_normed)

        def pool_parts(pool, b, job):
            wait_alone(pool, s_rest, 4 * b + job + 1, s_passed)
            nc.gpsimd.tensor_copy(parts[:, job, 1, :], rest[:, job % 2, :]).then_inc(s_part2, 1)
            pool.wait_ge(s_part2, 4 * b + job + 1)
            nc.gpsimd.tensor_tensor(parts[:, job, 2, :], rest[:, job % 2, :], parts[:, job, 1, :],
                                    ALU.subtract).then_inc(s_part3, 1)

        def pool_max_parts(pool, v, k):
            wait_alone(pool, s_mrest, v + 1, s_passed)
            nc.gpsimd.tensor_copy(max_parts[:, k, 1, :], max_rest[:, k, :]).then_inc(s_m2, 1)
            pool.wait_ge(s_m2, v + 1)
            nc.gpsimd.tensor_tensor(max_parts[:, k, 2, :], max_rest[:, k, :], max_parts[:, k, 1, :],
                                    ALU.subtract).then_inc(s_m3, 1)

        def pool_residual(pool, b, par, steps):
            pool_rstd(pool, 1, b, s_amom, steps)
            wait_alone(pool, s_res, 16 * (b + 1), s_passed)
            for t in range(TILES):
                pool_normalise(1, t, rows[:, t, DIM:ROW], attn[:, par, t, :], s_attn_n)
            pool.wait_ge(s_attn_n, TILES * (b + 1))
            nc.gpsimd.tensor_tensor(rows[:, :, DIM:ROW], rows[:, :, DIM:ROW], x_res[:], ALU.add).then_inc(s_x1, 1)

        def pool_feats(pool, b, steps):
            pool_rstd(pool, 2, b, s_x1mom, steps)
            for t in range(TILES):
                pool_normalise(2, t, rows[:, t, 0:DIM], rows[:, t, DIM:ROW], s_feats)

        def pool_batch(pool, b, par, first=False, last=False):
            steps = 2 + 2 * b + (4 * (b - 1) if not first else 0)
            if not last:
                pool_normed(pool, b + 1, steps)
            pool_max_parts(pool, 4 * b + 1, 1)
            if not last:
                pool_parts(pool, b + 1, 0)
            pool_max_parts(pool, 4 * b + 2, 0)
            if not last:
                for job in (1, 2, 3):
                    pool_parts(pool, b + 1, job)
            if not first:
                pool_residual(pool, b - 1, 1 - par, steps + (0 if last else 2))
            pool_max_parts(pool, 4 * b + 3, 1)
            if not first:
                pool_feats(pool, b - 1, steps + (2 if last else 4))
            if not last:
                pool_max_parts(pool, 4 * b + 4, 0)

        out_rows = out.rearrange("b s d -> (b s) d")

        def pool_gather(pool, n, ring):
            wait_alone(pool, s_prep, 2 * n + 2, s_passed)
            nc.gpsimd.indirect_dma_start(
                out=got[:, ring, :], out_offset=None, in_=rows_dram,
                in_offset=bass.IndirectOffsetOnAxis(ap=index_now[:, ring, 0:1].bitcast(U32), axis=0),
                bounds_check=TOKENS - 1, oob_is_err=False).then_inc(s_gather[ring], 16)

        def pool_slot_rstd(pool, which, k, step, done):
            nc.gpsimd.tensor_scalar(slot_rstd[:, which, k:k + 1], slot_mom[:, which, k, 1:2], EPS, None,
                                    ALU.add).then_inc(s_chain, 1)
            pool.wait_ge(s_chain, step)
            nc.gpsimd.tensor_tensor(slot_rstd[:, which, k:k + 1], slot_rstd[:, which, k:k + 1], half_neg[:, 0:1],
                                    ALU.pow).then_inc(done, 1)

        def pool_scatter(pool, n, ring):
            wait_alone(pool, s_new, n + 1, s_passed)
            nc.gpsimd.indirect_dma_start(
                out=out_rows, out_offset=bass.IndirectOffsetOnAxis(ap=index_now[:, ring, 1:2].bitcast(U32), axis=0),
                in_=new_rows[:, ring, :], in_offset=None,
                bounds_check=TOKENS - 1, oob_is_err=False).then_inc(s_scatter[ring], 16)

        def pool_slot_step(pool, r, k):
            known = isinstance(r, int)
            j, _, _ = slot_at(r, k, 0)
            n, ring, _ = slot_at(r, k, AHEAD)
            if not known or n < SLOTS:
                pool_gather(pool, n, ring)
            m, _, _ = slot_at(r, k, 3)
            step = j * 2 + 4
            if not known or m < SLOTS:
                wait_alone(pool, s_gmom, m + 1, s_passed)
                pool_slot_rstd(pool, 0, (k + 1) % 2, step, s_grstd)
                step = step + 1
            elif j > SLOTS - 3:
                step = step - (j - (SLOTS - 3))
            if not known or j > 0:
                pool_scatter(pool, r * RING + (k - 1), (k - 1) % RING)
            wait_alone(pool, s_mmom, j + 1, s_passed)
            pool_slot_rstd(pool, 1, k % 2, step, s_mrstd)

        @block.gpsimd
        def _(pool):
            nc.gpsimd.memset(half_neg[:], -0.5).then_inc(s_fill, 1)
            nc.gpsimd.memset(values[:, :, :, :, HEAD:HEAD + 1], 1.0).then_inc(s_fill, 1)
            nc.gpsimd.memset(values[:, :, :, :, HEAD + 1:32], 0.0).then_inc(s_fill, 1)
            nc.gpsimd.memset(scoreT[:], 0.0).then_inc(s_fill, 1)
            pool.wait_ge(s_fill, FILLS)
            pool_normed(pool, 0, 0)
            for job in range(4):
                pool_parts(pool, 0, job)
            pool_max_parts(pool, 0, 0)
            pool_batch(pool, 0, 0, first=True)
            with pool.Fori(0, 3) as r:
                pool_batch(pool, r * 2 + 1, 1)
                pool_batch(pool, r * 2 + 2, 0)
            pool_batch(pool, 7, 1, last=True)
            steps = 2 + 2 * 7 + 4 * 7
            pool_residual(pool, 7, 1, steps)
            pool_feats(pool, 7, steps + 2)
            pool.wait_ge(s_rows, 16 * BATCHES)
            pool.wait_ge(s_index, 1)
            for n in range(4):
                pool_gather(pool, n, n)
            for n in range(3):
                wait_alone(pool, s_gmom, n + 1, s_passed)
                pool_slot_rstd(pool, 0, n % 2, n + 1, s_grstd)
            for k in range(RING):
                pool_slot_step(pool, 0, k)
            with pool.Fori(1, LOOPED // RING) as r:
                for k in range(RING):
                    pool_slot_step(pool, r, k)
            for k in range(PEELED):
                pool_slot_step(pool, LOOPED // RING, k)
            pool_scatter(pool, SLOTS - 1, (SLOTS - 1) % RING)


def table():
    t = np.zeros((P, C_END), np.float32)
    t[:, C_IDENT:C_IDENT + P] = np.eye(P)
    t[:, C_BELOW:C_BELOW + P] = np.triu(np.ones((P, P)), 1)
    half = HEAD // 2
    theta = 1.0 / 10000.0 ** (np.arange(0, HEAD, 2, dtype=np.float32) / np.float32(HEAD))
    for b in range(BATCHES):
        angle = (np.float32(b) * theta.astype(np.float32)).astype(np.float64)
        factor = np.concatenate([np.cos(angle) + np.sin(angle), np.cos(angle) - np.sin(angle)])
        t[:, C_ROPE + b] = np.tile(factor * factor / np.sqrt(HEAD), P // HEAD)
    t[:, C_COUNT:C_COUNT + P] = np.arange(P)
    t[:, C_PART] = np.arange(P)
    return t


def kernel(L0_attn_x, L0_attn_Wq, L0_attn_Wk, L0_attn_Wv, L0_ffn_centroids, L0_ffn_gamma, L0_ffn_beta,
           L0_ffn_W1, L0_ffn_b1, L0_ffn_W2, L0_ffn_b2):
    import concourse.bacc as bacc
    import ml_dtypes
    from concourse.bass_utils import run_bass_kernel_spmd

    def laid(a, *order):
        return np.ascontiguousarray(np.transpose(np.asarray(a), order))

    E, C = EXPERTS, CHUNKS
    arrays = {
        "x": np.ascontiguousarray(L0_attn_x),
        "wqt": laid(L0_attn_Wq, 1, 0), "wkt": laid(L0_attn_Wk, 1, 0), "wvt": laid(L0_attn_Wv, 1, 0),
        "cent": np.ascontiguousarray(L0_ffn_centroids),
        "cent_t": laid(L0_ffn_centroids, 1, 0),
        "gamma_t": laid(np.asarray(L0_ffn_gamma).reshape(E, C, P), 2, 0, 1),
        "beta_t": laid(np.asarray(L0_ffn_beta).reshape(E, C, P), 2, 0, 1),
        "w1t": laid(np.asarray(L0_ffn_W1).reshape(E, HIDDEN, C, P), 0, 3, 2, 1),
        "b1_t": laid(np.asarray(L0_ffn_b1).reshape(E, BLOCKS, P), 2, 0, 1),
        "w2t": laid(np.asarray(L0_ffn_W2).reshape(E, DIM, BLOCKS, P), 3, 0, 2, 1),
        "b2": np.ascontiguousarray(L0_ffn_b2),
        "consts": table(),
        "minus_ones": np.full((FULL - STACK, 2, HEADS, SEQ), -1, ml_dtypes.bfloat16),
    }
    nc = bacc.Bacc("TRN2", target_bir_lowering=False, num_devices=1)
    args = [nc.dram_tensor(name, a.shape, mybir.dt.from_np(a.dtype), kind="ExternalInput").ap() for name, a in arrays.items()]
    out = nc.dram_tensor("out", (BATCHES, SEQ, DIM), F32, kind="ExternalOutput").ap()
    build(nc, *args, out)
    result = run_bass_kernel_spmd(nc, [arrays], core_ids=[0])
    return result.results[0]["out"]
```

```python
from contextlib import ExitStack

import numpy as np

import concourse.bass as bass
from concourse import mybir
from concourse.alu_op_type import AluOpType as ALU

ACT = mybir.ActivationFunctionType
F32 = mybir.dt.float32
BF16 = mybir.dt.bfloat16
I32 = mybir.dt.int32
U32 = mybir.dt.uint32
AX = mybir.AxisListType.X

P = 128
EPS = 1e-5
BATCHES, SEQ, DIM = 8, 512, 256
HEADS, HEAD = 16, 16
CHUNKS = DIM // P
TILES = SEQ // P
GROUPS = 4
UNIT_HEADS = HEADS // GROUPS
UNITS = BATCHES * GROUPS
TOKENS = BATCHES * SEQ
TOKEN_TILES = TOKENS // P
EXPERTS, HIDDEN = 8, 1024
BLOCKS = HIDDEN // P
SLOTS = (TOKENS - EXPERTS) // P + EXPERTS
ROW = 2 * DIM
SKIP = 2 * TOKENS

Q_PARTS = (0, 0, 1, 1, 0, 2)
K_PARTS = (0, 1, 0, 1, 2, 0)
STACK = len(Q_PARTS) * HEAD
MAX_PARTS = 3
FULL = STACK + MAX_PARTS

C_IDENT, C_BELOW, C_ROPE, C_COUNT, C_PART, C_END = 0, P, 2 * P, 2 * P + BATCHES, 3 * P + BATCHES, 3 * P + BATCHES + 1

RING = 6
W1_RING = 3
AHEAD = 4
LOOPED = (SLOTS - AHEAD) // RING * RING
PEELED = SLOTS - LOOPED
FILLS = 4
LOADS = 6


def wait(eng, sem, value):
    if not isinstance(value, int) or value > 0:
        eng.wait_ge(sem, value)


def wait_alone(eng, sem, value, passed):
    eng.wait_ge(sem, value).then_inc(passed, 1)


def build(nc, x, wqt, wkt, wvt, cent, cent_t, gamma_t, beta_t, w1t, b1_t, w2t, b2, consts, minus_ones, out):
    ctx = ExitStack()
    with ctx:
        def sb(name, shape, dt=F32):
            return ctx.enter_context(nc.sbuf_tensor(name, shape, dt))

        def sem(name):
            return ctx.enter_context(nc.semaphore(name))

        def dram(name, shape, dt=F32):
            return nc.dram_tensor(name, shape, dt, kind="Internal").ap()

        parts_dram = dram("parts_dram", (2, 4, MAX_PARTS, P, SEQ), BF16)
        max_dram = dram("max_dram", (2, MAX_PARTS, HEADS, P), BF16)
        rows_dram = dram("rows_dram", (TOKENS, ROW))

        cst = sb("cst", [P, C_END])
        ident = cst[:, C_IDENT:C_IDENT + P]
        wq = sb("wq", [P, CHUNKS, DIM])
        wk = sb("wk", [P, CHUNKS, DIM])
        wv = sb("wv", [P, CHUNKS, DIM])
        centT = sb("centT", [P, CHUNKS, EXPERTS])
        half_neg = sb("half_neg", [P, TILES])
        x_in = sb("x_in", [P, TILES, DIM])
        x_res = sb("x_res", [P, TILES, DIM])
        normedT = sb("normedT", [P, CHUNKS, SEQ])
        parts = sb("parts", [P, 4, MAX_PARTS, SEQ], BF16)
        rest = sb("rest", [P, 2, SEQ])
        QS = sb("QS", [P, 2, HEADS, SEQ], BF16)
        KS = sb("KS", [P, 2, HEADS, SEQ], BF16)
        values = sb("values", [P, 2, TILES, HEADS, 32])
        big = sb("big", [P, 2 * UNIT_HEADS, TILES * SEQ])
        probs = big[:, :, :].rearrange("p (u h) (t q) -> p u h t q", u=2, t=TILES)
        w2 = big[:, :, :].rearrange("p e (f d) -> p e f d", f=BLOCKS)
        row_max = sb("row_max", [P, 2, UNIT_HEADS * TILES])
        max_parts = sb("max_parts", [UNIT_HEADS * TILES, 2, MAX_PARTS, P], BF16)
        max_rest = sb("max_rest", [UNIT_HEADS * TILES, 2, P])
        outT = sb("outT", [P, SEQ])
        attn = sb("attn", [P, 2, TILES, DIM])
        inv_sum = sb("inv_sum", [P, TILES, UNIT_HEADS])
        rows = sb("rows", [P, TILES, ROW])
        featsT = normedT
        scoreT = sb("scoreT", [P, SEQ])
        scores = sb("scores", [P, TOKEN_TILES, EXPERTS])
        stats = sb("stats", [P, 3, TILES, 6])
        moments = sb("moments", [P, 3, TILES, 2])
        rstd = sb("rstd", [P, 3, TILES])
        shift = sb("shift", [P, 3, TILES])

        score_bank = [ctx.enter_context(nc.psum_tensor(f"score_bank{i}", [P, SEQ], F32)) for i in range(3)]
        keyed_bank = [ctx.enter_context(nc.psum_tensor(f"keyed_bank{i}", [P, SEQ], F32)) for i in range(2)]
        value_bank = ctx.enter_context(nc.psum_tensor("value_bank", [P, SEQ], F32))
        misc = [ctx.enter_context(nc.psum_tensor(f"misc{i}", [P, SEQ], F32)) for i in range(2)]

        s_const = sem("s_const")
        s_fill = sem("s_fill")
        s_passed = sem("s_passed")
        s_x = sem("s_x")
        s_res = sem("s_res")
        s_xst = sem("s_xst")
        s_xmom = sem("s_xmom")
        s_pool = sem("s_pool")
        s_scale = [sem(f"s_scale{i}") for i in range(3)]
        s_normed = sem("s_normed")
        s_nT_ps = sem("s_nT_ps")
        s_nT = sem("s_nT")
        s_qk_ps = sem("s_qk_ps")
        s_part1 = sem("s_part1")
        s_rest = sem("s_rest")
        s_part2 = sem("s_part2")
        s_part3 = sem("s_part3")
        s_parts_out = [sem("s_parts_out0"), sem("s_parts_out1")]
        s_stack = [sem("s_stack0"), sem("s_stack1")]
        s_v_ps = sem("s_v_ps")
        s_v = sem("s_v")
        s_score = sem("s_score")
        s_rowmax = sem("s_rowmax")
        s_mT_ps = sem("s_mT_ps")
        s_m1 = sem("s_m1")
        s_mrest = sem("s_mrest")
        s_m2 = sem("s_m2")
        s_mrest2 = sem("s_mrest2")
        s_m3 = sem("s_m3")
        s_m_out = [sem("s_m_out0"), sem("s_m_out1")]
        s_m_row = [sem("s_m_row0"), sem("s_m_row1")]
        s_keyed = sem("s_keyed")
        s_exp = sem("s_exp")
        s_pv = sem("s_pv")
        s_outT = sem("s_outT")
        s_out_ps = sem("s_out_ps")
        s_inv = sem("s_inv")
        s_attn = sem("s_attn")
        s_ast = sem("s_ast")
        s_amom = sem("s_amom")
        s_attn_n = sem("s_attn_n")
        s_x1 = sem("s_x1")
        s_x1st = sem("s_x1st")
        s_x1mom = sem("s_x1mom")
        s_feats = sem("s_feats")
        s_rows = sem("s_rows")
        s_fT_ps = sem("s_fT_ps")
        s_fT = sem("s_fT")
        s_sc_ps = sem("s_sc_ps")
        s_sc = sem("s_sc")
        s_scT_ps = sem("s_scT_ps")
        s_scores = sem("s_scores")

        count = cst[:, C_COUNT:C_COUNT + P]
        small = rest[:].rearrange("p a n -> p (a n)")
        one_hot, running, masked, no_carry = (small[:, i * 256:(i + 1) * 256].rearrange(
            "p (e t) -> p e t", e=EXPERTS) for i in range(4))
        hits = x_res[:, 0, :].rearrange("p (t e) -> p t e", e=EXPERTS)
        count_bf = x_res[:, 1, 0:P // 2].bitcast(BF16)
        slot_ge = x_in[:].rearrange("p t d -> p (t d)")[:, 0:SLOTS * EXPERTS].rearrange("p (s e) -> p s e", e=EXPERTS)
        ones = outT[:, 0:P]
        place_hot = attn[:].rearrange("p a t d -> p (a t d)").bitcast(BF16).rearrange("p (t r) -> p t r", r=P)
        first = QS[:].rearrange("p a h n -> p (a h n)").bitcast(F32)
        second = KS[:].rearrange("p a h n -> p (a h n)").bitcast(F32)
        W = HIDDEN * CHUNKS
        w1 = first[:, 0:W1_RING * W].rearrange("p (k c f) -> p k c f", k=W1_RING, c=CHUNKS)
        hidden = first[:, W1_RING * W:(W1_RING + 1) * W].rearrange("p (k f t) -> p k f t", k=2, f=BLOCKS)
        third = values[:].rearrange("p a t h d -> p (a t h d)")
        tokT = third[:, 0:512].rearrange("p (k c t) -> p k c t", k=2, c=CHUNKS)
        new_rows = third[:, 512:512 + RING * DIM].rearrange("p (k d) -> p k d", k=RING)
        product = third[:, 512 + RING * DIM:768 + RING * DIM]
        slot_eq = third[:, 0:TOKEN_TILES * SLOTS].rearrange("p (t s) -> p t s", s=SLOTS)
        n_hot = TOKEN_TILES * 3 * SLOTS
        slot_hot = third[:, TOKEN_TILES * SLOTS:TOKEN_TILES * SLOTS + n_hot // 2].bitcast(BF16).rearrange(
            "p (t m s) -> p t m s", m=3, s=SLOTS)
        b2_all = second[:, 0:W].rearrange("p (e d) -> p e d", e=EXPERTS)
        cent_all = second[:, W:2 * W].rearrange("p (e d) -> p e d", e=EXPERTS)
        got = second[:, 2 * W:2 * W + RING * ROW].rearrange("p (k r) -> p k r", k=RING)
        tok_n = second[:, 2 * W + RING * ROW:2 * W + RING * ROW + 512].rearrange("p (k d) -> p k d", k=2)
        mixed = second[:, 2 * W + RING * ROW + 512:4 * W].rearrange("p (k d) -> p k d", k=2)
        best = sb("best", [P, TOKEN_TILES])
        first_hit = sb("first_hit", [P, TOKEN_TILES])
        less_8 = sb("less_8", [P, EXPERTS])
        tiles_i = sb("tiles_i", [P, EXPERTS], I32)
        tiles_f = sb("tiles_f", [P, EXPERTS])
        tiles_end = sb("tiles_end", [P, EXPERTS])
        offset = sb("offset", [P, EXPERTS])
        place = sb("place", [P, TOKEN_TILES])
        place_i = sb("place_i", [P, TOKEN_TILES], I32)
        slot_f = sb("slot_f", [P, TOKEN_TILES])
        within = sb("within", [P, TOKEN_TILES])
        expert_f = sb("expert_f", [P, SLOTS])
        expert_of = sb("expert_of", [P, SLOTS], I32)
        found = sb("found", [P, 3, SLOTS])
        token_f = sb("token_f", [P, SLOTS])
        index_all = sb("index_all", [P, SLOTS, 2], I32)
        index_now = sb("index_now", [P, RING, 2], I32)
        NPAR = 2 * CHUNKS + BLOCKS
        params = sb("params", [P, EXPERTS, NPAR])
        params_now = sb("params_now", [P, RING, NPAR])
        slot_stats = sb("slot_stats", [P, 2, 2, 6])
        slot_mom = sb("slot_mom", [P, 2, 2, 2])
        slot_rstd = sb("slot_rstd", [P, 2, 2])
        dot = sb("dot", [P, RING])
        minus = sb("minus", [P, RING])
        alpha = sb("alpha", [P, RING])

        hidden_bank = ((score_bank[0], score_bank[1]), (score_bank[2], keyed_bank[0]))
        y_bank = (keyed_bank[1], value_bank)

        s_route = sem("s_route")
        s_counted = sem("s_counted")
        s_totals = sem("s_totals")
        s_experts = sem("s_experts")
        s_hot = sem("s_hot")
        s_found = sem("s_found")
        s_index = sem("s_index")
        s_par = sem("s_par")
        s_w2 = sem("s_w2")
        s_w1 = [sem(f"s_w1_{i}") for i in range(W1_RING)]
        s_prep = sem("s_prep")
        s_gather = [sem(f"s_gather{i}") for i in range(RING)]
        s_scatter = [sem(f"s_scatter{i}") for i in range(RING)]
        s_gst = sem("s_gst")
        s_gmom = sem("s_gmom")
        s_dot = sem("s_dot")
        s_minus = sem("s_minus")
        s_plus1 = sem("s_plus1")
        s_alpha = sem("s_alpha")
        s_chain = sem("s_chain")
        s_grstd = sem("s_grstd")
        s_mrstd = sem("s_mrstd")
        s_tok = sem("s_tok")
        s_tokT_ps = sem("s_tokT_ps")
        s_tokT = sem("s_tokT")
        s_h_ps = sem("s_h_ps")
        s_h = sem("s_h")
        s_y_ps = sem("s_y_ps")
        s_y = sem("s_y")
        s_mix = sem("s_mix")
        s_mst = sem("s_mst")
        s_mmom = sem("s_mmom")
        s_mixn = sem("s_mixn")
        s_new = sem("s_new")

        block = ctx.enter_context(nc.Block())
        x_tiled = x.rearrange("b (t p) d -> b p t d", p=P)
        rows_tiled = rows_dram.rearrange("(b t p) r -> b p t r", p=P, t=TILES)

        def slot_at(r, k, ahead):
            return r * RING + (k + ahead), (k + ahead) % RING, r + (k + ahead) // RING

        def expert_reg(eng, n):
            return eng.value_load(expert_of[0:1, bass.ds(n, 1)], min_val=0, max_val=EXPERTS - 1)

        def sp_load_x(sp, b):
            wait(sp, s_nT_ps, CHUNKS * b)
            sp.dma_start(x_in[:], x_tiled[b]).then_inc(s_x, 16)

        def sp_load_residual(sp, b):
            sp.dma_start(x_res[:], x_tiled[b]).then_inc(s_res, 16)

        def sp_parts_out(sp, b, par, half):
            for kind in (0, 1):
                job = 2 * half + kind
                sp.wait_ge(s_part3, 4 * b + job + 1)
                sp.dma_start(parts_dram[par, job].rearrange("k p n -> p k n"),
                             parts[:, job]).then_inc(s_parts_out[half], 16)

        def sp_stack(sp, b, par, half):
            wait(sp, s_keyed, 64 * (b - 1) if not isinstance(b, int) else max(0, 64 * (b - 1)))
            sp.wait_ge(s_parts_out[half], 32 * (b + 1))
            for kind, stack, order in ((0, QS, Q_PARTS), (1, KS, K_PARTS)):
                for blk, part in enumerate(order):
                    src = parts_dram[par, 2 * half + kind, part].rearrange("(h d) n -> d h n", d=HEAD)
                    sp.dma_start(stack[blk * HEAD:(blk + 1) * HEAD, par, half * 8:half * 8 + 8, :],
                                 src).then_inc(s_stack[half], 16)

        def sp_max_out(sp, b, group):
            k = group % 2
            sp.wait_ge(s_m3, 4 * b + group + 1)
            sp.dma_start(max_dram[k].rearrange("m r n -> r m n"), max_parts[:, k]).then_inc(s_m_out[k], 16)

        def sp_max_rows(sp, b, group, par):
            k = group % 2
            sp.wait_ge(s_m_out[k], (2 * b + group // 2 + 1) * 16)
            rows_of = QS[STACK:FULL, par, 4 * group:4 * group + 4, :].rearrange("m h (t q) -> m (h t) q", t=TILES)
            sp.dma_start(rows_of, max_dram[k]).then_inc(s_m_row[k], 16)

        def sp_store_rows(sp, b):
            sp.wait_ge(s_feats, TILES * (b + 1))
            sp.dma_start(rows_tiled[b], rows[:]).then_inc(s_rows, 16)

        def sp_batch(sp, b, par, first=False, last=False):
            if not last:
                sp_load_x(sp, b + 1)
            if not first:
                sp_load_residual(sp, b - 1)
            sp_max_out(sp, b, 1)
            sp_max_rows(sp, b, 1, par)
            if not last:
                sp_parts_out(sp, b + 1, 1 - par, 0)
            sp_max_out(sp, b, 2)
            if not last:
                sp_stack(sp, b + 1, 1 - par, 0)
            sp_max_rows(sp, b, 2, par)
            if not last:
                sp_parts_out(sp, b + 1, 1 - par, 1)
                sp_stack(sp, b + 1, 1 - par, 1)
            sp_max_out(sp, b, 3)
            sp_max_rows(sp, b, 3, par)
            if not first:
                sp_store_rows(sp, b - 1)
                sp.wait_ge(s_rows, 16 * b)
            if not last:
                sp_max_out(sp, b + 1, 0)
                sp_max_rows(sp, b + 1, 0, 1 - par)

        def sp_w1(sp, n, k):
            e = expert_reg(sp, n)
            sp.dma_start(w1[:, k], w1t[bass.ds(e, 1)].rearrange("o p c f -> (o p) c f")).then_inc(s_w1[k], 16)

        def sp_slot(sp, r, k):
            n, _, _ = slot_at(r, k, 0)
            if not isinstance(r, int) or n + W1_RING < SLOTS:
                sp.wait_ge(s_h_ps, 2 * (n + 1))
                sp_w1(sp, n + W1_RING, k % W1_RING)

        @block.sync
        def _(sp):
            sp.dma_start(x_in[:], x_tiled[0]).then_inc(s_x, 16)
            sp.dma_start(cst[:], consts).then_inc(s_const, 16)
            for tile, src in ((wq, wqt), (wk, wkt), (wv, wvt)):
                sp.dma_start(tile[:], src.rearrange("(c p) n -> p c n", p=P)).then_inc(s_const, 16)
            sp.dma_start(centT[:], cent_t.rearrange("(c p) e -> p c e", p=P)).then_inc(s_const, 16)
            sp.dma_start(KS[STACK:FULL, :, :, :], minus_ones).then_inc(s_const, 16)
            for half in range(2):
                sp_parts_out(sp, 0, 0, half)
                sp_stack(sp, 0, 0, half)
            sp_max_out(sp, 0, 0)
            sp_max_rows(sp, 0, 0, 0)
            sp_batch(sp, 0, 0, first=True)
            with sp.Fori(0, 3) as r:
                sp_batch(sp, r * 2 + 1, 1)
                sp_batch(sp, r * 2 + 2, 0)
            sp_batch(sp, 7, 1, last=True)
            sp_load_residual(sp, 7)
            sp_store_rows(sp, 7)
            sp.wait_ge(s_keyed, 16 * UNITS)
            sp.dma_start(b2_all, b2.partition_broadcast(P)).then_inc(s_par, 16)
            sp.dma_start(cent_all, cent.partition_broadcast(P)).then_inc(s_par, 16)
            sp.dma_start(params[:, :, 0:CHUNKS], gamma_t).then_inc(s_par, 16)
            sp.dma_start(params[:, :, CHUNKS:2 * CHUNKS], beta_t).then_inc(s_par, 16)
            sp.dma_start(params[:, :, 2 * CHUNKS:NPAR], b1_t).then_inc(s_par, 16)
            sp.wait_ge(s_pv, UNITS)
            for e in range(EXPERTS):
                sp.dma_start(w2[:, e], w2t[:, e]).then_inc(s_w2, 16)
            sp.wait_ge(s_experts, 1)
            for n in range(W1_RING):
                sp_w1(sp, n, n)
            with sp.Fori(0, LOOPED // RING) as r:
                for k in range(RING):
                    sp_slot(sp, r, k)
            for k in range(PEELED):
                sp_slot(sp, LOOPED // RING, k)
            for k in range(RING):
                sp.wait_ge(s_scatter[k], 16 * ((SLOTS - k + RING - 1) // RING))

        def pe_normed_t(c):
            for t in range(TILES):
                last = nc.tensor.transpose(misc[c][:, t * P:(t + 1) * P], x_in[:, t, c * P:(c + 1) * P], ident)
            last.then_inc(s_nT_ps, 1)

        def pe_project(bank, weight, half, chunks=range(CHUNKS)):
            for c in chunks:
                last = nc.tensor.matmul(misc[bank][:], weight[:, c, half * P:(half + 1) * P], normedT[:, c, :],
                                        start=(c == 0), stop=(c == CHUNKS - 1))
            if c == CHUNKS - 1:
                last.then_inc(s_qk_ps, 1)

        def pe_values(bank, pair, which=range(2)):
            for i in which:
                t = 2 * pair + i
                for c in range(CHUNKS):
                    last = nc.tensor.matmul(misc[bank][:, i * DIM:(i + 1) * DIM], normedT[:, c, t * P:(t + 1) * P],
                                            wv[:, c, :], start=(c == 0), stop=(c == CHUNKS - 1))
            if i == 1:
                last.then_inc(s_v_ps, 1)

        def pe_max_t(bank, k):
            nc.tensor.transpose(misc[bank][0:UNIT_HEADS * TILES, 0:P], row_max[:, k, :], ident).then_inc(s_mT_ps, 1)

        def pe_out_t(bank):
            for t in range(TILES):
                last = nc.tensor.transpose(misc[bank][:, t * P:(t + 1) * P], outT[:, t * P:(t + 1) * P], ident)
            last.then_inc(s_out_ps, 1)

        def pe_feats_t(c):
            for t in range(TILES):
                last = nc.tensor.transpose(misc[c][:, t * P:(t + 1) * P], rows[:, t, c * P:(c + 1) * P], ident)
            last.then_inc(s_fT_ps, 1)

        def pe_expert_scores():
            for c in range(CHUNKS):
                last = nc.tensor.matmul(misc[0][0:EXPERTS, :], centT[:, c, :], featsT[:, c, :],
                                        start=(c == 0), stop=(c == CHUNKS - 1))
            last.then_inc(s_sc_ps, 1)

        def pe_expert_scores_t():
            for t in range(TILES):
                last = nc.tensor.transpose(misc[0][:, t * P:(t + 1) * P], scoreT[:, t * P:(t + 1) * P], ident)
            last.then_inc(s_scT_ps, 1)

        def pe_score(pe, tile_no, i, par, group):
            head, t = 4 * group + i // TILES, i % TILES
            back = 3 if i >= 3 else (1 if i == 0 else 3)
            wait(pe, s_rowmax, tile_no - back + 1)
            nc.tensor.matmul(score_bank[i % 3][:], QS[0:STACK, par, head, t * P:(t + 1) * P],
                             KS[0:STACK, par, head, :], start=True, stop=True).then_inc(s_score, 1)

        def pe_keyed(pe, tile_no, i, par, group):
            head, t = 4 * group + i // TILES, i % TILES
            wait(pe, s_exp, tile_no - 1)
            nc.tensor.matmul(keyed_bank[i % 2][:], KS[0:FULL, par, head, t * P:(t + 1) * P],
                             QS[0:FULL, par, head, :], start=True, stop=True).then_inc(s_keyed, 1)

        def pe_values_sum(t, j, k, par, group):
            return nc.tensor.matmul(value_bank[32 * j:32 * j + 32, :], values[:, par, t, 4 * group + j, :],
                                    probs[:, k, j, t, :], start=(t == 0), stop=(t == TILES - 1),
                                    tile_position=(0, 32 * j))

        def pe_unit_start(pe, b, group, par, scoring):
            v = 4 * b + group
            pe.wait_ge(s_m_row[group % 2], (2 * b + group // 2 + 1) * 16)
            if scoring:
                half_b = b if group < 2 else b + 1
                pe.wait_ge(s_stack[1 if group < 2 else 0], 192 * (half_b + 1))

        def pe_slot(pe, b, par, s, first=False, last=False):
            g, j = s // 4, s % 4
            u = 4 * b + g
            scoring = not (last and g >= 2)
            v_par, v_group = (par, g + 2) if g < 2 else (1 - par, g - 2)
            if j == 0:
                pe_unit_start(pe, b, g, par, scoring)
            w_par, w_group = (par, g - 1) if g else (1 - par, 3)
            for c in range(TILES):
                i = TILES * j + c
                if scoring:
                    pe_score(pe, 16 * (u + 2) + i, i, v_par, v_group)
                pe_keyed(pe, 16 * u + i, i, par, g)
                pe_jobs(pe, b, par, s, c, first, last)
                if first and g == 0:
                    continue
                for head in ((), (), (0, 1), (2, 3))[c] if j == 0 else (c,):
                    if j == 0 and head == 0:
                        wait(pe, s_outT, u - 1)
                    done = pe_values_sum(j, head, (g + 1) % 2, w_par, w_group)
            if j == 3 and not (first and g == 0):
                done.then_inc(s_pv, 1)

        def pe_max_job(pe, b, group, bank):
            pe.wait_ge(s_rowmax, 16 * (4 * b + group + 1))
            pe_max_t(bank, group % 2)

        def pe_out_job(pe, w, bank):
            pe.wait_ge(s_outT, w + 1)
            pe_out_t(bank)

        def pe_jobs(pe, b, par, s, c, first, last):
            at = (s, c)
            if at == (0, 2):
                pe_max_job(pe, b, 1, 0)
            if at == (1, 0) and not first:
                wait(pe, s_attn, 4 * b - 2)
                pe_out_job(pe, 4 * b - 2, 1)
            if at == (2, 2) and not last:
                pe.wait_ge(s_normed, TILES * (b + 2))
                pe.wait_ge(s_mrest, 4 * b + 2)
                pe_normed_t(0)
            if at == (2, 3) and not last:
                if first:
                    pe.wait_ge(s_v, 2)
                else:
                    pe.wait_ge(s_attn, 4 * b - 1)
                pe_normed_t(1)
            if at == (3, 1) and not last:
                pe.wait_ge(s_nT, 2 * (b + 1) + 1)
                pe_project(0, wq, 0, (0,))
            if at == (3, 2) and not last:
                pe.wait_ge(s_nT, 2 * (b + 1) + 2)
                pe_project(0, wq, 0, (1,))
            if at == (3, 3) and not last:
                pe_project(1, wk, 0, (0,))
            if at == (4, 0) and not last:
                pe_project(1, wk, 0, (1,))
            if at == (4, 2):
                if last:
                    pe.wait_ge(s_mrest, 4 * b + 2)
                else:
                    pe.wait_ge(s_rest, 4 * (b + 1) + 1)
                pe_max_job(pe, b, 2, 0)
            if at == (5, 0) and not first:
                if last:
                    pe.wait_ge(s_attn, 4 * b - 1)
                else:
                    pe.wait_ge(s_rest, 4 * (b + 1) + 2)
                pe_out_job(pe, 4 * b - 1, 1)
            if at == (6, 0) and not last:
                pe.wait_ge(s_mrest, 4 * b + 3)
                pe_project(0, wq, 1, (0,))
            if at == (6, 1) and not last:
                pe_project(0, wq, 1, (1,))
            if at == (6, 2) and not last:
                if first:
                    pe.wait_ge(s_rest, 6)
                else:
                    pe.wait_ge(s_attn, 4 * b)
                pe_project(1, wk, 1, (0,))
            if at == (6, 3) and not last:
                pe_project(1, wk, 1, (1,))
            if at == (7, 2) and not last:
                pe.wait_ge(s_rest, 4 * (b + 1) + 3)
                pe_values(0, 0, (0,))
            if at == (7, 3) and not last:
                pe_values(0, 0, (1,))
            if at == (8, 2):
                if last:
                    pe.wait_ge(s_attn, 4 * b)
                else:
                    pe.wait_ge(s_rest, 4 * (b + 1) + 4)
                pe_max_job(pe, b, 3, 1)
            if at == (9, 0):
                if last:
                    pe.wait_ge(s_mrest, 4 * b + 3)
                else:
                    pe.wait_ge(s_v, 2 * (b + 1) + 1)
                pe_out_job(pe, 4 * b, 0)
            if at == (10, 0) and not last:
                pe.wait_ge(s_mrest, 4 * b + 4)
                pe_values(1, 1, (0,))
            if at == (10, 1) and not last:
                pe_values(1, 1, (1,))
            if at == (12, 2) and not last:
                pe.wait_ge(s_attn, 4 * b + 1)
                pe_max_job(pe, b + 1, 0, 0)
            if at == (13, 0):
                if last:
                    pe.wait_ge(s_mrest, 4 * b + 4)
                else:
                    pe.wait_ge(s_v, 2 * (b + 1) + 2)
                pe_out_job(pe, 4 * b + 1, 1)
            if at == (14, 0) and not first:
                pe.wait_ge(s_feats, TILES * b)
                if last:
                    pe.wait_ge(s_attn, 4 * b + 1)
                else:
                    pe.wait_ge(s_mrest, 4 * b + 5)
                pe_feats_t(0)
            if at == (14, 1) and not first:
                pe.wait_ge(s_attn, 4 * b + 2)
                pe_feats_t(1)
            if at == (14, 3) and not first:
                pe.wait_ge(s_fT, 2 * b)
                pe_expert_scores()
            if at == (15, 2) and not first:
                pe.wait_ge(s_sc, b)
                pe_expert_scores_t()

        def pe_tok_t(pe, n, k):
            pe.wait_ge(s_tok, n + 1)
            for c in range(CHUNKS):
                last = nc.tensor.transpose(misc[k][:, c * P:(c + 1) * P], tok_n[:, k, c * P:(c + 1) * P], ident)
            last.then_inc(s_tokT_ps, 1)

        def pe_hidden(pe, n, k, ring, w1_loads):
            pe.wait_ge(s_w1[ring], 16 * w1_loads)
            pe.wait_ge(s_tokT, CHUNKS * (n + 1))
            for f in range(BLOCKS):
                dst = hidden_bank[k][f // 4][:, (f % 4) * P:(f % 4 + 1) * P]
                for c in range(CHUNKS):
                    last = nc.tensor.matmul(dst, w1[:, ring, c, f * P:(f + 1) * P], tokT[:, k, c, :],
                                            start=(c == 0), stop=(c == CHUNKS - 1))
                if f % 4 == 3:
                    last.then_inc(s_h_ps, 1)

        def pe_second(pe, n, k, expert):
            pe.wait_ge(s_h, BLOCKS * (n + 1))
            for f in range(BLOCKS):
                last = nc.tensor.matmul(y_bank[k][:, 0:DIM], hidden[:, k, f, :],
                                        w2[:, bass.ds(expert, 1), f, :].rearrange("p o d -> p (o d)"),
                                        start=(f == 0), stop=(f == BLOCKS - 1))
            last.then_inc(s_y_ps, 1)

        def pe_slot_step(pe, r, k):
            n, _, _ = slot_at(r, k, 0)
            expert = expert_reg(pe, n)
            known = isinstance(r, int)
            if not known or n + 1 < SLOTS:
                pe_hidden(pe, n + 1, (k + 1) % 2, (k + 1) % W1_RING,
                          r * (RING // W1_RING) + (k + 1) // W1_RING + 1)
            if not known or n + 2 < SLOTS:
                pe_tok_t(pe, n + 2, k % 2)
            else:
                pe.wait_ge(s_y, n - 1)
            pe_second(pe, n, k % 2, expert)

        @block.tensor
        def _(pe):
            pe.wait_ge(s_const, 16 * LOADS)
            pe.wait_ge(s_fill, FILLS)
            pe.wait_ge(s_normed, TILES)
            pe_normed_t(0)
            pe_normed_t(1)
            pe.wait_ge(s_nT, 2)
            pe_project(0, wq, 0)
            pe_project(1, wk, 0)
            pe.wait_ge(s_rest, 1)
            pe_project(0, wq, 1)
            pe.wait_ge(s_rest, 2)
            pe_project(1, wk, 1)
            pe.wait_ge(s_rest, 3)
            pe_values(0, 0)
            pe.wait_ge(s_rest, 4)
            pe_values(1, 1)
            for v in range(2):
                pe.wait_ge(s_stack[0], 192)
                for i in range(16):
                    pe_score(pe, 16 * v + i, i, 0, v)
                if v == 0:
                    pe.wait_ge(s_v, 1)
                    pe_max_job(pe, 0, 0, 0)
            pe.wait_ge(s_mrest, 1)
            for s in range(16):
                pe_slot(pe, 0, 0, s, first=True)
            pe.wait_ge(s_mrest, 5)
            with pe.Fori(0, 3) as r:
                for k in range(2):
                    for s in range(16):
                        pe_slot(pe, r * 2 + 1 + k, 1 - k, s)
            for s in range(16):
                pe_slot(pe, 7, 1, s, last=True)
            pe.wait_ge(s_attn, UNITS - 2)
            pe_out_job(pe, UNITS - 2, 1)
            pe.wait_ge(s_exp, 16 * UNITS)
            for t in range(TILES):
                for head in range(UNIT_HEADS):
                    done = pe_values_sum(t, head, 1, 1, 3)
            done.then_inc(s_pv, 1)
            pe.wait_ge(s_scores, BATCHES - 1)
            pe_out_job(pe, UNITS - 1, 0)
            pe.wait_ge(s_feats, TILES * BATCHES)
            pe_feats_t(0)
            pe_feats_t(1)
            pe.wait_ge(s_fT, 2 * BATCHES)
            pe_expert_scores()
            pe.wait_ge(s_sc, BATCHES)
            pe_expert_scores_t()
            pe.wait_ge(s_counted, 1)
            nc.tensor.matmul(score_bank[0][:, 0:EXPERTS], cst[:, C_BELOW:C_BELOW + P], running[:, :, TOKEN_TILES - 1],
                             start=True, stop=True)
            nc.tensor.matmul(score_bank[0][:, EXPERTS:2 * EXPERTS], ones, running[:, :, TOKEN_TILES - 1],
                             start=True, stop=True).then_inc(s_totals, 1)
            pe.wait_ge(s_hot, 1)
            for t in range(TOKEN_TILES):
                last = nc.tensor.matmul(score_bank[1][:, 0:3 * SLOTS], place_hot[:, t, :],
                                        slot_hot[:, t].rearrange("p m s -> p (m s)"),
                                        start=(t == 0), stop=(t == TOKEN_TILES - 1))
            last.then_inc(s_found, 1)
            pe.wait_ge(s_index, 1)
            pe.wait_ge(s_w2, 16 * EXPERTS)
            pe_tok_t(pe, 0, 0)
            pe_hidden(pe, 0, 0, 0, 1)
            pe_tok_t(pe, 1, 1)
            with pe.Fori(0, LOOPED // RING) as r:
                for k in range(RING):
                    pe_slot_step(pe, r, k)
            for k in range(PEELED):
                pe_slot_step(pe, LOOPED // RING, k)

        def act_normalise(which, t, dst, src, done):
            nc.scalar.activation(dst, src, ACT.Identity, bias=shift[:, which, t:t + 1],
                                 scale=rstd[:, which, t:t + 1]).then_inc(done, 1)

        def act_normed(act, b, t):
            if t == 0:
                act.wait_ge(s_scale[0], b + 1)
            act_normalise(0, t, x_in[:, t, :], x_in[:, t, :], s_normed)

        def act_attn_normed(act, b, par, t):
            if t == 0:
                act.wait_ge(s_scale[1], b + 1)
                wait(act, s_rows, 16 * b)
            act_normalise(1, t, rows[:, t, DIM:ROW], attn[:, par, t, :], s_attn_n)

        def act_feats(act, b, t):
            if t == 0:
                act.wait_ge(s_scale[2], b + 1)
            act_normalise(2, t, rows[:, t, 0:DIM], rows[:, t, DIM:ROW], s_feats)

        def act_normed_t(act, b, c):
            act.wait_ge(s_nT_ps, 2 * b + c + 1)
            nc.scalar.activation(normedT[:, c, :], misc[c][:], ACT.Copy).then_inc(s_nT, 1)

        def act_part(act, b, job, bank):
            wait(act, s_parts_out[job // 2], 32 * b)
            wait_alone(act, s_qk_ps, 4 * b + job + 1, s_passed)
            scale = cst[:, bass.ds(C_ROPE + b, 1)] if job % 2 == 0 else 1.0
            nc.scalar.activation(parts[:, job, 0, :], misc[bank][:], ACT.Copy if job % 2 else ACT.Identity,
                                 scale=scale).then_inc(s_part1, 1)

        def act_values(act, b, par, pair, bank):
            act.wait_ge(s_v_ps, 2 * b + pair + 1)
            if pair == 0:
                wait(act, s_pv, 4 * (b - 1) if not isinstance(b, int) else max(0, 4 * (b - 1)))
            src = misc[bank][:].rearrange("p (t h d) -> p t h d", t=2, d=HEAD)
            nc.scalar.activation(values[:, par, 2 * pair:2 * pair + 2, :, 0:HEAD], src,
                                 ACT.Copy).then_inc(s_v, 1)

        def act_out(act, w):
            act.wait_ge(s_pv, w + 1)
            nc.scalar.activation(outT[:], value_bank[:], ACT.Copy).then_inc(s_outT, 1)

        def act_feats_t(act, b, c):
            act.wait_ge(s_fT_ps, 2 * b + c + 1)
            nc.scalar.activation(featsT[:, c, :], misc[c][:], ACT.Copy).then_inc(s_fT, 1)

        def act_scores(act, b):
            act.wait_ge(s_sc_ps, b + 1)
            nc.scalar.activation(scoreT[0:EXPERTS, :], misc[0][0:EXPERTS, :], ACT.Copy).then_inc(s_sc, 1)

        def act_scores_t(act, b):
            wait_alone(act, s_scT_ps, b + 1, s_passed)
            nc.scalar.activation(scores[:, bass.ds(b * TILES, TILES), :],
                                 misc[0][:].rearrange("p (t k) -> p t k", t=TILES)[:, :, 0:EXPERTS],
                                 ACT.Copy).then_inc(s_scores, 1)

        def act_slot(act, b, par, s, first=False, last=False):
            g, j = s // 4, s % 4
            u = 4 * b + g
            if j == 0:
                wait(act, s_pv, u - 1)
            for c in range(TILES):
                i = TILES * j + c
                act.wait_ge(s_keyed, 16 * u + i + 1)
                nc.scalar.activation(probs[:, g % 2, j, c, :], keyed_bank[i % 2][:], ACT.Exp).then_inc(s_exp, 1)
                act_jobs(act, b, par, s, c, first, last)

        def act_jobs(act, b, par, s, c, first, last):
            at = (s, c)
            if s % 4 == 0 and c == 0 and not (first and s < 8):
                act_out(act, 4 * b + s // 4 - 2)
            if not last:
                if at in ((1, 1), (1, 2), (1, 3), (2, 0)):
                    act_normed(act, b + 1, 4 * (s - 1) + c - 1)
                if at in ((2, 3), (3, 0)):
                    act_normed_t(act, b + 1, s - 2)
                if at in ((3, 3), (4, 1), (6, 2), (7, 0)):
                    job = {3: 0, 4: 1, 6: 2, 7: 3}[s]
                    act_part(act, b + 1, job, job % 2)
                if at in ((8, 1), (10, 2)):
                    pair = int(s == 10)
                    act_values(act, b + 1, 1 - par, pair, pair)
            if not first:
                if at in ((7, 2), (7, 3), (8, 2), (8, 3)):
                    act_attn_normed(act, b - 1, 1 - par, 2 * (s - 7) + c - 2)
                if at in ((11, 2), (11, 3), (12, 2), (12, 3)):
                    act_feats(act, b - 1, 2 * (s - 11) + c - 2)
                if at in ((14, 1), (14, 2)):
                    act_feats_t(act, b - 1, c - 1)
                if at == (15, 1):
                    act_scores(act, b - 1)
                if at == (15, 3):
                    act_scores_t(act, b - 1)

        def act_tok_t(act, n, k, ring):
            act.wait_ge(s_tokT_ps, n + 1)
            for c in range(CHUNKS):
                nc.scalar.activation(tokT[:, k, c, :], misc[k][:, c * P:(c + 1) * P], ACT.Identity,
                                     bias=params_now[:, ring, CHUNKS + c:CHUNKS + c + 1],
                                     scale=params_now[:, ring, c:c + 1]).then_inc(s_tokT, 1)

        def act_minus(act, n, ring):
            act.wait_ge(s_dot, n + 1)
            nc.scalar.activation(minus[:, ring:ring + 1], dot[:, ring:ring + 1], ACT.Exp,
                                 scale=-1.0).then_inc(s_minus, 1)

        def act_hidden(act, n, k, ring):
            for f in range(BLOCKS):
                if f % 4 == 0:
                    act.wait_ge(s_h_ps, 2 * n + f // 4 + 1)
                col = 2 * CHUNKS + f
                nc.scalar.activation(hidden[:, k, f, :], hidden_bank[k][f // 4][:, (f % 4) * P:(f % 4 + 1) * P],
                                     ACT.Relu, bias=params_now[:, ring, col:col + 1]).then_inc(s_h, 1)

        def act_slot_step(act, r, k):
            known = isinstance(r, int)
            n, ring, _ = slot_at(r, k, 1)
            if not known or n < SLOTS:
                act_hidden(act, n, (k + 1) % 2, ring)
            n, ring, _ = slot_at(r, k, 2)
            if not known or n < SLOTS:
                act_tok_t(act, n, k % 2, ring)
            n, ring, _ = slot_at(r, k, 3)
            if not known or n < SLOTS:
                act_minus(act, n, ring)

        @block.scalar
        def _(act):
            act.wait_ge(s_const, 16 * LOADS)
            for t in range(TILES):
                act_normed(act, 0, t)
            for c in range(CHUNKS):
                act_normed_t(act, 0, c)
            for job in range(4):
                act_part(act, 0, job, job % 2)
            for pair in range(2):
                act_values(act, 0, 0, pair, pair)
            for s in range(16):
                act_slot(act, 0, 0, s, first=True)
            with act.Fori(0, 3) as r:
                for k in range(2):
                    for s in range(16):
                        act_slot(act, r * 2 + 1 + k, 1 - k, s)
            for s in range(16):
                act_slot(act, 7, 1, s, last=True)
            act_out(act, UNITS - 2)
            act.wait_ge(s_out_ps, UNITS - 1)
            act_out(act, UNITS - 1)
            for t in range(TILES):
                act_attn_normed(act, BATCHES - 1, 1, t)
            for t in range(TILES):
                act_feats(act, BATCHES - 1, t)
            for c in range(CHUNKS):
                act_feats_t(act, BATCHES - 1, c)
            act_scores(act, BATCHES - 1)
            act_scores_t(act, BATCHES - 1)
            for n in range(3):
                act_minus(act, n, n)
            for n in range(2):
                act_tok_t(act, n, n, n)
            act_hidden(act, 0, 0, 0)
            with act.Fori(0, LOOPED // RING) as r:
                for k in range(RING):
                    act_slot_step(act, r, k)
            for k in range(PEELED):
                act_slot_step(act, LOOPED // RING, k)

        def dve_stats(which, t, src, done):
            nc.vector.bn_stats(stats[:, which, t, :], src).then_inc(done, 1)

        def dve_moments(dve, which, b, stats_done, done):
            wait_alone(dve, stats_done, TILES * (b + 1), s_passed)
            for t in range(TILES):
                nc.vector.bn_aggr(moments[:, which, t, :], stats[:, which, t, :]).then_inc(done, 1)

        def dve_rest(dve, b, job, bank):
            dve.wait_ge(s_part1, 4 * b + job + 1)
            wait(dve, s_part3, 4 * b + job - 1)
            if job % 2 == 0:
                nc.vector.scalar_tensor_tensor(rest[:, job % 2, :], misc[bank][:], cst[:, bass.ds(C_ROPE + b, 1)],
                                               parts[:, job, 0, :], ALU.mult, ALU.subtract).then_inc(s_rest, 1)
            else:
                nc.vector.tensor_tensor(rest[:, job % 2, :], misc[bank][:], parts[:, job, 0, :],
                                        ALU.subtract).then_inc(s_rest, 1)

        def dve_max_part(dve, v, k, bank):
            dve.wait_ge(s_mT_ps, v + 1)
            wait(dve, s_m_out[k], (v - k) * 8)
            nc.vector.tensor_copy(max_parts[:, k, 0, :], misc[bank][0:UNIT_HEADS * TILES, 0:P]).then_inc(s_m1, 1)

        def dve_max_rest(dve, v, k, bank):
            dve.wait_ge(s_m1, v + 1)
            nc.vector.tensor_tensor(max_rest[:, k, :], misc[bank][0:UNIT_HEADS * TILES, 0:P],
                                    max_parts[:, k, 0, :], ALU.subtract).then_inc(s_mrest, 1)

        def dve_inv(dve, w, bank):
            dve.wait_ge(s_out_ps, w + 1)
            src = misc[bank][:].rearrange("p (t h d) -> p t h d", t=TILES, d=32)
            nc.vector.reciprocal(inv_sum[:], src[:, :, :, HEAD]).then_inc(s_inv, 1)

        def dve_attn(dve, w, bank, par, group):
            dve.wait_ge(s_inv, w + 1)
            src = misc[bank][:].rearrange("p (t h d) -> p t h d", t=TILES, d=32)[:, :, :, 0:HEAD]
            dst = attn[:, par, :, 64 * group:64 * group + 64].rearrange("p t (h d) -> p t h d", d=HEAD)
            inv = inv_sum[:].unsqueeze(3).broadcast_to([P, TILES, UNIT_HEADS, HEAD])
            nc.vector.tensor_tensor(dst, src, inv, ALU.mult).then_inc(s_attn, 1)

        def dve_rowmax(dve, tile_no, i, k):
            dve.wait_ge(s_score, tile_no + 1)
            nc.vector.reduce_max(row_max[:, k, i:i + 1], score_bank[i % 3][:], AX).then_inc(s_rowmax, 1)

        def dve_slot(dve, b, par, s, first=False, last=False):
            g, j = s // 4, s % 4
            u = 4 * b + g
            scoring = not (last and g >= 2)
            if j == 0 and scoring:
                dve.wait_ge(s_mT_ps, u + 1)
            for c in range(TILES):
                if scoring:
                    dve_rowmax(dve, 16 * (u + 2) + TILES * j + c, TILES * j + c, g % 2)
                dve_between(dve, b, par, s, c, first, last)

        def dve_between(dve, b, par, s, c, first, last):
            at = (s, c)
            if not last:
                if s == 0 and c < 2:
                    if c == 0:
                        dve.wait_ge(s_x, 16 * (b + 2))
                    for t in (2 * c, 2 * c + 1):
                        dve_stats(0, t, x_in[:, t, :], s_xst)
                if at == (0, 2):
                    dve_moments(dve, 0, b + 1, s_xst, s_xmom)
            if s in (1, 5, 9) or (s == 13 and not last):
                v, k, bank = {1: (4 * b + 1, 1, 0), 5: (4 * b + 2, 0, 0), 9: (4 * b + 3, 1, 1),
                              13: (4 * b + 4, 0, 0)}[s]
                if c == 0:
                    dve_max_part(dve, v, k, bank)
                if c == 1:
                    dve_max_rest(dve, v, k, bank)
            if s % 4 == 1 and not (first and s < 8):
                bank = int(s != 9)
                if c == 2:
                    dve_inv(dve, 4 * b + s // 4 - 2, bank)
                if c == 3:
                    w_par, w_group = (1 - par, 2 + s // 4) if s < 8 else (par, s // 4 - 2)
                    dve_attn(dve, 4 * b + s // 4 - 2, bank, w_par, w_group)
            if at in ((4, 0), (4, 2), (6, 3), (7, 1)) and not last:
                job = {(4, 0): 0, (4, 2): 1, (6, 3): 2, (7, 1): 3}[at]
                dve_rest(dve, b + 1, job, job % 2)
            if not first:
                if s == 6 and c < 2:
                    if c == 0:
                        dve.wait_ge(s_attn, 4 * b)
                    for t in (2 * c, 2 * c + 1):
                        dve_stats(1, t, attn[:, 1 - par, t, :], s_ast)
                if at == (6, 2):
                    dve_moments(dve, 1, b - 1, s_ast, s_amom)
                if s == 10:
                    dve.wait_ge(s_x1, TILES * (b - 1) + c + 1)
                    dve_stats(2, c, rows[:, c, DIM:ROW], s_x1st)
                if at == (10, 3):
                    dve_moments(dve, 2, b - 1, s_x1st, s_x1mom)

        def dve_route(dve):
            V = nc.vector
            steps = [0]

            def step(ins):
                ins.then_inc(s_route, 1)
                steps[0] += 1
                dve.wait_ge(s_route, steps[0])

            def over(ap, n):
                return ap.unsqueeze(2).broadcast_to([P, ap.shape[1], n])

            def under(ap, n):
                return ap.unsqueeze(1).broadcast_to([P, n, ap.shape[1]])

            dve.wait_ge(s_out_ps, UNITS)
            step(V.memset(ones, 1.0))
            step(V.memset(no_carry, 1.0))
            step(V.memset(no_carry[:, :, 0:1], 0.0))
            step(V.tensor_scalar(less_8[:], count[:, 0:EXPERTS], float(EXPERTS), None, ALU.subtract))
            step(V.tensor_copy(count_bf, count))
            dve.wait_ge(s_scores, BATCHES)
            step(V.tensor_reduce(best[:], scores[:], AX, ALU.max))
            step(V.tensor_tensor(hits, scores[:], over(best[:], EXPERTS), ALU.is_equal))
            step(V.tensor_tensor(hits, hits, under(less_8[:], TOKEN_TILES), ALU.mult))
            step(V.tensor_reduce(first_hit[:], hits, AX, ALU.min))
            step(V.tensor_tensor(one_hot, over(less_8[:], TOKEN_TILES), under(first_hit[:], EXPERTS), ALU.is_equal))
            flat = [a.rearrange("p e t -> p (e t)") for a in (running, no_carry, one_hot)]
            step(V.tensor_tensor_scan(flat[0], flat[1], flat[2], 0.0, ALU.mult, ALU.add))
            V.tensor_copy(masked, running).then_inc(s_counted, 1)
            dve.wait_ge(s_totals, 1)
            step(V.tensor_scalar(tiles_i[:], score_bank[0][:, EXPERTS:2 * EXPERTS], float(P - 1), None, ALU.add))
            step(V.tensor_scalar(tiles_i[:], tiles_i[:], 7, None, ALU.arith_shift_right))
            step(V.tensor_copy(tiles_f[:], tiles_i[:]))
            step(V.tensor_tensor_scan(tiles_end[:], ones[:, 0:EXPERTS], tiles_f[:], 0.0, ALU.mult, ALU.add))
            step(V.tensor_tensor(slot_ge, over(count[:, 0:SLOTS], EXPERTS), under(tiles_end[:], SLOTS), ALU.is_ge))
            step(V.tensor_reduce(expert_f[:], slot_ge, AX, ALU.add))
            V.tensor_scalar(expert_of[:], expert_f[:], float(EXPERTS - 1), None, ALU.min).then_inc(s_experts, 1)
            step(V.tensor_tensor(offset[:], tiles_end[:], tiles_f[:], ALU.subtract))
            step(V.scalar_tensor_tensor(offset[:], offset[:], float(P), score_bank[0][:, 0:EXPERTS],
                                        ALU.mult, ALU.add))
            step(V.tensor_tensor(masked, running, over(offset[:], TOKEN_TILES), ALU.add))
            step(V.scalar_tensor_tensor(masked, masked, -1.0, one_hot, ALU.add, ALU.mult))
            step(V.tensor_reduce(place[:], masked.rearrange("p e t -> p t e"), AX, ALU.add))
            step(V.tensor_copy(place_i[:], place[:]))
            step(V.tensor_scalar(place_i[:], place_i[:], 7, None, ALU.arith_shift_right))
            step(V.tensor_copy(slot_f[:], place_i[:]))
            step(V.scalar_tensor_tensor(within[:], slot_f[:], -float(P), place[:], ALU.mult, ALU.add))
            for t in range(TOKEN_TILES):
                V.tensor_scalar(place_hot[:, t, :], count_bf, within[:, t:t + 1], None, ALU.is_equal)
            step(V.tensor_tensor(slot_eq, under(count[:, 0:SLOTS], TOKEN_TILES), over(slot_f[:], SLOTS),
                                 ALU.is_equal))
            V.tensor_scalar(slot_hot[:, :, 0, :], slot_eq, cst[:, C_PART:C_PART + 1], None, ALU.mult)
            V.tensor_tensor(slot_hot[:, :, 1, :], slot_eq, over(count[:, 0:TOKEN_TILES], SLOTS), ALU.mult)
            V.tensor_copy(slot_hot[:, :, 2, :], slot_eq).then_inc(s_hot, 1)
            dve.wait_ge(s_found, 1)
            step(V.tensor_copy(found[:], score_bank[1][:, 0:3 * SLOTS].rearrange("p (m s) -> p m s", m=3)))
            step(V.scalar_tensor_tensor(token_f[:], found[:, 1, :], float(P), found[:, 0, :], ALU.mult, ALU.add))
            step(V.tensor_copy(index_all[:, :, 0], token_f[:]))
            step(V.tensor_scalar(found[:, 2, :], found[:, 2, :], -float(SKIP), float(SKIP), ALU.mult, ALU.add))
            V.tensor_tensor(index_all[:, :, 1], token_f[:], found[:, 2, :], ALU.add).then_inc(s_index, 1)
            dve.wait_ge(s_index, 1)
            dve.wait_ge(s_par, 16 * 5)

        def dve_prepare(dve, n, ring):
            e = expert_reg(dve, n)
            nc.vector.tensor_copy(index_now[:, ring, :].unsqueeze(1), index_all[:, bass.ds(n, 1), :]).then_inc(s_prep, 1)
            nc.vector.tensor_copy(params_now[:, ring, :].unsqueeze(1), params[:, bass.ds(e, 1), :]).then_inc(s_prep, 1)

        def dve_features(dve, n, ring, round_1, k):
            e = expert_reg(dve, n)
            dve.wait_ge(s_gather[ring], 16 * round_1)
            nc.vector.bn_stats(slot_stats[:, 0, k, :], got[:, ring, 0:DIM]).then_inc(s_gst, 1)
            nc.vector.scalar_tensor_tensor(product, got[:, ring, 0:DIM], 1.0,
                                           cent_all[:, bass.ds(e, 1), :].rearrange("p o d -> p (o d)"),
                                           ALU.mult, ALU.mult, accum_out=dot[:, ring:ring + 1]).then_inc(s_dot, 1)
            wait_alone(dve, s_gst, n + 1, s_passed)
            nc.vector.bn_aggr(slot_mom[:, 0, k, :], slot_stats[:, 0, k, :]).then_inc(s_gmom, 1)

        def dve_alpha(dve, n, ring):
            dve.wait_ge(s_minus, n + 1)
            nc.vector.tensor_scalar(minus[:, ring:ring + 1], minus[:, ring:ring + 1], 1.0, None,
                                    ALU.add).then_inc(s_plus1, 1)
            dve.wait_ge(s_plus1, n + 1)
            nc.vector.reciprocal(alpha[:, ring:ring + 1], minus[:, ring:ring + 1]).then_inc(s_alpha, 1)

        def dve_finish(dve, n, ring, k):
            e = expert_reg(dve, n)
            dve.wait_ge(s_y_ps, n + 1)
            nc.vector.tensor_tensor(mixed[:, k, :], y_bank[k][:, 0:DIM],
                                    b2_all[:, bass.ds(e, 1), :].rearrange("p o d -> p (o d)"),
                                    ALU.add).then_inc(s_y, 1)
            dve.wait_ge(s_y, n + 1)
            dve.wait_ge(s_alpha, n + 1)
            nc.vector.scalar_tensor_tensor(mixed[:, k, :], mixed[:, k, :], alpha[:, ring:ring + 1],
                                           got[:, ring, 0:DIM], ALU.mult, ALU.add).then_inc(s_mix, 1)
            dve.wait_ge(s_mix, n + 1)
            nc.vector.bn_stats(slot_stats[:, 1, k, :], mixed[:, k, :]).then_inc(s_mst, 1)
            wait_alone(dve, s_mst, n + 1, s_passed)
            nc.vector.bn_aggr(slot_mom[:, 1, k, :], slot_stats[:, 1, k, :]).then_inc(s_mmom, 1)

        def dve_tok(dve, n, ring, k):
            wait(dve, s_tokT_ps, n - 1)
            dve.wait_ge(s_grstd, n + 1)
            nc.vector.tensor_scalar(tok_n[:, k, :], got[:, ring, 0:DIM], slot_mom[:, 0, k, 0:1],
                                    slot_rstd[:, 0, k:k + 1], ALU.subtract, ALU.mult).then_inc(s_tok, 1)

        def dve_new(dve, n, ring, k):
            dve.wait_ge(s_mrstd, n + 1)
            nc.vector.tensor_scalar(new_rows[:, ring, :], mixed[:, k, :], slot_mom[:, 1, k, 0:1],
                                    slot_rstd[:, 1, k:k + 1], ALU.subtract, ALU.mult).then_inc(s_mixn, 1)
            dve.wait_ge(s_mixn, n + 1)
            nc.vector.tensor_tensor(new_rows[:, ring, :], new_rows[:, ring, :], got[:, ring, DIM:ROW],
                                    ALU.add).then_inc(s_new, 1)

        def dve_slot_step(dve, r, k):
            known = isinstance(r, int)
            j, ring0, _ = slot_at(r, k, 0)
            n, ring, rnd = slot_at(r, k, AHEAD)
            if not known or n < SLOTS:
                wait(dve, s_scatter[ring], 16 * rnd)
                dve_prepare(dve, n, ring)
            n, ring, rnd = slot_at(r, k, 3)
            if not known or n < SLOTS:
                dve_features(dve, n, ring, rnd + 1, (k + 1) % 2)
            if not known or j > 0:
                dve_new(dve, r * RING + (k - 1), (k - 1) % RING, (k - 1) % 2)
            m, ring2, _ = slot_at(r, k, 2)
            if not known or m < SLOTS:
                dve_alpha(dve, m, ring2)
            if not known or n < SLOTS:
                dve_tok(dve, n, ring, (k + 1) % 2)
            dve_finish(dve, j, ring0, k % 2)

        @block.vector
        def _(dve):
            dve.wait_ge(s_x, 16)
            for t in range(TILES):
                dve_stats(0, t, x_in[:, t, :], s_xst)
            dve_moments(dve, 0, 0, s_xst, s_xmom)
            dve.wait_ge(s_const, 16 * LOADS)
            for job in range(4):
                dve_rest(dve, 0, job, job % 2)
            for v in range(2):
                for i in range(16):
                    dve_rowmax(dve, 16 * v + i, i, v)
                if v == 0:
                    dve_max_part(dve, 0, 0, 0)
                    dve_max_rest(dve, 0, 0, 0)
            for s in range(16):
                dve_slot(dve, 0, 0, s, first=True)
            with dve.Fori(0, 3) as r:
                for k in range(2):
                    for s in range(16):
                        dve_slot(dve, r * 2 + 1 + k, 1 - k, s)
            for s in range(16):
                dve_slot(dve, 7, 1, s, last=True)
            for w, bank in ((UNITS - 2, 1), (UNITS - 1, 0)):
                dve.wait_ge(s_attn, w)
                dve_inv(dve, w, bank)
                dve_attn(dve, w, bank, 1, w % 4)
            dve.wait_ge(s_attn, UNITS)
            for t in range(TILES):
                dve_stats(1, t, attn[:, 1, t, :], s_ast)
            dve_moments(dve, 1, BATCHES - 1, s_ast, s_amom)
            dve.wait_ge(s_x1, TILES * BATCHES)
            for t in range(TILES):
                dve_stats(2, t, rows[:, t, DIM:ROW], s_x1st)
            dve_moments(dve, 2, BATCHES - 1, s_x1st, s_x1mom)
            dve_route(dve)
            for n in range(4):
                dve_prepare(dve, n, n)
            for n in range(3):
                dve_features(dve, n, n, 1, n % 2)
                dve_tok(dve, n, n, n % 2)
            for n in range(2):
                dve_alpha(dve, n, n)
            for k in range(RING):
                dve_slot_step(dve, 0, k)
            with dve.Fori(1, LOOPED // RING) as r:
                for k in range(RING):
                    dve_slot_step(dve, r, k)
            for k in range(PEELED):
                dve_slot_step(dve, LOOPED // RING, k)
            dve_new(dve, SLOTS - 1, (SLOTS - 1) % RING, (SLOTS - 1) % 2)

        def pool_scale(pool, which, b, moments_done, steps):
            wait_alone(pool, moments_done, TILES * (b + 1), s_passed)
            nc.gpsimd.tensor_scalar(rstd[:, which, :], moments[:, which, :, 1], EPS, None,
                                    ALU.add).then_inc(s_pool, 1)
            nc.gpsimd.tensor_scalar(shift[:, which, :], moments[:, which, :, 0], -1.0, None,
                                    ALU.mult).then_inc(s_pool, 1)
            pool.wait_ge(s_pool, steps + 2)
            nc.gpsimd.tensor_tensor(rstd[:, which, :], rstd[:, which, :], half_neg[:], ALU.pow).then_inc(s_pool, 1)
            pool.wait_ge(s_pool, steps + 3)
            nc.gpsimd.tensor_tensor(shift[:, which, :], shift[:, which, :], rstd[:, which, :],
                                    ALU.mult).then_inc(s_scale[which], 1)

        def pool_parts(pool, b, job):
            wait_alone(pool, s_rest, 4 * b + job + 1, s_passed)
            nc.gpsimd.tensor_copy(parts[:, job, 1, :], rest[:, job % 2, :]).then_inc(s_part2, 1)
            pool.wait_ge(s_part2, 4 * b + job + 1)
            nc.gpsimd.tensor_tensor(parts[:, job, 2, :], rest[:, job % 2, :], parts[:, job, 1, :],
                                    ALU.subtract).then_inc(s_part3, 1)

        def pool_max_parts(pool, v, k):
            wait_alone(pool, s_mrest, v + 1, s_passed)
            nc.gpsimd.tensor_copy(max_parts[:, k, 1, :], max_rest[:, k, :]).then_inc(s_m2, 1)
            pool.wait_ge(s_m2, v + 1)
            nc.gpsimd.tensor_tensor(max_parts[:, k, 2, :], max_rest[:, k, :], max_parts[:, k, 1, :],
                                    ALU.subtract).then_inc(s_m3, 1)

        def pool_residual(pool, b):
            pool.wait_ge(s_res, 16 * (b + 1))
            for t in range(TILES):
                pool.wait_ge(s_attn_n, TILES * b + t + 1)
                nc.gpsimd.tensor_tensor(rows[:, t, DIM:ROW], rows[:, t, DIM:ROW], x_res[:, t, :],
                                        ALU.add).then_inc(s_x1, 1)

        def pool_batch(pool, b, par, first=False, last=False):
            steps = 3 + 3 * b + (6 * (b - 1) if not first else 0)
            if not last:
                pool_scale(pool, 0, b + 1, s_xmom, steps)
                steps = steps + 3
            pool_max_parts(pool, 4 * b + 1, 1)
            if not last:
                pool_parts(pool, b + 1, 0)
                pool_parts(pool, b + 1, 1)
            pool_max_parts(pool, 4 * b + 2, 0)
            if not first:
                pool_scale(pool, 1, b - 1, s_amom, steps)
            if not last:
                pool_parts(pool, b + 1, 2)
                pool_parts(pool, b + 1, 3)
            if not first:
                pool_residual(pool, b - 1)
            pool_max_parts(pool, 4 * b + 3, 1)
            if not first:
                pool_scale(pool, 2, b - 1, s_x1mom, steps + 3)
            if not last:
                pool_max_parts(pool, 4 * b + 4, 0)

        out_rows = out.rearrange("b s d -> (b s) d")

        def pool_gather(pool, n, ring):
            wait_alone(pool, s_prep, 2 * n + 2, s_passed)
            nc.gpsimd.indirect_dma_start(
                out=got[:, ring, :], out_offset=None, in_=rows_dram,
                in_offset=bass.IndirectOffsetOnAxis(ap=index_now[:, ring, 0:1].bitcast(U32), axis=0),
                bounds_check=TOKENS - 1, oob_is_err=False).then_inc(s_gather[ring], 16)

        def pool_slot_rstd(pool, which, k, step, done):
            nc.gpsimd.tensor_scalar(slot_rstd[:, which, k:k + 1], slot_mom[:, which, k, 1:2], EPS, None,
                                    ALU.add).then_inc(s_chain, 1)
            pool.wait_ge(s_chain, step)
            nc.gpsimd.tensor_tensor(slot_rstd[:, which, k:k + 1], slot_rstd[:, which, k:k + 1], half_neg[:, 0:1],
                                    ALU.pow).then_inc(done, 1)

        def pool_scatter(pool, n, ring):
            wait_alone(pool, s_new, n + 1, s_passed)
            nc.gpsimd.indirect_dma_start(
                out=out_rows, out_offset=bass.IndirectOffsetOnAxis(ap=index_now[:, ring, 1:2].bitcast(U32), axis=0),
                in_=new_rows[:, ring, :], in_offset=None,
                bounds_check=TOKENS - 1, oob_is_err=False).then_inc(s_scatter[ring], 16)

        def pool_slot_step(pool, r, k):
            known = isinstance(r, int)
            j, _, _ = slot_at(r, k, 0)
            n, ring, _ = slot_at(r, k, AHEAD)
            if not known or n < SLOTS:
                pool_gather(pool, n, ring)
            m, _, _ = slot_at(r, k, 3)
            step = j * 2 + 4
            if not known or m < SLOTS:
                wait_alone(pool, s_gmom, m + 1, s_passed)
                pool_slot_rstd(pool, 0, (k + 1) % 2, step, s_grstd)
                step = step + 1
            elif j > SLOTS - 3:
                step = step - (j - (SLOTS - 3))
            if not known or j > 0:
                pool_scatter(pool, r * RING + (k - 1), (k - 1) % RING)
            wait_alone(pool, s_mmom, j + 1, s_passed)
            pool_slot_rstd(pool, 1, k % 2, step, s_mrstd)

        @block.gpsimd
        def _(pool):
            nc.gpsimd.memset(half_neg[:], -0.5).then_inc(s_fill, 1)
            nc.gpsimd.memset(values[:, :, :, :, HEAD:HEAD + 1], 1.0).then_inc(s_fill, 1)
            nc.gpsimd.memset(values[:, :, :, :, HEAD + 1:32], 0.0).then_inc(s_fill, 1)
            nc.gpsimd.memset(scoreT[:], 0.0).then_inc(s_fill, 1)
            pool.wait_ge(s_fill, FILLS)
            pool_scale(pool, 0, 0, s_xmom, 0)
            for job in range(4):
                pool_parts(pool, 0, job)
            pool_max_parts(pool, 0, 0)
            pool_batch(pool, 0, 0, first=True)
            with pool.Fori(0, 3) as r:
                pool_batch(pool, r * 2 + 1, 1)
                pool_batch(pool, r * 2 + 2, 0)
            pool_batch(pool, 7, 1, last=True)
            steps = 3 + 3 * 7 + 6 * 7
            pool_scale(pool, 1, 7, s_amom, steps)
            pool_residual(pool, 7)
            pool_scale(pool, 2, 7, s_x1mom, steps + 3)
            pool.wait_ge(s_rows, 16 * BATCHES)
            pool.wait_ge(s_index, 1)
            for n in range(4):
                pool_gather(pool, n, n)
            for n in range(3):
                wait_alone(pool, s_gmom, n + 1, s_passed)
                pool_slot_rstd(pool, 0, n % 2, n + 1, s_grstd)
            for k in range(RING):
                pool_slot_step(pool, 0, k)
            with pool.Fori(1, LOOPED // RING) as r:
                for k in range(RING):
                    pool_slot_step(pool, r, k)
            for k in range(PEELED):
                pool_slot_step(pool, LOOPED // RING, k)
            pool_scatter(pool, SLOTS - 1, (SLOTS - 1) % RING)


def table():
    t = np.zeros((P, C_END), np.float32)
    t[:, C_IDENT:C_IDENT + P] = np.eye(P)
    t[:, C_BELOW:C_BELOW + P] = np.triu(np.ones((P, P)), 1)
    half = HEAD // 2
    theta = 1.0 / 10000.0 ** (np.arange(0, HEAD, 2, dtype=np.float32) / np.float32(HEAD))
    for b in range(BATCHES):
        angle = (np.float32(b) * theta.astype(np.float32)).astype(np.float64)
        factor = np.concatenate([np.cos(angle) + np.sin(angle), np.cos(angle) - np.sin(angle)])
        t[:, C_ROPE + b] = np.tile(factor * factor / np.sqrt(HEAD), P // HEAD)
    t[:, C_COUNT:C_COUNT + P] = np.arange(P)
    t[:, C_PART] = np.arange(P)
    return t


def kernel(L0_attn_x, L0_attn_Wq, L0_attn_Wk, L0_attn_Wv, L0_ffn_centroids, L0_ffn_gamma, L0_ffn_beta,
           L0_ffn_W1, L0_ffn_b1, L0_ffn_W2, L0_ffn_b2):
    import concourse.bacc as bacc
    import ml_dtypes
    from concourse.bass_utils import run_bass_kernel_spmd

    def laid(a, *order):
        return np.ascontiguousarray(np.transpose(np.asarray(a), order))

    E, C = EXPERTS, CHUNKS
    arrays = {
        "x": np.ascontiguousarray(L0_attn_x),
        "wqt": laid(L0_attn_Wq, 1, 0), "wkt": laid(L0_attn_Wk, 1, 0), "wvt": laid(L0_attn_Wv, 1, 0),
        "cent": np.ascontiguousarray(L0_ffn_centroids),
        "cent_t": laid(L0_ffn_centroids, 1, 0),
        "gamma_t": laid(np.asarray(L0_ffn_gamma).reshape(E, C, P), 2, 0, 1),
        "beta_t": laid(np.asarray(L0_ffn_beta).reshape(E, C, P), 2, 0, 1),
        "w1t": laid(np.asarray(L0_ffn_W1).reshape(E, HIDDEN, C, P), 0, 3, 2, 1),
        "b1_t": laid(np.asarray(L0_ffn_b1).reshape(E, BLOCKS, P), 2, 0, 1),
        "w2t": laid(np.asarray(L0_ffn_W2).reshape(E, DIM, BLOCKS, P), 3, 0, 2, 1),
        "b2": np.ascontiguousarray(L0_ffn_b2),
        "consts": table(),
        "minus_ones": np.full((FULL - STACK, 2, HEADS, SEQ), -1, ml_dtypes.bfloat16),
    }
    nc = bacc.Bacc("TRN2", target_bir_lowering=False, num_devices=1)
    args = [nc.dram_tensor(name, a.shape, mybir.dt.from_np(a.dtype), kind="ExternalInput").ap() for name, a in arrays.items()]
    out = nc.dram_tensor("out", (BATCHES, SEQ, DIM), F32, kind="ExternalOutput").ap()
    build(nc, *args, out)
    result = run_bass_kernel_spmd(nc, [arrays], core_ids=[0])
    return result.results[0]["out"]
```

```python
from contextlib import ExitStack

import numpy as np

import concourse.bass as bass
from concourse import mybir
from concourse.alu_op_type import AluOpType as ALU

ACT = mybir.ActivationFunctionType
F32 = mybir.dt.float32
BF16 = mybir.dt.bfloat16
I32 = mybir.dt.int32
U32 = mybir.dt.uint32
AX = mybir.AxisListType.X

P = 128
EPS = 1e-5
BATCHES, SEQ, DIM = 8, 512, 256
HEADS, HEAD = 16, 16
CHUNKS = DIM // P
TILES = SEQ // P
GROUPS = 4
UNIT_HEADS = HEADS // GROUPS
UNITS = BATCHES * GROUPS
TOKENS = BATCHES * SEQ
TOKEN_TILES = TOKENS // P
EXPERTS, HIDDEN = 8, 1024
BLOCKS = HIDDEN // P
SLOTS = (TOKENS - EXPERTS) // P + EXPERTS
ROW = 2 * DIM
SKIP = 2 * TOKENS
ACT_SHARE, DVE_SHARE = (0, 1), (2, 3)

Q_PARTS = (0, 0, 1, 1, 0, 2)
K_PARTS = (0, 1, 0, 1, 2, 0)
STACK = len(Q_PARTS) * HEAD
MAX_PARTS = 3
FULL = STACK + MAX_PARTS

C_IDENT, C_BELOW, C_ROPE, C_COUNT, C_PART, C_END = 0, P, 2 * P, 2 * P + BATCHES, 3 * P + BATCHES, 3 * P + BATCHES + 1

RING = 6
VALUES_AT = 2
PART2_AT = ((4, 1), (4, 2))
REST_AT = ((3, 2), (4, 0), (6, 3), (7, 1))
AHEAD = 4
LOOPED = (SLOTS - AHEAD) // RING * RING
PEELED = SLOTS - LOOPED
FILLS = 4
LOADS = 6


def wait(eng, sem, value):
    if not isinstance(value, int) or value > 0:
        eng.wait_ge(sem, value)


def wait_alone(eng, sem, value, passed):
    eng.wait_ge(sem, value).then_inc(passed, 1)


def build(nc, x, wqt, wkt, wvt, cent, cent_t, gamma_t, beta_t, w1t, b1_t, w2t, b2, consts, minus_ones, out):
    ctx = ExitStack()
    with ctx:
        def sb(name, shape, dt=F32):
            return ctx.enter_context(nc.sbuf_tensor(name, shape, dt))

        def sem(name):
            return ctx.enter_context(nc.semaphore(name))

        def dram(name, shape, dt=F32):
            return nc.dram_tensor(name, shape, dt, kind="Internal").ap()

        parts_dram = dram("parts_dram", (2, 4, MAX_PARTS, P, SEQ), BF16)
        max_dram = dram("max_dram", (2, MAX_PARTS, HEADS, P), BF16)
        rows_dram = dram("rows_dram", (TOKENS, ROW))

        cst = sb("cst", [P, C_END])
        ident = cst[:, C_IDENT:C_IDENT + P]
        wqkv = sb("wqkv", [P, 3, CHUNKS, DIM])
        wq, wk, wv = (wqkv[:, i] for i in range(3))
        centT = sb("centT", [P, CHUNKS, 32])
        half_neg = sb("half_neg", [P, TILES])
        x_in = sb("x_in", [P, TILES, DIM])
        x_res = sb("x_res", [P, TILES, DIM])
        normedT = sb("normedT", [P, CHUNKS, SEQ])
        parts = sb("parts", [P, 4, MAX_PARTS, SEQ], BF16)
        rest = sb("rest", [P, 2, SEQ])
        QUARTER = HEADS * SEQ
        store = sb("store", [P, 4, QUARTER])
        stacks = store[:, 0:2, :].bitcast(BF16).rearrange("p a (k h n) -> p a k h n", k=2, h=HEADS)
        QS, KS = stacks[:, :, 0], stacks[:, :, 1]
        probs = store[:, 2:4, :].rearrange("p u (h t q) -> p u h t q", h=UNIT_HEADS, t=TILES)
        values = sb("values", [P, 2, TILES, HEADS, 32])
        row_max = sb("row_max", [P, 2, UNIT_HEADS * TILES])
        max_parts = sb("max_parts", [UNIT_HEADS * TILES, 2, MAX_PARTS, P], BF16)
        max_rest = sb("max_rest", [UNIT_HEADS * TILES, 2, P])
        outT = sb("outT", [P, SEQ])
        attn = sb("attn", [P, 2, TILES, DIM])
        inv_sum = sb("inv_sum", [P, TILES, UNIT_HEADS])
        rows = sb("rows", [P, TILES, ROW])
        featsT = normedT
        scoreT = sb("scoreT", [P, SEQ])
        scores = sb("scores", [P, TOKEN_TILES, EXPERTS])
        stats = sb("stats", [P, 3, TILES, 6])
        moments = sb("moments", [P, 3, TILES, 2])
        rstd = sb("rstd", [P, 3, TILES])
        shift = sb("shift", [P, 3, TILES])

        score_bank = [ctx.enter_context(nc.psum_tensor(f"score_bank{i}", [P, SEQ], F32)) for i in range(3)]
        keyed_bank = [ctx.enter_context(nc.psum_tensor(f"keyed_bank{i}", [P, SEQ], F32)) for i in range(2)]
        value_bank = ctx.enter_context(nc.psum_tensor("value_bank", [P, SEQ], F32))
        misc = [ctx.enter_context(nc.psum_tensor(f"misc{i}", [P, SEQ], F32)) for i in range(2)]

        s_const = sem("s_const")
        s_fill = sem("s_fill")
        s_passed = sem("s_passed")
        s_x = sem("s_x")
        s_res = sem("s_res")
        s_xst = sem("s_xst")
        s_xmom = sem("s_xmom")
        s_pool = sem("s_pool")
        s_scale = [sem(f"s_scale{i}") for i in range(3)]
        s_normed = sem("s_normed")
        s_nT_ps = sem("s_nT_ps")
        s_nT = sem("s_nT")
        s_qk_ps = sem("s_qk_ps")
        s_part1 = sem("s_part1")
        s_rest = sem("s_rest")
        s_part2 = sem("s_part2")
        s_part3 = sem("s_part3")
        s_parts_out = [sem("s_parts_out0"), sem("s_parts_out1")]
        s_stack = [sem("s_stack0"), sem("s_stack1")]
        s_v_ps = sem("s_v_ps")
        s_v = sem("s_v")
        s_score = sem("s_score")
        s_rowmax = sem("s_rowmax")
        s_mT_ps = sem("s_mT_ps")
        s_m1 = sem("s_m1")
        s_mrest = sem("s_mrest")
        s_m2 = sem("s_m2")
        s_mrest2 = sem("s_mrest2")
        s_m3 = sem("s_m3")
        s_m_out = [sem("s_m_out0"), sem("s_m_out1")]
        s_m_row = [sem("s_m_row0"), sem("s_m_row1")]
        s_keyed = sem("s_keyed")
        s_exp = sem("s_exp")
        s_pv = sem("s_pv")
        s_outT = sem("s_outT")
        s_out_ps = sem("s_out_ps")
        s_inv = sem("s_inv")
        s_attn = sem("s_attn")
        s_ast = sem("s_ast")
        s_amom = sem("s_amom")
        s_attn_n = sem("s_attn_n")
        s_x1 = sem("s_x1")
        s_share = sem("s_share")
        s_x1st = sem("s_x1st")
        s_x1mom = sem("s_x1mom")
        s_feats = sem("s_feats")
        s_rows = sem("s_rows")
        s_fT_ps = sem("s_fT_ps")
        s_fT = sem("s_fT")
        s_sc_ps = sem("s_sc_ps")
        s_sc = sem("s_sc")
        s_scT_ps = sem("s_scT_ps")
        s_scores = sem("s_scores")

        count = cst[:, C_COUNT:C_COUNT + P]
        small = rest[:].rearrange("p a n -> p (a n)")
        one_hot, running, masked, no_carry = (small[:, i * 256:(i + 1) * 256].rearrange(
            "p (e t) -> p e t", e=EXPERTS) for i in range(4))
        hits = x_res[:, 0, :].rearrange("p (t e) -> p t e", e=EXPERTS)
        count_bf = x_res[:, 1, 0:P // 2].bitcast(BF16)
        slot_ge = x_in[:].rearrange("p t d -> p (t d)")[:, 0:SLOTS * EXPERTS].rearrange("p (s e) -> p s e", e=EXPERTS)
        ones = outT[:, 0:P]
        flat_attn = attn[:].rearrange("p a t d -> p (a t d)")
        place_hot = attn[:].rearrange("p a t d -> p (a t d)").bitcast(BF16).rearrange("p (t r) -> p t r", r=P)
        w2 = store[:, 0:2, :].rearrange("p a (e f d) -> p (a e) f d", f=BLOCKS, d=DIM)
        w1 = store[:, 2:4, :].rearrange("p a (e c f) -> p (a e) c f", c=CHUNKS, f=HIDDEN)
        hidden = rows[:].rearrange("p t r -> p (t r)").rearrange("p (k f t) -> p k f t", k=2, f=BLOCKS)
        cent_all, b2_all = (values[:, a].rearrange("p t h d -> p (t h d)").rearrange("p (e d) -> p e d", e=EXPERTS)
                            for a in range(2))
        flat_parts = parts[:].rearrange("p j k n -> p (j k n)")
        got = flat_parts.bitcast(F32).rearrange("p (k r) -> p k r", k=RING)
        n_eq = TOKEN_TILES * SLOTS
        slot_eq = flat_parts[:, 0:n_eq].rearrange("p (t s) -> p t s", s=SLOTS)
        slot_hot = flat_parts[:, n_eq:4 * n_eq].rearrange("p (t m s) -> p t m s", m=3, s=SLOTS)
        tokT = flat_attn[:, 0:512].rearrange("p (k c t) -> p k c t", k=2, c=CHUNKS)
        new_rows = flat_attn[:, 512:512 + RING * DIM].rearrange("p (k d) -> p k d", k=RING)
        tok_n, mixed = x_in[:, 0:2, :], x_in[:, 2:4, :]
        product = outT[:, 0:DIM]
        b2_now = (scoreT[:, 0:DIM], scoreT[:, DIM:2 * DIM], outT[:, DIM:2 * DIM])
        w1_now = ((normedT[:].rearrange("p c n -> p (c n)"), rest[:].rearrange("p c n -> p (c n)")),
                  (x_res[:].rearrange("p t d -> p (t d)"),
                   wqkv[:].rearrange("p i c d -> p (i c d)")[:, 0:HIDDEN]))
        best = sb("best", [P, TOKEN_TILES])
        first_hit = sb("first_hit", [P, TOKEN_TILES])
        less_8 = sb("less_8", [P, EXPERTS])
        tiles_i = sb("tiles_i", [P, EXPERTS], I32)
        tiles_f = sb("tiles_f", [P, EXPERTS])
        tiles_end = sb("tiles_end", [P, EXPERTS])
        offset = sb("offset", [P, EXPERTS])
        place = sb("place", [P, TOKEN_TILES])
        place_i = sb("place_i", [P, TOKEN_TILES], I32)
        slot_f = sb("slot_f", [P, TOKEN_TILES])
        within = sb("within", [P, TOKEN_TILES])
        expert_f = sb("expert_f", [P, SLOTS])
        expert_of = sb("expert_of", [P, SLOTS], I32)
        found = sb("found", [P, 3, SLOTS])
        token_f = sb("token_f", [P, SLOTS])
        index_all = sb("index_all", [P, SLOTS, 2], I32)
        index_now = sb("index_now", [P, RING, 2], I32)
        NPAR = 2 * CHUNKS + BLOCKS
        params = sb("params", [P, EXPERTS, NPAR])
        params_now = sb("params_now", [P, RING, NPAR])
        slot_stats = sb("slot_stats", [P, 2, 2, 6])
        slot_mom = sb("slot_mom", [P, 2, 2, 2])
        slot_rstd = sb("slot_rstd", [P, 2, 2])
        dot = sb("dot", [P, RING])
        minus = sb("minus", [P, RING])
        alpha = sb("alpha", [P, RING])

        hidden_bank = ((score_bank[0], score_bank[1]), (score_bank[2], keyed_bank[0]))
        y_bank = (keyed_bank[1], value_bank)

        s_route = sem("s_route")
        s_counted = sem("s_counted")
        s_totals = sem("s_totals")
        s_experts = sem("s_experts")
        s_slot_eq = sem("s_slot_eq")
        s_hot = sem("s_hot")
        s_hot_act = sem("s_hot_act")
        s_place = sem("s_place")
        s_found = sem("s_found")
        s_index = sem("s_index")
        s_par = sem("s_par")
        s_weights = sem("s_weights")
        s_b2_now = sem("s_b2_now")
        s_w1_now = sem("s_w1_now")
        s_prep = sem("s_prep")
        s_gather = [sem(f"s_gather{i}") for i in range(RING)]
        s_scatter = [sem(f"s_scatter{i}") for i in range(RING)]
        s_gst = sem("s_gst")
        s_gmom = sem("s_gmom")
        s_dot = sem("s_dot")
        s_minus = sem("s_minus")
        s_plus1 = sem("s_plus1")
        s_alpha = sem("s_alpha")
        s_chain = sem("s_chain")
        s_grstd = sem("s_grstd")
        s_mrstd = sem("s_mrstd")
        s_tok = sem("s_tok")
        s_tokT_ps = sem("s_tokT_ps")
        s_tokT = sem("s_tokT")
        s_h_ps = sem("s_h_ps")
        s_h = sem("s_h")
        s_y_ps = sem("s_y_ps")
        s_y = sem("s_y")
        s_mix = sem("s_mix")
        s_mst = sem("s_mst")
        s_mmom = sem("s_mmom")
        s_mixn = sem("s_mixn")
        s_new = sem("s_new")

        block = ctx.enter_context(nc.Block())
        x_tiled = x.rearrange("b (t p) d -> b p t d", p=P)
        rows_tiled = rows_dram.rearrange("(b t p) r -> b p t r", p=P, t=TILES)

        def slot_at(r, k, ahead):
            return r * RING + (k + ahead), (k + ahead) % RING, r + (k + ahead) // RING

        def expert_reg(eng, n):
            return eng.value_load(expert_of[0:1, bass.ds(n, 1)], min_val=0, max_val=EXPERTS - 1)

        def sp_load_x(sp, b):
            wait(sp, s_nT_ps, CHUNKS * b)
            sp.dma_start(x_in[:], x_tiled[b]).then_inc(s_x, 16)

        def sp_load_residual(sp, b):
            sp.dma_start(x_res[:], x_tiled[b]).then_inc(s_res, 16)

        def sp_parts_out(sp, b, par, half):
            for kind in (0, 1):
                job = 2 * half + kind
                sp.wait_ge(s_part3, 4 * b + job + 1)
                sp.dma_start(parts_dram[par, job].rearrange("k p n -> p k n"),
                             parts[:, job]).then_inc(s_parts_out[half], 16)

        def sp_stack(sp, b, par, half, kinds=(0, 1)):
            wait(sp, s_keyed, 64 * (b - 1) if not isinstance(b, int) else max(0, 64 * (b - 1)))
            sp.wait_ge(s_parts_out[half], 32 * (b + 1))
            for kind in kinds:
                stack, order = ((QS, Q_PARTS), (KS, K_PARTS))[kind]
                for blk, part in enumerate(order):
                    src = parts_dram[par, 2 * half + kind, part].rearrange("(h d) n -> d h n", d=HEAD)
                    sp.dma_start(stack[blk * HEAD:(blk + 1) * HEAD, par, half * 8:half * 8 + 8, :],
                                 src).then_inc(s_stack[half], 16)

        def sp_max_out(sp, b, group):
            k = group % 2
            sp.wait_ge(s_m3, 4 * b + group + 1)
            sp.dma_start(max_dram[k].rearrange("m r n -> r m n"), max_parts[:, k]).then_inc(s_m_out[k], 16)

        def sp_max_rows(sp, b, group, par):
            k = group % 2
            sp.wait_ge(s_m_out[k], (2 * b + group // 2 + 1) * 16)
            rows_of = QS[STACK:FULL, par, 4 * group:4 * group + 4, :].rearrange("m h (t q) -> m (h t) q", t=TILES)
            sp.dma_start(rows_of, max_dram[k]).then_inc(s_m_row[k], 16)

        def sp_store_rows(sp, b):
            sp.wait_ge(s_feats, TILES * (b + 1))
            sp.dma_start(rows_tiled[b], rows[:]).then_inc(s_rows, 16)

        def sp_weights(sp, tile, src, e):
            sp.dma_start(tile[:, e], src[e]).then_inc(s_weights, 16)

        def sp_batch(sp, b, par, first=False, last=False):
            sp_max_out(sp, b, 1)
            sp_max_rows(sp, b, 1, par)
            if last:
                sp.wait_ge(s_keyed, 64 * b)
                for e in range(2):
                    sp_weights(sp, w2, w2t, e)
            if not last:
                sp_parts_out(sp, b + 1, 1 - par, 0)
            sp_max_out(sp, b, 2)
            if not last:
                sp_stack(sp, b + 1, 1 - par, 0)
            sp_max_rows(sp, b, 2, par)
            if last:
                for e in range(2, 4):
                    sp_weights(sp, w2, w2t, e)
            if not last:
                sp_parts_out(sp, b + 1, 1 - par, 1)
            sp_max_out(sp, b, 3)
            sp_max_rows(sp, b, 3, par)
            if not last:
                sp_stack(sp, b + 1, 1 - par, 1)
            if not isinstance(b, int) or b + 2 < BATCHES:
                sp_load_x(sp, b + 2)
            if last:
                sp.wait_ge(s_pv, 4 * b)
                sp.dma_start(cent_all, cent.partition_broadcast(P)).then_inc(s_par, 16)
                sp.wait_ge(s_keyed, 64 * b + 32)
                for e in (4, 6):
                    sp_weights(sp, w2, w2t, e)
            if not last:
                sp_max_out(sp, b + 1, 0)
                sp_max_rows(sp, b + 1, 0, 1 - par)
            if not first:
                sp_store_rows(sp, b - 1)
                sp.wait_ge(s_rows, 16 * b)
            sp_load_residual(sp, b)

        @block.sync
        def _(sp):
            sp.dma_start(x_in[:], x_tiled[0]).then_inc(s_x, 16)
            sp.dma_start(cst[:], consts).then_inc(s_const, 16)
            for tile, src in ((wq, wqt), (wk, wkt), (wv, wvt)):
                sp.dma_start(tile, src.rearrange("(c p) n -> p c n", p=P)).then_inc(s_const, 16)
            sp.wait_ge(s_fill, FILLS)
            sp.dma_start(centT[:, :, 0:EXPERTS], cent_t.rearrange("(c p) e -> p c e", p=P)).then_inc(s_const, 16)
            sp.dma_start(KS[STACK:FULL, :, :, :], minus_ones).then_inc(s_const, 16)
            for half in range(2):
                sp_parts_out(sp, 0, 0, half)
                sp_stack(sp, 0, 0, half, (0,))
            sp_load_x(sp, 1)
            sp_max_out(sp, 0, 0)
            sp_max_rows(sp, 0, 0, 0)
            sp_batch(sp, 0, 0, first=True)
            sp_batch(sp, 1, 1)
            with sp.Fori(0, 2) as r:
                sp_batch(sp, r * 2 + 2, 0)
                sp_batch(sp, r * 2 + 3, 1)
            sp_batch(sp, 6, 0)
            sp_batch(sp, 7, 1, last=True)
            for tile, src in ((params[:, :, 0:CHUNKS], gamma_t), (params[:, :, CHUNKS:2 * CHUNKS], beta_t),
                              (params[:, :, 2 * CHUNKS:NPAR], b1_t)):
                sp.dma_start(tile, src).then_inc(s_par, 16)
            sp.wait_ge(s_keyed, 16 * UNITS)
            for e in (5, 7):
                sp_weights(sp, w2, w2t, e)
            sp.wait_ge(s_pv, UNITS - 1)
            for e in range(4):
                sp_weights(sp, w1, w1t, e)
            sp.wait_ge(s_pv, UNITS)
            for e in range(4, 8):
                sp_weights(sp, w1, w1t, e)
            sp.dma_start(b2_all, b2.partition_broadcast(P)).then_inc(s_par, 16)
            sp_store_rows(sp, 7)
            for k in range(RING):
                sp.wait_ge(s_scatter[k], 16 * ((SLOTS - k + RING - 1) // RING))

        def score_place(i):
            if i == 4 * UNIT_HEADS - 1:
                return 1, 2
            return i % 3, (4, 2, 4)[i] if i < 3 else 3

        def pe_normed_t(c):
            for t in range(TILES):
                last = nc.tensor.transpose(misc[c][:, t * P:(t + 1) * P], x_in[:, t, c * P:(c + 1) * P], ident)
            last.then_inc(s_nT_ps, 1)

        def pe_project(bank, weight, half, chunks=range(CHUNKS)):
            for c in chunks:
                last = nc.tensor.matmul(misc[bank][:], weight[:, c, half * P:(half + 1) * P], normedT[:, c, :],
                                        start=(c == 0), stop=(c == CHUNKS - 1))
            if c == CHUNKS - 1:
                last.then_inc(s_qk_ps, 1)

        def pe_values(bank, pair, which=range(2)):
            for i in which:
                t = 2 * pair + i
                for c in range(CHUNKS):
                    last = nc.tensor.matmul(misc[bank][:, i * DIM:(i + 1) * DIM], normedT[:, c, t * P:(t + 1) * P],
                                            wv[:, c, :], start=(c == 0), stop=(c == CHUNKS - 1))
            if i == 1:
                last.then_inc(s_v_ps, 1)

        def pe_max_t(bank, k):
            nc.tensor.transpose(misc[bank][0:UNIT_HEADS * TILES, 0:P], row_max[:, k, :], ident).then_inc(s_mT_ps, 1)

        def pe_out_t(bank):
            for t in range(TILES):
                last = nc.tensor.transpose(misc[bank][:, t * P:(t + 1) * P], outT[:, t * P:(t + 1) * P], ident)
            last.then_inc(s_out_ps, 1)

        def pe_feats_t(c):
            for t in range(TILES):
                last = nc.tensor.transpose(misc[c][:, t * P:(t + 1) * P], rows[:, t, c * P:(c + 1) * P], ident)
            last.then_inc(s_fT_ps, 1)

        def pe_expert_scores():
            for c in range(CHUNKS):
                for t in range(TILES):
                    last = nc.tensor.matmul(misc[0][32 * t:32 * t + 32, 0:P], centT[:, c, :],
                                            featsT[:, c, t * P:(t + 1) * P], start=(c == 0), stop=(c == CHUNKS - 1),
                                            tile_position=(0, 32 * t))
            last.then_inc(s_sc_ps, 1)

        def pe_expert_scores_t():
            nc.tensor.transpose(misc[0][:, 0:P], scoreT[:, 0:P], ident).then_inc(s_scT_ps, 1)

        def pe_score(pe, tile_no, i, par, group):
            head, t = 4 * group + i // TILES, i % TILES
            bank, back = score_place(i)
            wait(pe, s_rowmax, tile_no - back + 1)
            nc.tensor.matmul(score_bank[bank][:], QS[0:STACK, par, head, t * P:(t + 1) * P],
                             KS[0:STACK, par, head, :], start=True, stop=True).then_inc(s_score, 1)

        def pe_keyed(pe, tile_no, i, par, group):
            head, t = 4 * group + i // TILES, i % TILES
            wait(pe, s_exp, tile_no - 1)
            nc.tensor.matmul(keyed_bank[i % 2][:], KS[0:FULL, par, head, t * P:(t + 1) * P],
                             QS[0:FULL, par, head, :], start=True, stop=True).then_inc(s_keyed, 1)

        def pe_values_sum(t, k, par, group):
            for j in range(UNIT_HEADS):
                last = nc.tensor.matmul(value_bank[32 * j:32 * j + 32, :], values[:, par, t, 4 * group + j, :],
                                        probs[:, k, j, t, :], start=(t == 0), stop=(t == TILES - 1),
                                        tile_position=(0, 32 * j))
            return last

        def pe_unit_start(pe, b, group, par, scoring):
            v = 4 * b + group
            pe.wait_ge(s_m_row[group % 2], (2 * b + group // 2 + 1) * 16)
            if scoring:
                half_b = b if group < 2 else b + 1
                pe.wait_ge(s_stack[1 if group < 2 else 0], 192 * (half_b + 1))

        def pe_slot(pe, b, par, s, first=False, last=False):
            g, j = s // 4, s % 4
            u = 4 * b + g
            scoring = not (last and g >= 2)
            v_par, v_group = (par, g + 2) if g < 2 else (1 - par, g - 2)
            if j == 0:
                pe_unit_start(pe, b, g, par, scoring)
            w_par, w_group = (par, g - 1) if g else (1 - par, 3)
            for c in range(TILES):
                i = TILES * j + c
                if scoring:
                    pe_score(pe, 16 * (u + 2) + i, i, v_par, v_group)
                pe_keyed(pe, 16 * u + i, i, par, g)
                pe_jobs(pe, b, par, s, c, first, last)
                if c == VALUES_AT and not (first and g == 0):
                    if j == 0:
                        wait(pe, s_outT, u - 1)
                    done = pe_values_sum(j, (g + 1) % 2, w_par, w_group)
                    if j == TILES - 1:
                        done.then_inc(s_pv, 1)

        def pe_max_job(pe, b, group, bank):
            pe.wait_ge(s_rowmax, 16 * (4 * b + group + 1))
            pe_max_t(bank, group % 2)

        def pe_out_job(pe, w, bank):
            pe.wait_ge(s_outT, w + 1)
            pe_out_t(bank)

        def pe_jobs(pe, b, par, s, c, first, last):
            at = (s, c)
            if at == (0, 2):
                pe_max_job(pe, b, 1, 0)
            if at == (1, 0) and not first:
                wait(pe, s_attn, 4 * b - 2)
                pe_out_job(pe, 4 * b - 2, 1)
            if at == (1, 3) and not last:
                pe.wait_ge(s_normed, TILES * (b + 2))
                pe.wait_ge(s_mrest, 4 * b + 2)
                pe_normed_t(0)
            if at == (2, 1) and not last:
                if first:
                    pe.wait_ge(s_v, 2)
                else:
                    pe.wait_ge(s_attn, 4 * b - 1)
                pe_normed_t(1)
            if at == (2, 3) and not last:
                pe.wait_ge(s_nT, 2 * (b + 1) + 1)
                pe_project(0, wq, 0, (0,))
            if at == (3, 0) and not last:
                pe.wait_ge(s_nT, 2 * (b + 1) + 2)
                pe_project(0, wq, 0, (1,))
            if at == (3, 1) and not last:
                pe_project(1, wk, 0, (0,))
            if at == (3, 2) and not last:
                pe_project(1, wk, 0, (1,))
            if at == (4, 2):
                if last:
                    pe.wait_ge(s_mrest, 4 * b + 2)
                else:
                    pe.wait_ge(s_rest, 4 * (b + 1) + 1)
                pe_max_job(pe, b, 2, 0)
            if at == (5, 0) and not first:
                if last:
                    pe.wait_ge(s_attn, 4 * b - 1)
                else:
                    pe.wait_ge(s_rest, 4 * (b + 1) + 2)
                pe_out_job(pe, 4 * b - 1, 1)
            if at == (6, 0) and not last:
                pe.wait_ge(s_mrest, 4 * b + 3)
                pe_project(0, wq, 1, (0,))
            if at == (6, 1) and not last:
                pe_project(0, wq, 1, (1,))
            if at == (6, 2) and not last:
                if first:
                    pe.wait_ge(s_rest, 6)
                else:
                    pe.wait_ge(s_attn, 4 * b)
                pe_project(1, wk, 1, (0,))
            if at == (6, 3) and not last:
                pe_project(1, wk, 1, (1,))
            if at == (7, 2) and not last:
                pe.wait_ge(s_rest, 4 * (b + 1) + 3)
                pe_values(0, 0, (0,))
            if at == (7, 3) and not last:
                pe_values(0, 0, (1,))
            if at == (8, 2):
                if last:
                    pe.wait_ge(s_attn, 4 * b)
                else:
                    pe.wait_ge(s_rest, 4 * (b + 1) + 4)
                pe_max_job(pe, b, 3, 1)
            if at == (9, 0):
                if last:
                    pe.wait_ge(s_mrest, 4 * b + 3)
                else:
                    pe.wait_ge(s_v, 2 * (b + 1) + 1)
                pe_out_job(pe, 4 * b, 0)
            if at == (10, 0) and not last:
                pe.wait_ge(s_mrest, 4 * b + 4)
                pe_values(1, 1, (0,))
            if at == (10, 1) and not last:
                pe_values(1, 1, (1,))
            if at == (12, 2) and not last:
                pe.wait_ge(s_attn, 4 * b + 1)
                pe_max_job(pe, b + 1, 0, 0)
            if at == (13, 0):
                if last:
                    pe.wait_ge(s_mrest, 4 * b + 4)
                else:
                    pe.wait_ge(s_v, 2 * (b + 1) + 2)
                pe_out_job(pe, 4 * b + 1, 1)
            if at == (13, 3) and not first:
                pe.wait_ge(s_feats, TILES * b)
                if last:
                    pe.wait_ge(s_attn, 4 * b + 1)
                else:
                    pe.wait_ge(s_mrest, 4 * b + 5)
                pe_feats_t(0)
            if at == (14, 1) and not first:
                pe.wait_ge(s_attn, 4 * b + 2)
                pe_feats_t(1)
            if at == (15, 0) and not first:
                pe.wait_ge(s_fT, 2 * b)
                pe_expert_scores()
            if at == (15, 3) and not first:
                pe.wait_ge(s_sc, b)
                pe_expert_scores_t()

        def pe_tok_t(pe, n, k):
            pe.wait_ge(s_tok, n + 1)
            for c in range(CHUNKS):
                last = nc.tensor.transpose(misc[k][:, c * P:(c + 1) * P], tok_n[:, k, c * P:(c + 1) * P], ident)
            last.then_inc(s_tokT_ps, 1)

        def pe_hidden(pe, n, k):
            pe.wait_ge(s_w1_now, CHUNKS * (n + 1))
            pe.wait_ge(s_tokT, CHUNKS * (n + 1))
            for f in range(BLOCKS):
                dst = hidden_bank[k][f // 4][:, (f % 4) * P:(f % 4 + 1) * P]
                for c in range(CHUNKS):
                    last = nc.tensor.matmul(dst, w1_now[k][c][:, f * P:(f + 1) * P], tokT[:, k, c, :],
                                            start=(c == 0), stop=(c == CHUNKS - 1))
                if f % 4 == 3:
                    last.then_inc(s_h_ps, 1)

        def pe_second(pe, n, k, expert):
            pe.wait_ge(s_h, BLOCKS * (n + 1))
            for f in range(BLOCKS):
                last = nc.tensor.matmul(y_bank[k][:, 0:DIM], hidden[:, k, f, :],
                                        w2[:, bass.ds(expert, 1), f, :].rearrange("p o d -> p (o d)"),
                                        start=(f == 0), stop=(f == BLOCKS - 1))
            last.then_inc(s_y_ps, 1)

        def pe_slot_step(pe, r, k):
            n, _, _ = slot_at(r, k, 0)
            expert = expert_reg(pe, n)
            known = isinstance(r, int)
            if not known or n + 1 < SLOTS:
                pe_hidden(pe, n + 1, (k + 1) % 2)
            if not known or n + 2 < SLOTS:
                pe_tok_t(pe, n + 2, k % 2)
            else:
                pe.wait_ge(s_y, n - 1)
            pe_second(pe, n, k % 2, expert)

        @block.tensor
        def _(pe):
            pe.wait_ge(s_const, 16 * LOADS)
            pe.wait_ge(s_fill, FILLS)
            pe.wait_ge(s_normed, TILES)
            pe_normed_t(0)
            pe_normed_t(1)
            pe.wait_ge(s_nT, 2)
            pe_project(0, wq, 0)
            pe_project(1, wk, 0)
            pe.wait_ge(s_rest, 1)
            pe_project(0, wq, 1)
            pe.wait_ge(s_rest, 2)
            pe_project(1, wk, 1)
            pe.wait_ge(s_rest, 3)
            pe_values(0, 0)
            pe.wait_ge(s_rest, 4)
            pe_values(1, 1)
            for v in range(2):
                pe.wait_ge(s_stack[0], 192)
                for i in range(16):
                    pe_score(pe, 16 * v + i, i, 0, v)
                if v == 0:
                    pe.wait_ge(s_v, 1)
                    pe_max_job(pe, 0, 0, 0)
            pe.wait_ge(s_mrest, 1)
            for s in range(16):
                pe_slot(pe, 0, 0, s, first=True)
            pe.wait_ge(s_mrest, 5)
            with pe.Fori(0, 3) as r:
                for k in range(2):
                    for s in range(16):
                        pe_slot(pe, r * 2 + 1 + k, 1 - k, s)
            for s in range(16):
                pe_slot(pe, 7, 1, s, last=True)
            pe.wait_ge(s_attn, UNITS - 2)
            pe_out_job(pe, UNITS - 2, 1)
            pe.wait_ge(s_exp, 16 * UNITS)
            for t in range(TILES):
                done = pe_values_sum(t, 1, 1, 3)
            done.then_inc(s_pv, 1)
            pe.wait_ge(s_scores, BATCHES - 1)
            pe_out_job(pe, UNITS - 1, 0)
            pe.wait_ge(s_feats, TILES * BATCHES)
            pe_feats_t(0)
            pe_feats_t(1)
            pe.wait_ge(s_fT, 2 * BATCHES)
            pe_expert_scores()
            pe.wait_ge(s_sc, BATCHES)
            pe_expert_scores_t()
            pe.wait_ge(s_counted, 1)
            nc.tensor.matmul(score_bank[0][:, 0:EXPERTS], cst[:, C_BELOW:C_BELOW + P], running[:, :, TOKEN_TILES - 1],
                             start=True, stop=True)
            nc.tensor.matmul(score_bank[0][:, EXPERTS:2 * EXPERTS], ones, running[:, :, TOKEN_TILES - 1],
                             start=True, stop=True).then_inc(s_totals, 1)
            pe.wait_ge(s_hot, 1)
            pe.wait_ge(s_hot_act, 2)
            for t in range(TOKEN_TILES):
                pe.wait_ge(s_place, t + 1)
                last = nc.tensor.matmul(score_bank[1][:, 0:3 * SLOTS], place_hot[:, t, :],
                                        slot_hot[:, t].rearrange("p m s -> p (m s)"),
                                        start=(t == 0), stop=(t == TOKEN_TILES - 1))
            last.then_inc(s_found, 1)
            pe.wait_ge(s_index, 1)
            pe.wait_ge(s_weights, 16 * 2 * EXPERTS)
            pe_tok_t(pe, 0, 0)
            pe_tok_t(pe, 1, 1)
            pe_hidden(pe, 0, 0)
            with pe.Fori(0, LOOPED // RING) as r:
                for k in range(RING):
                    pe_slot_step(pe, r, k)
            for k in range(PEELED):
                pe_slot_step(pe, LOOPED // RING, k)

        def act_normalise(which, t, dst, src, done):
            nc.scalar.activation(dst, src, ACT.Identity, bias=shift[:, which, t:t + 1],
                                 scale=rstd[:, which, t:t + 1]).then_inc(done, 1)

        def act_normed(act, b, t):
            if t == 0:
                act.wait_ge(s_scale[0], b + 1)
            act_normalise(0, t, x_in[:, t, :], x_in[:, t, :], s_normed)

        def act_attn_normed(act, b, par, t):
            if t == 0:
                act.wait_ge(s_scale[1], b + 1)
                act.wait_ge(s_res, 16 * (b + 1))
            act_normalise(1, t, rows[:, t, DIM:ROW], attn[:, par, t, :], s_attn_n)

        def act_feats(act, b, t):
            if t == 0:
                act.wait_ge(s_scale[2], b + 1)
            act_normalise(2, t, rows[:, t, 0:DIM], rows[:, t, DIM:ROW], s_feats)

        def act_normed_t(act, b, c):
            act.wait_ge(s_nT_ps, 2 * b + c + 1)
            nc.scalar.activation(normedT[:, c, :], misc[c][:], ACT.Copy).then_inc(s_nT, 1)

        def act_part(act, b, job, bank):
            wait(act, s_parts_out[job // 2], 32 * b)
            wait_alone(act, s_qk_ps, 4 * b + job + 1, s_passed)
            scale = cst[:, bass.ds(C_ROPE + b, 1)] if job % 2 == 0 else 1.0
            nc.scalar.activation(parts[:, job, 0, :], misc[bank][:], ACT.Copy if job % 2 else ACT.Identity,
                                 scale=scale).then_inc(s_part1, 1)

        def act_part2(act, b, job):
            act.wait_ge(s_rest, 4 * b + job + 1)
            nc.scalar.activation(parts[:, job, 1, :], rest[:, job % 2, :], ACT.Copy).then_inc(s_part2, 1)

        def act_values(act, b, par, pair, bank):
            act.wait_ge(s_v_ps, 2 * b + pair + 1)
            if pair == 0:
                wait(act, s_pv, 4 * (b - 1) if not isinstance(b, int) else max(0, 4 * (b - 1)))
            src = misc[bank][:].rearrange("p (t h d) -> p t h d", t=2, d=HEAD)
            nc.scalar.activation(values[:, par, 2 * pair:2 * pair + 2, :, 0:HEAD], src,
                                 ACT.Copy).then_inc(s_v, 1)

        def act_out(act, w):
            act.wait_ge(s_pv, w + 1)
            nc.scalar.activation(outT[:], value_bank[:], ACT.Copy).then_inc(s_outT, 1)

        def act_feats_t(act, b, c):
            act.wait_ge(s_fT_ps, 2 * b + c + 1)
            nc.scalar.activation(featsT[:, c, :], misc[c][:], ACT.Copy).then_inc(s_fT, 1)

        def act_scores(act, b):
            act.wait_ge(s_sc_ps, b + 1)
            nc.scalar.activation(scoreT[:, 0:P], misc[0][:, 0:P], ACT.Copy).then_inc(s_sc, 1)

        def act_scores_t(act, b):
            wait_alone(act, s_scT_ps, b + 1, s_passed)
            nc.scalar.activation(scores[:, bass.ds(b * TILES, TILES), :],
                                 misc[0][:, 0:P].rearrange("p (t k) -> p t k", t=TILES)[:, :, 0:EXPERTS],
                                 ACT.Copy).then_inc(s_scores, 1)

        def act_slot(act, b, par, s, first=False, last=False):
            g, j = s // 4, s % 4
            u = 4 * b + g
            if j == 0:
                wait(act, s_pv, u - 1)
            for c in range(TILES):
                i = TILES * j + c
                act.wait_ge(s_keyed, 16 * u + i + 1)
                nc.scalar.activation(probs[:, g % 2, j, c, :], keyed_bank[i % 2][:], ACT.Exp).then_inc(s_exp, 1)
                act_jobs(act, b, par, s, c, first, last)

        def act_jobs(act, b, par, s, c, first, last):
            at = (s, c)
            if s % 4 == 0 and c == 0 and not (first and s < 8):
                act_out(act, 4 * b + s // 4 - 2)
            if not last:
                if at in ((0, 2), (1, 1)):
                    act_normed(act, b + 1, s)
                if at in ((2, 0), (2, 2)):
                    act_normed_t(act, b + 1, c // 2)
                if at in ((3, 1), (3, 3), (6, 2), (7, 0)):
                    job = {(3, 1): 0, (3, 3): 1, (6, 2): 2, (7, 0): 3}[at]
                    act_part(act, b + 1, job, job % 2)
                if at in PART2_AT:
                    act_part2(act, b + 1, PART2_AT.index(at))
                if at in ((8, 1), (10, 2)):
                    pair = int(s == 10)
                    act_values(act, b + 1, 1 - par, pair, pair)
            if not first:
                if at in ((7, 2), (7, 3), (8, 2), (8, 3)):
                    act_attn_normed(act, b - 1, 1 - par, 2 * (s - 7) + c - 2)
                if at in ((14, 0), (14, 2)):
                    act_feats_t(act, b - 1, c // 2)
                if at == (15, 1):
                    act_scores(act, b - 1)
                if at == (15, 3):
                    act_scores_t(act, b - 1)

        def act_tok_t(act, n, k, ring):
            act.wait_ge(s_tokT_ps, n + 1)
            for c in range(CHUNKS):
                nc.scalar.activation(tokT[:, k, c, :], misc[k][:, c * P:(c + 1) * P], ACT.Identity,
                                     bias=params_now[:, ring, CHUNKS + c:CHUNKS + c + 1],
                                     scale=params_now[:, ring, c:c + 1]).then_inc(s_tokT, 1)

        def act_minus(act, n, ring):
            act.wait_ge(s_dot, n + 1)
            nc.scalar.activation(minus[:, ring:ring + 1], dot[:, ring:ring + 1], ACT.Exp,
                                 scale=-1.0).then_inc(s_minus, 1)

        def act_hidden(act, n, k, ring):
            for f in range(BLOCKS):
                if f % 4 == 0:
                    act.wait_ge(s_h_ps, 2 * n + f // 4 + 1)
                col = 2 * CHUNKS + f
                nc.scalar.activation(hidden[:, k, f, :], hidden_bank[k][f // 4][:, (f % 4) * P:(f % 4 + 1) * P],
                                     ACT.Relu, bias=params_now[:, ring, col:col + 1]).then_inc(s_h, 1)

        def act_slot_step(act, r, k):
            known = isinstance(r, int)
            n, ring, _ = slot_at(r, k, 1)
            if not known or n < SLOTS:
                act_hidden(act, n, (k + 1) % 2, ring)
            n, ring, _ = slot_at(r, k, 2)
            if not known or n < SLOTS:
                act_tok_t(act, n, k % 2, ring)
            n, ring, _ = slot_at(r, k, 3)
            if not known or n < SLOTS:
                act_minus(act, n, ring)

        @block.scalar
        def _(act):
            act.wait_ge(s_fill, 1)
            nc.scalar.activation(minus[:, 0:1], half_neg[:, 0:1], ACT.Exp)
            for t in range(TILES):
                act_normed(act, 0, t)
            act.wait_ge(s_const, 16 * LOADS)
            for c in range(CHUNKS):
                act_normed_t(act, 0, c)
            act_part(act, 0, 0, 0)
            for job in range(1, 4):
                act_part(act, 0, job, job % 2)
                act_part2(act, 0, job - 1)
            act_part2(act, 0, 3)
            for pair in range(2):
                act_values(act, 0, 0, pair, pair)
            for half in range(2):
                sp_stack(act, 0, 0, half, (1,))
            for s in range(16):
                act_slot(act, 0, 0, s, first=True)
            with act.Fori(0, 3) as r:
                for k in range(2):
                    for s in range(16):
                        act_slot(act, r * 2 + 1 + k, 1 - k, s)
            for s in range(16):
                act_slot(act, 7, 1, s, last=True)
            act_out(act, UNITS - 2)
            act.wait_ge(s_out_ps, UNITS - 1)
            act_out(act, UNITS - 1)
            for t in ACT_SHARE:
                act_attn_normed(act, BATCHES - 1, 1, t)
            for t in ACT_SHARE:
                act_feats(act, BATCHES - 1, t)
            for c in range(CHUNKS):
                act_feats_t(act, BATCHES - 1, c)
            act_scores(act, BATCHES - 1)
            act_scores_t(act, BATCHES - 1)
            act.wait_ge(s_slot_eq, 1)
            nc.scalar.activation(slot_hot[:, :, 0, :], slot_eq, ACT.Identity,
                                 scale=cst[:, C_PART:C_PART + 1]).then_inc(s_hot_act, 1)
            nc.scalar.activation(slot_hot[:, :, 2, :], slot_eq, ACT.Copy).then_inc(s_hot_act, 1)
            for n in range(2):
                act_minus(act, n, n)
                act_tok_t(act, n, n, n)
            act_minus(act, 2, 2)
            act_hidden(act, 0, 0, 0)
            with act.Fori(0, LOOPED // RING) as r:
                for k in range(RING):
                    act_slot_step(act, r, k)
            for k in range(PEELED):
                act_slot_step(act, LOOPED // RING, k)

        def dve_stats(which, t, src, done):
            nc.vector.bn_stats(stats[:, which, t, :], src).then_inc(done, 1)

        def dve_normalise(which, t, dst, src, done):
            nc.vector.tensor_scalar(dst, src, moments[:, which, t, 0:1], rstd[:, which, t:t + 1],
                                    ALU.subtract, ALU.mult).then_inc(done, 1)

        def dve_moments(dve, which, b, stats_done, done):
            wait_alone(dve, stats_done, TILES * (b + 1), s_passed)
            for t in range(TILES):
                nc.vector.bn_aggr(moments[:, which, t, :], stats[:, which, t, :]).then_inc(done, 1)

        def dve_rest(dve, b, job, bank):
            dve.wait_ge(s_part1, 4 * b + job + 1)
            wait(dve, s_part3, 4 * b + job - 1)
            if job % 2 == 0:
                nc.vector.scalar_tensor_tensor(rest[:, job % 2, :], misc[bank][:], cst[:, bass.ds(C_ROPE + b, 1)],
                                               parts[:, job, 0, :], ALU.mult, ALU.subtract).then_inc(s_rest, 1)
            else:
                nc.vector.tensor_tensor(rest[:, job % 2, :], misc[bank][:], parts[:, job, 0, :],
                                        ALU.subtract).then_inc(s_rest, 1)

        def dve_max_part(dve, v, k, bank):
            dve.wait_ge(s_mT_ps, v + 1)
            wait(dve, s_m_out[k], (v - k) * 8)
            nc.vector.tensor_copy(max_parts[:, k, 0, :], misc[bank][0:UNIT_HEADS * TILES, 0:P]).then_inc(s_m1, 1)

        def dve_max_rest(dve, v, k, bank):
            dve.wait_ge(s_m1, v + 1)
            nc.vector.tensor_tensor(max_rest[:, k, :], misc[bank][0:UNIT_HEADS * TILES, 0:P],
                                    max_parts[:, k, 0, :], ALU.subtract).then_inc(s_mrest, 1)

        def dve_inv(dve, w, bank):
            dve.wait_ge(s_out_ps, w + 1)
            src = misc[bank][:].rearrange("p (t h d) -> p t h d", t=TILES, d=32)
            nc.vector.reciprocal(inv_sum[:], src[:, :, :, HEAD]).then_inc(s_inv, 1)

        def dve_attn(dve, w, bank, par, group):
            dve.wait_ge(s_inv, w + 1)
            src = misc[bank][:].rearrange("p (t h d) -> p t h d", t=TILES, d=32)[:, :, :, 0:HEAD]
            dst = attn[:, par, :, 64 * group:64 * group + 64].rearrange("p t (h d) -> p t h d", d=HEAD)
            inv = inv_sum[:].unsqueeze(3).broadcast_to([P, TILES, UNIT_HEADS, HEAD])
            nc.vector.tensor_tensor(dst, src, inv, ALU.mult).then_inc(s_attn, 1)

        def dve_rowmax(dve, tile_no, i, k):
            dve.wait_ge(s_score, tile_no + 1)
            nc.vector.reduce_max(row_max[:, k, i:i + 1], score_bank[score_place(i)[0]][:], AX).then_inc(s_rowmax, 1)

        def dve_slot(dve, b, par, s, first=False, last=False):
            g, j = s // 4, s % 4
            u = 4 * b + g
            scoring = not (last and g >= 2)
            if j == 0 and scoring:
                dve.wait_ge(s_mT_ps, u + 1)
            for c in range(TILES):
                if scoring:
                    dve_rowmax(dve, 16 * (u + 2) + TILES * j + c, TILES * j + c, g % 2)
                dve_between(dve, b, par, s, c, first, last)

        def dve_between(dve, b, par, s, c, first, last):
            at = (s, c)
            if not isinstance(b, int) or b + 2 < BATCHES:
                if s == 14:
                    if c == 0:
                        dve.wait_ge(s_x, 16 * (b + 3))
                    dve_stats(0, c, x_in[:, c, :], s_xst)
                if at == (15, 0):
                    dve_moments(dve, 0, b + 2, s_xst, s_xmom)
            if s in (1, 5, 9) or (s == 13 and not last):
                v, k, bank = {1: (4 * b + 1, 1, 0), 5: (4 * b + 2, 0, 0), 9: (4 * b + 3, 1, 1),
                              13: (4 * b + 4, 0, 0)}[s]
                if c == 0:
                    dve_max_part(dve, v, k, bank)
                if c == 1:
                    dve_max_rest(dve, v, k, bank)
            if s % 4 == 1 and not (first and s < 8):
                bank = int(s != 9)
                if c == 2:
                    dve_inv(dve, 4 * b + s // 4 - 2, bank)
                if c == 3:
                    w_par, w_group = (1 - par, 2 + s // 4) if s < 8 else (par, s // 4 - 2)
                    dve_attn(dve, 4 * b + s // 4 - 2, bank, w_par, w_group)
            if at in REST_AT and not last:
                job = REST_AT.index(at)
                dve_rest(dve, b + 1, job, job % 2)
            if not first:
                if s == 6 and c < 2:
                    if c == 0:
                        dve.wait_ge(s_attn, 4 * b)
                    for t in (2 * c, 2 * c + 1):
                        dve_stats(1, t, attn[:, 1 - par, t, :], s_ast)
                if at == (6, 2):
                    dve_moments(dve, 1, b - 1, s_ast, s_amom)
                if s == 10:
                    dve.wait_ge(s_x1, TILES * (b - 1) + c + 1)
                    dve_stats(2, c, rows[:, c, DIM:ROW], s_x1st)
                if at == (10, 3):
                    dve_moments(dve, 2, b - 1, s_x1st, s_x1mom)

        def dve_route(dve):
            V = nc.vector
            steps = [0]

            def step(ins):
                ins.then_inc(s_route, 1)
                steps[0] += 1
                dve.wait_ge(s_route, steps[0])

            def over(ap, n):
                return ap.unsqueeze(2).broadcast_to([P, ap.shape[1], n])

            def under(ap, n):
                return ap.unsqueeze(1).broadcast_to([P, n, ap.shape[1]])

            dve.wait_ge(s_out_ps, UNITS)
            step(V.memset(ones, 1.0))
            step(V.memset(no_carry, 1.0))
            step(V.memset(no_carry[:, :, 0:1], 0.0))
            step(V.tensor_scalar(less_8[:], count[:, 0:EXPERTS], float(EXPERTS), None, ALU.subtract))
            step(V.tensor_copy(count_bf, count))
            dve.wait_ge(s_scale[2], BATCHES)
            for t in DVE_SHARE:
                dve_normalise(2, t, rows[:, t, 0:DIM], rows[:, t, DIM:ROW], s_feats)
            dve.wait_ge(s_scores, BATCHES)
            step(V.tensor_reduce(best[:], scores[:], AX, ALU.max))
            step(V.tensor_tensor(hits, scores[:], over(best[:], EXPERTS), ALU.is_equal))
            step(V.tensor_tensor(hits, hits, under(less_8[:], TOKEN_TILES), ALU.mult))
            step(V.tensor_reduce(first_hit[:], hits, AX, ALU.min))
            step(V.tensor_tensor(one_hot, over(less_8[:], TOKEN_TILES), under(first_hit[:], EXPERTS), ALU.is_equal))
            flat = [a.rearrange("p e t -> p (e t)") for a in (running, no_carry, one_hot)]
            step(V.tensor_tensor_scan(flat[0], flat[1], flat[2], 0.0, ALU.mult, ALU.add))
            V.tensor_copy(masked, running).then_inc(s_counted, 1)
            dve.wait_ge(s_totals, 1)
            step(V.tensor_scalar(tiles_i[:], score_bank[0][:, EXPERTS:2 * EXPERTS], float(P - 1), None, ALU.add))
            step(V.tensor_scalar(tiles_i[:], tiles_i[:], 7, None, ALU.arith_shift_right))
            step(V.tensor_copy(tiles_f[:], tiles_i[:]))
            step(V.tensor_tensor_scan(tiles_end[:], ones[:, 0:EXPERTS], tiles_f[:], 0.0, ALU.mult, ALU.add))
            step(V.tensor_tensor(slot_ge, over(count[:, 0:SLOTS], EXPERTS), under(tiles_end[:], SLOTS), ALU.is_ge))
            step(V.tensor_reduce(expert_f[:], slot_ge, AX, ALU.add))
            V.tensor_scalar(expert_of[:], expert_f[:], float(EXPERTS - 1), None, ALU.min).then_inc(s_experts, 1)
            step(V.tensor_tensor(offset[:], tiles_end[:], tiles_f[:], ALU.subtract))
            step(V.scalar_tensor_tensor(offset[:], offset[:], float(P), score_bank[0][:, 0:EXPERTS],
                                        ALU.mult, ALU.add))
            step(V.tensor_tensor(masked, running, over(offset[:], TOKEN_TILES), ALU.add))
            step(V.scalar_tensor_tensor(masked, masked, -1.0, one_hot, ALU.add, ALU.mult))
            step(V.tensor_reduce(place[:], masked.rearrange("p e t -> p t e"), AX, ALU.add))
            step(V.tensor_copy(place_i[:], place[:]))
            step(V.tensor_scalar(place_i[:], place_i[:], 7, None, ALU.arith_shift_right))
            step(V.tensor_copy(slot_f[:], place_i[:]))
            step(V.scalar_tensor_tensor(within[:], slot_f[:], -float(P), place[:], ALU.mult, ALU.add))
            V.tensor_tensor(slot_eq, under(count[:, 0:SLOTS], TOKEN_TILES), over(slot_f[:], SLOTS),
                            ALU.is_equal).then_inc(s_slot_eq, 1)
            for t in range(TOKEN_TILES):
                V.tensor_scalar(place_hot[:, t, :], count_bf, within[:, t:t + 1], None,
                                ALU.is_equal).then_inc(s_place, 1)
            dve.wait_ge(s_found, 1)
            step(V.tensor_copy(found[:], score_bank[1][:, 0:3 * SLOTS].rearrange("p (m s) -> p m s", m=3)))
            step(V.scalar_tensor_tensor(token_f[:], found[:, 1, :], float(P), found[:, 0, :], ALU.mult, ALU.add))
            step(V.tensor_copy(index_all[:, :, 0], token_f[:]))
            step(V.tensor_scalar(found[:, 2, :], found[:, 2, :], -float(SKIP), float(SKIP), ALU.mult, ALU.add))
            V.tensor_tensor(index_all[:, :, 1], token_f[:], found[:, 2, :], ALU.add).then_inc(s_index, 1)
            dve.wait_ge(s_index, 1)
            dve.wait_ge(s_par, 16 * 5)

        def dve_index(n, ring):
            nc.vector.tensor_copy(index_now[:, ring, :].unsqueeze(1), index_all[:, bass.ds(n, 1), :]).then_inc(s_prep, 1)

        def dve_weights(dve, n, k, k3):
            e = expert_reg(dve, n)
            for c in range(CHUNKS):
                nc.vector.tensor_copy(w1_now[k][c].unsqueeze(1), w1[:, bass.ds(e, 1), c, :]).then_inc(s_w1_now, 1)
            nc.vector.tensor_copy(b2_now[k3].unsqueeze(1), b2_all[:, bass.ds(e, 1), :]).then_inc(s_b2_now, 1)

        def dve_features(dve, n, ring, round_1, k):
            e = expert_reg(dve, n)
            nc.vector.tensor_copy(params_now[:, ring, :].unsqueeze(1), params[:, bass.ds(e, 1), :])
            dve.wait_ge(s_gather[ring], 16 * round_1)
            nc.vector.bn_stats(slot_stats[:, 0, k, :], got[:, ring, 0:DIM]).then_inc(s_gst, 1)
            nc.vector.scalar_tensor_tensor(product, got[:, ring, 0:DIM], 1.0,
                                           cent_all[:, bass.ds(e, 1), :].rearrange("p o d -> p (o d)"),
                                           ALU.mult, ALU.mult, accum_out=dot[:, ring:ring + 1]).then_inc(s_dot, 1)
            wait_alone(dve, s_gst, n + 1, s_passed)
            nc.vector.bn_aggr(slot_mom[:, 0, k, :], slot_stats[:, 0, k, :]).then_inc(s_gmom, 1)

        def dve_alpha(dve, n, ring):
            dve.wait_ge(s_minus, n + 1)
            nc.vector.tensor_scalar(minus[:, ring:ring + 1], minus[:, ring:ring + 1], 1.0, None,
                                    ALU.add).then_inc(s_plus1, 1)
            dve.wait_ge(s_plus1, n + 1)
            nc.vector.reciprocal(alpha[:, ring:ring + 1], minus[:, ring:ring + 1]).then_inc(s_alpha, 1)

        def dve_finish(dve, n, ring, k, k3):
            dve.wait_ge(s_b2_now, n + 1)
            dve.wait_ge(s_y_ps, n + 1)
            nc.vector.tensor_tensor(mixed[:, k, :], y_bank[k][:, 0:DIM], b2_now[k3], ALU.add).then_inc(s_y, 1)
            dve.wait_ge(s_y, n + 1)
            dve.wait_ge(s_alpha, n + 1)
            nc.vector.scalar_tensor_tensor(mixed[:, k, :], mixed[:, k, :], alpha[:, ring:ring + 1],
                                           got[:, ring, 0:DIM], ALU.mult, ALU.add).then_inc(s_mix, 1)
            dve.wait_ge(s_mix, n + 1)
            nc.vector.bn_stats(slot_stats[:, 1, k, :], mixed[:, k, :]).then_inc(s_mst, 1)
            wait_alone(dve, s_mst, n + 1, s_passed)
            nc.vector.bn_aggr(slot_mom[:, 1, k, :], slot_stats[:, 1, k, :]).then_inc(s_mmom, 1)

        def dve_tok(dve, n, ring, k):
            wait(dve, s_tokT_ps, n - 1)
            dve.wait_ge(s_grstd, n + 1)
            nc.vector.tensor_scalar(tok_n[:, k, :], got[:, ring, 0:DIM], slot_mom[:, 0, k, 0:1],
                                    slot_rstd[:, 0, k:k + 1], ALU.subtract, ALU.mult).then_inc(s_tok, 1)

        def dve_new(dve, n, ring, k):
            dve.wait_ge(s_mrstd, n + 1)
            nc.vector.tensor_scalar(new_rows[:, ring, :], mixed[:, k, :], slot_mom[:, 1, k, 0:1],
                                    slot_rstd[:, 1, k:k + 1], ALU.subtract, ALU.mult).then_inc(s_mixn, 1)
            dve.wait_ge(s_mixn, n + 1)
            nc.vector.tensor_tensor(new_rows[:, ring, :], new_rows[:, ring, :], got[:, ring, DIM:ROW],
                                    ALU.add).then_inc(s_new, 1)

        def dve_slot_step(dve, r, k):
            known = isinstance(r, int)
            j, ring0, _ = slot_at(r, k, 0)
            n, ring, rnd = slot_at(r, k, AHEAD)
            if not known or n < SLOTS:
                wait(dve, s_scatter[ring], 16 * rnd)
                dve_index(n, ring)
            m, ring2, _ = slot_at(r, k, 2)
            if not known or m < SLOTS:
                if known and j == 0:
                    dve.wait_ge(s_h_ps, 2)
                dve_weights(dve, m, k % 2, (k + 2) % 3)
            n, ring, rnd = slot_at(r, k, 3)
            if not known or n < SLOTS:
                dve_features(dve, n, ring, rnd + 1, (k + 1) % 2)
            if not known or j > 0:
                dve_new(dve, r * RING + (k - 1), (k - 1) % RING, (k - 1) % 2)
            if not known or m < SLOTS:
                dve_alpha(dve, m, ring2)
            if not known or n < SLOTS:
                dve_tok(dve, n, ring, (k + 1) % 2)
            dve_finish(dve, j, ring0, k % 2, k % 3)

        @block.vector
        def _(dve):
            dve.wait_ge(s_x, 16)
            for t in range(TILES):
                dve_stats(0, t, x_in[:, t, :], s_xst)
            dve_moments(dve, 0, 0, s_xst, s_xmom)
            dve.wait_ge(s_const, 16 * LOADS)
            for job in range(4):
                dve_rest(dve, 0, job, job % 2)
            for v in range(2):
                for i in range(16):
                    dve_rowmax(dve, 16 * v + i, i, v)
                if v == 0:
                    dve_max_part(dve, 0, 0, 0)
                    dve_max_rest(dve, 0, 0, 0)
            dve.wait_ge(s_x, 32)
            for t in range(TILES):
                dve_stats(0, t, x_in[:, t, :], s_xst)
            dve_moments(dve, 0, 1, s_xst, s_xmom)
            for b in range(2):
                for s in range(16):
                    dve_slot(dve, b, b, s, first=(b == 0))
            with dve.Fori(0, 2) as r:
                for k in range(2):
                    for s in range(16):
                        dve_slot(dve, r * 2 + 2 + k, k, s)
            for b in (6, 7):
                for s in range(16):
                    dve_slot(dve, b, b % 2, s, last=(b == 7))
            for w, bank in ((UNITS - 2, 1), (UNITS - 1, 0)):
                dve.wait_ge(s_attn, w)
                dve_inv(dve, w, bank)
                dve_attn(dve, w, bank, 1, w % 4)
            dve.wait_ge(s_attn, UNITS)
            for t in range(TILES):
                dve_stats(1, t, attn[:, 1, t, :], s_ast)
            dve_moments(dve, 1, BATCHES - 1, s_ast, s_amom)
            dve.wait_ge(s_scale[1], BATCHES)
            dve.wait_ge(s_res, 16 * BATCHES)
            for t in DVE_SHARE:
                dve_normalise(1, t, rows[:, t, DIM:ROW], attn[:, 1, t, :], s_share)
            for i, t in enumerate(DVE_SHARE):
                dve.wait_ge(s_share, len(DVE_SHARE) + i)
                nc.vector.tensor_tensor(rows[:, t, DIM:ROW], rows[:, t, DIM:ROW], x_res[:, t, :],
                                        ALU.add).then_inc(s_share, 1)
            for i, t in enumerate(DVE_SHARE):
                dve.wait_ge(s_share, len(DVE_SHARE) + i + 1)
                dve_stats(2, t, rows[:, t, DIM:ROW], s_x1st)
            for t in ACT_SHARE:
                dve.wait_ge(s_x1, TILES * (BATCHES - 1) + t + 1)
                dve_stats(2, t, rows[:, t, DIM:ROW], s_x1st)
            dve_moments(dve, 2, BATCHES - 1, s_x1st, s_x1mom)
            dve_route(dve)
            for n in range(4):
                dve_index(n, n)
            dve.wait_ge(s_weights, 16 * 2 * EXPERTS)
            dve_weights(dve, 0, 0, 0)
            for n in range(3):
                dve_features(dve, n, n, 1, n % 2)
                dve_tok(dve, n, n, n % 2)
                if n == 0:
                    dve_weights(dve, 1, 1, 1)
            for n in range(2):
                dve_alpha(dve, n, n)
            for k in range(RING):
                dve_slot_step(dve, 0, k)
            with dve.Fori(1, LOOPED // RING) as r:
                for k in range(RING):
                    dve_slot_step(dve, r, k)
            for k in range(PEELED):
                dve_slot_step(dve, LOOPED // RING, k)
            dve_new(dve, SLOTS - 1, (SLOTS - 1) % RING, (SLOTS - 1) % 2)

        def pool_scale(pool, which, b, moments_done, steps):
            wait_alone(pool, moments_done, TILES * (b + 1), s_passed)
            nc.gpsimd.tensor_scalar(rstd[:, which, :], moments[:, which, :, 1], EPS, None,
                                    ALU.add).then_inc(s_pool, 1)
            nc.gpsimd.tensor_scalar(shift[:, which, :], moments[:, which, :, 0], -1.0, None,
                                    ALU.mult).then_inc(s_pool, 1)
            pool.wait_ge(s_pool, steps + 2)
            nc.gpsimd.tensor_tensor(rstd[:, which, :], rstd[:, which, :], half_neg[:], ALU.pow).then_inc(s_pool, 1)
            pool.wait_ge(s_pool, steps + 3)
            nc.gpsimd.tensor_tensor(shift[:, which, :], shift[:, which, :], rstd[:, which, :],
                                    ALU.mult).then_inc(s_scale[which], 1)

        def pool_normalise(which, t, dst, src, done):
            nc.gpsimd.tensor_scalar(dst, src, moments[:, which, t, 0:1], rstd[:, which, t:t + 1],
                                    ALU.subtract, ALU.mult).then_inc(done, 1)

        def pool_parts(pool, b, job, both=True):
            if both:
                wait_alone(pool, s_rest, 4 * b + job + 1, s_passed)
                nc.gpsimd.tensor_copy(parts[:, job, 1, :], rest[:, job % 2, :]).then_inc(s_part2, 1)
            pool.wait_ge(s_part2, 4 * b + job + 1)
            nc.gpsimd.tensor_tensor(parts[:, job, 2, :], rest[:, job % 2, :], parts[:, job, 1, :],
                                    ALU.subtract).then_inc(s_part3, 1)

        def pool_max_parts(pool, v, k):
            wait_alone(pool, s_mrest, v + 1, s_passed)
            nc.gpsimd.tensor_copy(max_parts[:, k, 1, :], max_rest[:, k, :]).then_inc(s_m2, 1)
            pool.wait_ge(s_m2, v + 1)
            nc.gpsimd.tensor_tensor(max_parts[:, k, 2, :], max_rest[:, k, :], max_parts[:, k, 1, :],
                                    ALU.subtract).then_inc(s_m3, 1)

        def pool_residual(pool, b, tiles=range(TILES)):
            pool.wait_ge(s_res, 16 * (b + 1))
            for t in tiles:
                pool.wait_ge(s_attn_n, TILES * b + t + 1)
                nc.gpsimd.tensor_tensor(rows[:, t, DIM:ROW], rows[:, t, DIM:ROW], x_res[:, t, :],
                                        ALU.add).then_inc(s_x1, 1)

        def pool_batch(pool, b, par, first=False, last=False):
            steps = 3 + 3 * b + (6 * (b - 1) if not first else 0)
            if not last:
                pool_scale(pool, 0, b + 1, s_xmom, steps)
                steps = steps + 3
                for t in (2, 3):
                    pool_normalise(0, t, x_in[:, t, :], x_in[:, t, :], s_normed)
            pool_max_parts(pool, 4 * b + 1, 1)
            if not last:
                pool_parts(pool, b + 1, 0, both=False)
                pool_parts(pool, b + 1, 1, both=False)
            pool_max_parts(pool, 4 * b + 2, 0)
            if not first:
                pool_scale(pool, 1, b - 1, s_amom, steps)
            if not last:
                pool_parts(pool, b + 1, 2)
                pool_parts(pool, b + 1, 3)
            if not first:
                pool_residual(pool, b - 1)
            pool_max_parts(pool, 4 * b + 3, 1)
            if not first:
                pool_scale(pool, 2, b - 1, s_x1mom, steps + 3)
                for t in range(TILES):
                    pool_normalise(2, t, rows[:, t, 0:DIM], rows[:, t, DIM:ROW], s_feats)
            if not last:
                pool_max_parts(pool, 4 * b + 4, 0)

        out_rows = out.rearrange("b s d -> (b s) d")

        def pool_gather(pool, n, ring):
            wait_alone(pool, s_prep, n + 1, s_passed)
            nc.gpsimd.indirect_dma_start(
                out=got[:, ring, :], out_offset=None, in_=rows_dram,
                in_offset=bass.IndirectOffsetOnAxis(ap=index_now[:, ring, 0:1].bitcast(U32), axis=0),
                bounds_check=TOKENS - 1, oob_is_err=False).then_inc(s_gather[ring], 16)

        def pool_slot_rstd(pool, which, k, step, done):
            nc.gpsimd.tensor_scalar(slot_rstd[:, which, k:k + 1], slot_mom[:, which, k, 1:2], EPS, None,
                                    ALU.add).then_inc(s_chain, 1)
            pool.wait_ge(s_chain, step)
            nc.gpsimd.tensor_tensor(slot_rstd[:, which, k:k + 1], slot_rstd[:, which, k:k + 1], half_neg[:, 0:1],
                                    ALU.pow).then_inc(done, 1)

        def pool_scatter(pool, n, ring):
            wait_alone(pool, s_new, n + 1, s_passed)
            nc.gpsimd.indirect_dma_start(
                out=out_rows, out_offset=bass.IndirectOffsetOnAxis(ap=index_now[:, ring, 1:2].bitcast(U32), axis=0),
                in_=new_rows[:, ring, :], in_offset=None,
                bounds_check=TOKENS - 1, oob_is_err=False).then_inc(s_scatter[ring], 16)

        def pool_slot_step(pool, r, k):
            known = isinstance(r, int)
            j, _, _ = slot_at(r, k, 0)
            n, ring, _ = slot_at(r, k, AHEAD)
            if not known or n < SLOTS:
                pool_gather(pool, n, ring)
            m, _, _ = slot_at(r, k, 3)
            step = j * 2 + 4
            if not known or m < SLOTS:
                wait_alone(pool, s_gmom, m + 1, s_passed)
                pool_slot_rstd(pool, 0, (k + 1) % 2, step, s_grstd)
                step = step + 1
            elif j > SLOTS - 3:
                step = step - (j - (SLOTS - 3))
            if not known or j > 0:
                pool_scatter(pool, r * RING + (k - 1), (k - 1) % RING)
            wait_alone(pool, s_mmom, j + 1, s_passed)
            pool_slot_rstd(pool, 1, k % 2, step, s_mrstd)

        @block.gpsimd
        def _(pool):
            nc.gpsimd.memset(half_neg[:], -0.5).then_inc(s_fill, 1)
            nc.gpsimd.memset(values[:, :, :, :, HEAD:HEAD + 1], 1.0).then_inc(s_fill, 1)
            nc.gpsimd.memset(values[:, :, :, :, HEAD + 1:32], 0.0).then_inc(s_fill, 1)
            nc.gpsimd.memset(centT[:], 0.0).then_inc(s_fill, 1)
            pool.wait_ge(s_fill, FILLS)
            pool_scale(pool, 0, 0, s_xmom, 0)
            for job in range(4):
                pool_parts(pool, 0, job, both=False)
            pool_max_parts(pool, 0, 0)
            pool_batch(pool, 0, 0, first=True)
            with pool.Fori(0, 3) as r:
                pool_batch(pool, r * 2 + 1, 1)
                pool_batch(pool, r * 2 + 2, 0)
            pool_batch(pool, 7, 1, last=True)
            steps = 3 + 3 * 7 + 6 * 7
            pool_scale(pool, 1, 7, s_amom, steps)
            pool_residual(pool, 7, ACT_SHARE)
            pool_scale(pool, 2, 7, s_x1mom, steps + 3)
            pool.wait_ge(s_slot_eq, 1)
            nc.gpsimd.tensor_tensor(slot_hot[:, :, 1, :], slot_eq,
                                    count[:, 0:TOKEN_TILES].unsqueeze(2).broadcast_to([P, TOKEN_TILES, SLOTS]),
                                    ALU.mult).then_inc(s_hot, 1)
            pool.wait_ge(s_rows, 16 * BATCHES)
            pool.wait_ge(s_index, 1)
            for n in range(4):
                pool_gather(pool, n, n)
            for n in range(3):
                wait_alone(pool, s_gmom, n + 1, s_passed)
                pool_slot_rstd(pool, 0, n % 2, n + 1, s_grstd)
            for k in range(RING):
                pool_slot_step(pool, 0, k)
            with pool.Fori(1, LOOPED // RING) as r:
                for k in range(RING):
                    pool_slot_step(pool, r, k)
            for k in range(PEELED):
                pool_slot_step(pool, LOOPED // RING, k)
            pool_scatter(pool, SLOTS - 1, (SLOTS - 1) % RING)


def table():
    t = np.zeros((P, C_END), np.float32)
    t[:, C_IDENT:C_IDENT + P] = np.eye(P)
    t[:, C_BELOW:C_BELOW + P] = np.triu(np.ones((P, P)), 1)
    half = HEAD // 2
    theta = 1.0 / 10000.0 ** (np.arange(0, HEAD, 2, dtype=np.float32) / np.float32(HEAD))
    for b in range(BATCHES):
        angle = (np.float32(b) * theta.astype(np.float32)).astype(np.float64)
        factor = np.concatenate([np.cos(angle) + np.sin(angle), np.cos(angle) - np.sin(angle)])
        t[:, C_ROPE + b] = np.tile(factor * factor / np.sqrt(HEAD), P // HEAD)
    t[:, C_COUNT:C_COUNT + P] = np.arange(P)
    t[:, C_PART] = np.arange(P)
    return t


def kernel(L0_attn_x, L0_attn_Wq, L0_attn_Wk, L0_attn_Wv, L0_ffn_centroids, L0_ffn_gamma, L0_ffn_beta,
           L0_ffn_W1, L0_ffn_b1, L0_ffn_W2, L0_ffn_b2):
    import concourse.bacc as bacc
    import ml_dtypes
    from concourse.bass_utils import run_bass_kernel_spmd

    def laid(a, *order):
        return np.ascontiguousarray(np.transpose(np.asarray(a), order))

    E, C = EXPERTS, CHUNKS
    arrays = {
        "x": np.ascontiguousarray(L0_attn_x),
        "wqt": laid(L0_attn_Wq, 1, 0), "wkt": laid(L0_attn_Wk, 1, 0), "wvt": laid(L0_attn_Wv, 1, 0),
        "cent": np.ascontiguousarray(L0_ffn_centroids),
        "cent_t": laid(L0_ffn_centroids, 1, 0),
        "gamma_t": laid(np.asarray(L0_ffn_gamma).reshape(E, C, P), 2, 0, 1),
        "beta_t": laid(np.asarray(L0_ffn_beta).reshape(E, C, P), 2, 0, 1),
        "w1t": laid(np.asarray(L0_ffn_W1).reshape(E, HIDDEN, C, P), 0, 3, 2, 1),
        "b1_t": laid(np.asarray(L0_ffn_b1).reshape(E, BLOCKS, P), 2, 0, 1),
        "w2t": laid(np.asarray(L0_ffn_W2).reshape(E, DIM, BLOCKS, P), 0, 3, 2, 1),
        "b2": np.ascontiguousarray(L0_ffn_b2),
        "consts": table(),
        "minus_ones": np.full((FULL - STACK, 2, HEADS, SEQ), -1, ml_dtypes.bfloat16),
    }
    nc = bacc.Bacc("TRN2", target_bir_lowering=False, num_devices=1)
    args = [nc.dram_tensor(name, a.shape, mybir.dt.from_np(a.dtype), kind="ExternalInput").ap() for name, a in arrays.items()]
    out = nc.dram_tensor("out", (BATCHES, SEQ, DIM), F32, kind="ExternalOutput").ap()
    build(nc, *args, out)
    result = run_bass_kernel_spmd(nc, [arrays], core_ids=[0])
    return result.results[0]["out"]
```
